# Optimizing a Trainium2 kernel written in Bass

```python
import numpy as np
import jax
import jax.numpy as jnp

def _softmax(x, axis=-1):
    return jax.nn.softmax(x, axis=axis)

def _gelu(x):
    return jax.nn.gelu(x, approximate=True)

def _silu(x):
    return jax.nn.silu(x)

def _sigmoid(x):
    return jax.nn.sigmoid(x)

def _layernorm(x, axis=-1, eps=1e-05):
    m = jnp.mean(x, axis=axis, keepdims=True)
    v = jnp.var(x, axis=axis, keepdims=True)
    return (x - m) / jnp.sqrt(v + eps)

def _scatter_add(tgt, idx, src, axis=0):
    return tgt.at[idx].add(src)

def _segment_sum(src, seg, n):
    return jax.ops.segment_sum(src, seg, n)
kernel_name = 'mk_flamingo_gated_d1_seqx_r2_793fd1'

def setup_inputs(seed: int=0):
    np.random.seed(seed)
    _w = jnp.asarray

    def _rec_inputs():
        import jax
        import jax.numpy as jnp
        _rk = jax.random.key(seed)
        x = 4.136e-05 + 0.9999 * jax.random.normal(jax.random.fold_in(_rk, 1), (4, 1024, 1024), jnp.float32)
        _lenS = 1024 - jax.random.randint(jax.random.fold_in(_rk, 7), (4,), 0, max(1, 1024 // 4) + 1, jnp.int32)
        _lenS2 = 1024 - jax.random.randint(jax.random.fold_in(_rk, 8), (4,), 0, max(1, 1024 // 4) + 1, jnp.int32)
        _ctx_1024P = jax.random.normal(jax.random.fold_in(_rk, 11), (4, 16, 512), jnp.float32)
        _ctx_1024c = jax.random.dirichlet(jax.random.fold_in(_rk, 511), 0.3 * jnp.ones((16,), jnp.float32), (4, 1024))
        _ctx_1024t = jnp.einsum('bsk,bkd->bsd', _ctx_1024c, _ctx_1024P)
        _ctx_1024t = _ctx_1024t * jax.lax.rsqrt(jnp.mean(jnp.square(_ctx_1024t)) + 1e-12) * 0.953939
        ctx_1024 = -0.000292821 + 1.00034 * (_ctx_1024t + 0.3 * jax.random.normal(jax.random.fold_in(_rk, 611), (4, 1024, 512), jnp.float32))
        _g = jax.random.normal(jax.random.fold_in(_rk, 9001), (2, 1), jnp.float32)
        _g = jnp.sign(_g) * jnp.maximum(jnp.abs(_g), 1.0) + (_g == 0) * 1.0
        g_xattn = _g[0]
        g_ffn = _g[1]
        return (x, ctx_1024, g_xattn, g_ffn)
    x, ctx_1024, g_xattn, g_ffn = _rec_inputs()

    def _L0_xattn_setup():
        import jax, jax.numpy as jnp
        import numpy as np
        import math
        B, L, DM = (2, 1024, 512)
        DS, DC, EXP = (16, 4, 2)
        DI = EXP * DM
        DR = math.ceil(DM / 16)
        DT_MIN, DT_MAX, DT_FLOOR = (0.001, 0.1, 0.0001)

        def _ssm_forward(hidden_states, z, in_proj_w, conv_w, conv_b, x_proj_w, dt_proj_w, dt_proj_b, A_log, D):
            b = hidden_states.shape[0]
            x = jnp.einsum('ed,bld->bel', in_proj_w, hidden_states)
            xp = jnp.pad(x, ((0, 0), (0, 0), (DC - 1, 0)))
            xc = jax.lax.conv_general_dilated(xp, conv_w[:, None, :], window_strides=(1,), padding='VALID', dimension_numbers=('NCH', 'OIH', 'NCH'), feature_group_count=DI)
            u = jax.nn.silu(xc + conv_b[None, :, None])
            x_dbl = jnp.einsum('ke,bel->bkl', x_proj_w, u)
            dt_lo = x_dbl[:, :DR]
            Bm = x_dbl[:, DR:DR + DS]
            Cm = x_dbl[:, DR + DS:]
            delta = jax.nn.softplus(jnp.einsum('er,brl->bel', dt_proj_w, dt_lo) + dt_proj_b[None, :, None])
            A = -jnp.exp(A_log)

            def step(state, xs):
                d_t, B_t, C_t, u_t = xs
                dA = jnp.exp(d_t[..., None] * A)
                state = state * dA + (d_t * u_t)[..., None] * B_t[:, None, :]
                y_t = jnp.einsum('ben,bn->be', state, C_t)
                return (state, y_t)
            xs = (jnp.moveaxis(delta, -1, 0), jnp.moveaxis(Bm, -1, 0), jnp.moveaxis(Cm, -1, 0), jnp.moveaxis(u, -1, 0))
            state0 = jnp.zeros((b, DI, DS), delta.dtype)
            _, ys = jax.lax.scan(step, state0, xs)
            y = jnp.moveaxis(ys, 0, -1)
            y = y + D[None, :, None] * u
            y = y * jax.nn.silu(z)
            return jnp.swapaxes(y, 1, 2)
        key = jax.random.key(seed)
        ks = jax.random.split(key, 8)
        hidden_states = jax.random.normal(ks[0], (B, L, DM), jnp.float32)
        z = jax.random.normal(ks[1], (B, DI, L), jnp.float32)
        in_proj_w = jax.random.normal(ks[2], (DI, DM), jnp.float32) * DM ** (-0.5)
        conv_w = jax.random.normal(ks[3], (DI, DC), jnp.float32) * DC ** (-0.5)
        conv_b = jnp.zeros((DI,), jnp.float32)
        x_proj_w = jax.random.normal(ks[4], (DR + 2 * DS, DI), jnp.float32) * DI ** (-0.5)
        dt_std = DR ** (-0.5)
        dt_proj_w = jax.random.uniform(ks[5], (DI, DR), jnp.float32, -dt_std, dt_std)
        dt = jnp.exp(jax.random.uniform(ks[6], (DI,), jnp.float32) * (math.log(DT_MAX) - math.log(DT_MIN)) + math.log(DT_MIN))
        dt = jnp.clip(dt, DT_FLOOR)
        dt_proj_b = dt + jnp.log(-jnp.expm1(-dt))
        A_log = jnp.log(jnp.broadcast_to(jnp.arange(1, DS + 1, dtype=jnp.float32), (DI, DS)))
        D = jnp.ones((DI,), jnp.float32)
        return dict(hidden_states=hidden_states, z=z, in_proj_w=in_proj_w, conv_w=conv_w, conv_b=conv_b, x_proj_w=x_proj_w, dt_proj_w=dt_proj_w, dt_proj_b=dt_proj_b, A_log=A_log, D=D)
    _L0_xattn_all = _L0_xattn_setup()
    _L0_xattn_in = {k: v for k, v in _L0_xattn_all.items() if k in ('in_proj_w', 'conv_w', 'conv_b', 'x_proj_w', 'dt_proj_w', 'dt_proj_b', 'A_log', 'D')}
    del _L0_xattn_all

    def _L0_ffn_setup():
        import jax, jax.numpy as jnp
        import numpy as np
        E = 32
        K = 4
        G = 4
        TG = 2
        H = 1024
        F = 512
        FS = 1024
        SCALE = 2.0
        B, S = (2, 512)
        N = B * S
        CAP = 2 * (N * K // E)

        def _gate(x, gate_w, gate_bias):
            logits = x @ gate_w.T
            scores = jax.nn.sigmoid(logits)
            sc = scores + gate_bias
            n = x.shape[0]
            grp = sc.reshape(n, G, E // G)
            group_scores = jax.lax.top_k(grp, 2)[0].sum(-1)
            _, gidx = jax.lax.top_k(group_scores, TG)
            gmask = jnp.zeros((n, G), sc.dtype).at[jnp.arange(n)[:, None], gidx].set(1.0)
            smask = jnp.repeat(gmask, E // G, axis=1)
            tmp = jnp.where(smask > 0, sc, 0.0)
            _, topk_idx = jax.lax.top_k(tmp, K)
            topk_w = jnp.take_along_axis(scores, topk_idx, axis=1)
            topk_w = topk_w / (topk_w.sum(-1, keepdims=True) + 1e-20)
            return (topk_idx, topk_w * SCALE)

        def _moe(x, topk_idx, topk_w, w1, w2, w3):
            n = x.shape[0]
            flat_e = topk_idx.reshape(-1)
            oh = jax.nn.one_hot(flat_e, E, dtype=jnp.int32)
            pos = (jnp.cumsum(oh, axis=0) * oh).sum(-1) - 1
            keep = pos < CAP
            slot = jnp.where(keep, pos, CAP)
            x_rep = jnp.repeat(x, K, axis=0)
            buf = jnp.zeros((E, CAP, H), x.dtype).at[flat_e, slot].set(x_rep, mode='drop')
            h = jax.nn.silu(jnp.einsum('ech,ehf->ecf', buf, w1)) * jnp.einsum('ech,ehf->ecf', buf, w3)
            ob = jnp.einsum('ecf,efh->ech', h, w2)
            y = ob[flat_e, jnp.minimum(slot, CAP - 1)]
            y = jnp.where(keep[:, None], y, 0.0)
            return (y.reshape(n, K, H) * topk_w[:, :, None]).sum(1)
        key = jax.random.key(seed)
        ks = jax.random.split(key, 9)
        w = 0.02
        return {'hidden_states': jax.random.normal(ks[0], (B, S, H), jnp.float32), 'gate_w': jax.random.normal(ks[1], (E, H), jnp.float32) * w, 'gate_bias': jax.random.normal(ks[2], (E,), jnp.float32) * w, 'w1': jax.random.normal(ks[3], (E, H, F), jnp.float32) * w, 'w2': jax.random.normal(ks[4], (E, F, H), jnp.float32) * w, 'w3': jax.random.normal(ks[5], (E, H, F), jnp.float32) * w, 'shared_gate': jax.random.normal(ks[6], (H, FS), jnp.float32) * w, 'shared_up': jax.random.normal(ks[7], (H, FS), jnp.float32) * w, 'shared_down': jax.random.normal(ks[8], (FS, H), jnp.float32) * w}
    _L0_ffn_all = _L0_ffn_setup()
    _L0_ffn_in = {k: v for k, v in _L0_ffn_all.items() if k in ('gate_w', 'gate_bias', 'w1', 'w2', 'w3', 'shared_gate', 'shared_up', 'shared_down')}
    del _L0_ffn_all
    return {'x': x, 'ctx_1024': ctx_1024, 'g_xattn': g_xattn, 'g_ffn': g_ffn, 'L0_xattn_in_proj_w': _L0_xattn_in['in_proj_w'], 'L0_xattn_conv_w': _L0_xattn_in['conv_w'], 'L0_xattn_conv_b': _L0_xattn_in['conv_b'], 'L0_xattn_x_proj_w': _L0_xattn_in['x_proj_w'], 'L0_xattn_dt_proj_w': _L0_xattn_in['dt_proj_w'], 'L0_xattn_dt_proj_b': _L0_xattn_in['dt_proj_b'], 'L0_xattn_A_log': _L0_xattn_in['A_log'], 'L0_xattn_D': _L0_xattn_in['D'], 'L0_ffn_gate_w': _L0_ffn_in['gate_w'], 'L0_ffn_gate_bias': _L0_ffn_in['gate_bias'], 'L0_ffn_w1': _L0_ffn_in['w1'], 'L0_ffn_w2': _L0_ffn_in['w2'], 'L0_ffn_w3': _L0_ffn_in['w3'], 'L0_ffn_shared_gate': _L0_ffn_in['shared_gate'], 'L0_ffn_shared_up': _L0_ffn_in['shared_up'], 'L0_ffn_shared_down': _L0_ffn_in['shared_down']}

def reference(x, ctx_1024, g_xattn, g_ffn, L0_xattn_in_proj_w, L0_xattn_conv_w, L0_xattn_conv_b, L0_xattn_x_proj_w, L0_xattn_dt_proj_w, L0_xattn_dt_proj_b, L0_xattn_A_log, L0_xattn_D, L0_ffn_gate_w, L0_ffn_gate_bias, L0_ffn_w1, L0_ffn_w2, L0_ffn_w3, L0_ffn_shared_gate, L0_ffn_shared_up, L0_ffn_shared_down):
    import jax
    import jax.numpy as jnp

    def _L0_xattn_ref(hidden_states, z, in_proj_w, conv_w, conv_b, x_proj_w, dt_proj_w, dt_proj_b, A_log, D):
        import jax, jax.numpy as jnp
        import numpy as np
        import math
        B, L, DM = (2, 1024, 512)
        DS, DC, EXP = (16, 4, 2)
        DI = EXP * DM
        DR = math.ceil(DM / 16)
        DT_MIN, DT_MAX, DT_FLOOR = (0.001, 0.1, 0.0001)

        def _ssm_forward(hidden_states, z, in_proj_w, conv_w, conv_b, x_proj_w, dt_proj_w, dt_proj_b, A_log, D):
            b = hidden_states.shape[0]
            x = jnp.einsum('ed,bld->bel', in_proj_w, hidden_states)
            xp = jnp.pad(x, ((0, 0), (0, 0), (DC - 1, 0)))
            xc = jax.lax.conv_general_dilated(xp, conv_w[:, None, :], window_strides=(1,), padding='VALID', dimension_numbers=('NCH', 'OIH', 'NCH'), feature_group_count=DI)
            u = jax.nn.silu(xc + conv_b[None, :, None])
            x_dbl = jnp.einsum('ke,bel->bkl', x_proj_w, u)
            dt_lo = x_dbl[:, :DR]
            Bm = x_dbl[:, DR:DR + DS]
            Cm = x_dbl[:, DR + DS:]
            delta = jax.nn.softplus(jnp.einsum('er,brl->bel', dt_proj_w, dt_lo) + dt_proj_b[None, :, None])
            A = -jnp.exp(A_log)

            def step(state, xs):
                d_t, B_t, C_t, u_t = xs
                dA = jnp.exp(d_t[..., None] * A)
                state = state * dA + (d_t * u_t)[..., None] * B_t[:, None, :]
                y_t = jnp.einsum('ben,bn->be', state, C_t)
                return (state, y_t)
            xs = (jnp.moveaxis(delta, -1, 0), jnp.moveaxis(Bm, -1, 0), jnp.moveaxis(Cm, -1, 0), jnp.moveaxis(u, -1, 0))
            state0 = jnp.zeros((b, DI, DS), delta.dtype)
            _, ys = jax.lax.scan(step, state0, xs)
            y = jnp.moveaxis(ys, 0, -1)
            y = y + D[None, :, None] * u
            y = y * jax.nn.silu(z)
            return jnp.swapaxes(y, 1, 2)
        return _ssm_forward(hidden_states, z, in_proj_w, conv_w, conv_b, x_proj_w, dt_proj_w, dt_proj_b, A_log, D)

    def _L0_ffn_ref(hidden_states, gate_w, gate_bias, w1, w2, w3, shared_gate, shared_up, shared_down):
        import jax, jax.numpy as jnp
        import numpy as np
        E = 32
        K = 4
        G = 4
        TG = 2
        H = 1024
        F = 512
        FS = 1024
        SCALE = 2.0
        B, S = (2, 512)
        N = B * S
        CAP = 2 * (N * K // E)

        def _gate(x, gate_w, gate_bias):
            logits = x @ gate_w.T
            scores = jax.nn.sigmoid(logits)
            sc = scores + gate_bias
            n = x.shape[0]
            grp = sc.reshape(n, G, E // G)
            group_scores = jax.lax.top_k(grp, 2)[0].sum(-1)
            _, gidx = jax.lax.top_k(group_scores, TG)
            gmask = jnp.zeros((n, G), sc.dtype).at[jnp.arange(n)[:, None], gidx].set(1.0)
            smask = jnp.repeat(gmask, E // G, axis=1)
            tmp = jnp.where(smask > 0, sc, 0.0)
            _, topk_idx = jax.lax.top_k(tmp, K)
            topk_w = jnp.take_along_axis(scores, topk_idx, axis=1)
            topk_w = topk_w / (topk_w.sum(-1, keepdims=True) + 1e-20)
            return (topk_idx, topk_w * SCALE)

        def _moe(x, topk_idx, topk_w, w1, w2, w3):
            n = x.shape[0]
            flat_e = topk_idx.reshape(-1)
            oh = jax.nn.one_hot(flat_e, E, dtype=jnp.int32)
            pos = (jnp.cumsum(oh, axis=0) * oh).sum(-1) - 1
            keep = pos < CAP
            slot = jnp.where(keep, pos, CAP)
            x_rep = jnp.repeat(x, K, axis=0)
            buf = jnp.zeros((E, CAP, H), x.dtype).at[flat_e, slot].set(x_rep, mode='drop')
            h = jax.nn.silu(jnp.einsum('ech,ehf->ecf', buf, w1)) * jnp.einsum('ech,ehf->ecf', buf, w3)
            ob = jnp.einsum('ecf,efh->ech', h, w2)
            y = ob[flat_e, jnp.minimum(slot, CAP - 1)]
            y = jnp.where(keep[:, None], y, 0.0)
            return (y.reshape(n, K, H) * topk_w[:, :, None]).sum(1)
        b, s, h = hidden_states.shape
        x = hidden_states.reshape(-1, h)
        topk_idx, topk_w = _gate(x, gate_w, gate_bias)
        out = _moe(x, topk_idx, topk_w, w1, w2, w3)
        shared = jax.nn.silu(x @ shared_gate) * (x @ shared_up) @ shared_down
        return (out + shared).reshape(b, s, h)
    x = x + jnp.tanh(g_xattn[0]) * _L0_xattn_ref(ctx_1024, _layernorm(x, axis=-1), L0_xattn_in_proj_w, L0_xattn_conv_w, L0_xattn_conv_b, L0_xattn_x_proj_w, L0_xattn_dt_proj_w, L0_xattn_dt_proj_b, L0_xattn_A_log, L0_xattn_D)
    x = x + jnp.tanh(g_ffn[0]) * _L0_ffn_ref(_layernorm(x, axis=-1), L0_ffn_gate_w, L0_ffn_gate_bias, L0_ffn_w1, L0_ffn_w2, L0_ffn_w3, L0_ffn_shared_gate, L0_ffn_shared_up, L0_ffn_shared_down)
    return x

_drawn_inputs = setup_inputs


def setup_inputs(seed=0):
    import zlib

    import numpy as np

    out = dict(_drawn_inputs(seed))
    spreads = {'L0_xattn_conv_b': (0.0, 0.1), 'L0_xattn_D': (1.0, 0.2)}
    factors = {'L0_xattn_dt_proj_w': 4.68}
    for name, (base, spread) in spreads.items():
        noise = np.random.default_rng([zlib.crc32(name.encode()), seed]).standard_normal(out[name].shape)
        drawn = base * np.exp(spread * noise) if base else spread * noise
        out[name] = jnp.asarray(drawn.astype(out[name].dtype))
    for name, factor in factors.items():
        out[name] = (out[name] * factor).astype(out[name].dtype)
    return out
```

```python
from contextlib import ExitStack

import concourse.bass as bass
from concourse import mybir

P = 128
B, L, DM = 4, 1024, 512
DI, NST, DR, DC = 1024, 16, 32, 4
H, F, FS = 1024, 512, 1024
NE, TOPK, NG, TG = 32, 4, 4, 2
CAP = 2 * (2 * 512 * TOPK // NE)
NT = B * L
SCALE, EPS = 2.0, 1e-5
ET = DI // P
KD = DM // P
KH = H // P
TT = NT // P
ST = NE * CAP // P
TPE = CAP // P
HB = 512
NEWTON = 4
ROOT = 3 + 3 * NEWTON
ROUTE = 27
DROPPED = 1 << 16

ALU = mybir.AluOpType
ACT = mybir.ActivationFunctionType
F32 = mybir.dt.float32
I32 = mybir.dt.int32
U32 = mybir.dt.uint32
AX = mybir.AxisListType.X


def after(eng, sem, value):
    if isinstance(value, int):
        if value > 0:
            eng.wait_ge(sem, value)
    else:
        assert value.min_val > 0
        eng.wait_ge(sem, value)


def turns(eng, n, body, last=False, first=1):
    for i in range(first):
        body(i)
    with eng.Fori(first, n - last) as i:
        body(i)
    if last:
        body(n - 1)


class Steps:

    def __init__(self, eng, sem, per):
        self.eng, self.sem, self.per, self.n, self.turn = eng, sem, per, 0, 0

    def start(self, turn):
        self.turn, self.n = turn, 0

    def end(self):
        assert self.n == self.per, (self.n, self.per)

    def then(self, ins, gate=None):
        ins.then_inc(self.sem, 1)
        self.n += 1
        self.eng.wait_ge(self.sem, self.turn * self.per + self.n)
        if gate is not None:
            self.eng.sem_inc(gate, 1)


def inverse_root(st, dve, y, var, tmp):
    st.then(dve.tensor_scalar(tmp[:, 0:1], var, EPS, None, ALU.add))
    st.then(dve.tensor_scalar(tmp[:, 1:2].bitcast(I32), tmp[:, 0:1].bitcast(I32), 1, None, ALU.arith_shift_right))
    st.then(dve.tensor_scalar(y.bitcast(I32), tmp[:, 1:2].bitcast(I32), -1.0, float(0x5F3759DF), ALU.mult, ALU.add))
    for _ in range(NEWTON):
        st.then(dve.scalar_tensor_tensor(out=tmp[:, 1:2], in0=y, scalar=y, in1=tmp[:, 0:1], op0=ALU.mult, op1=ALU.mult))
        st.then(dve.tensor_scalar(tmp[:, 1:2], tmp[:, 1:2], -0.5, 1.5, ALU.mult, ALU.add))
        st.then(dve.tensor_tensor(y, y, tmp[:, 1:2], ALU.mult))


def mamba_inputs(nc, io, dr):
    with ExitStack() as ctx:
        sb = lambda name, shape, dt=F32: ctx.enter_context(nc.sbuf_tensor(name, shape, dt))
        sem = lambda name: ctx.enter_context(nc.semaphore(name))
        w_in = sb("w_in", [P, KD, DI])
        w_x = sb("w_x", [P, ET, DR + 2 * NST])
        w_dt = sb("w_dt", [DR, DI])
        conv_w = sb("conv_w", [P, ET, DC])
        conv_b = sb("conv_b", [P, ET])
        dt_b = sb("dt_b", [P, ET])
        a_neg = sb("a_neg", [P, ET, NST + 1])
        ctxT = sb("ctxT", [P, KD, L])
        xpad = sb("xpad", [P, 2, L + DC])
        conv = sb("conv", [P, 2, L])
        u = sb("u", [P, ET, L])
        xd = sb("xd", [DR + 2 * NST, L])
        ebuf = sb("ebuf", [P, ET, L])
        rbuf = sb("rbuf", [P, ET, L])
        lbuf = sb("lbuf", [P, 2, L])
        cbuf = sb("cbuf", [P, 2, L])
        xz = sb("xz", [P, 2, L])
        stats = sb("stats", [P, 12])
        mv = sb("mv", [P, 2])
        rstd = sb("rstd", [P, 2, 2])
        root = sb("root", [P, 2])
        psX = [ctx.enter_context(nc.psum_tensor(f"psX{i}", [P, L], F32)) for i in range(2)]
        psD = ctx.enter_context(nc.psum_tensor("psD", [DR + 2 * NST, L], F32))

        s_w = sem("p1_weights")
        s_w2 = sem("p1_weights_ctx")
        s_ctx = sem("p1_ctx_loaded")
        s_pad0 = sem("p1_padding_zero")
        s_psx = sem("p1_psum_full")
        s_pad = sem("p1_xpad_full")
        s_conv = sem("p1_conv_done")
        s_u = sem("p1_u_ready")
        s_xp = sem("p1_xproj_done")
        s_xd = sem("p1_xd_ready")
        s_xdst = sem("p1_xd_stored")
        s_exp = sem("p1_exp_done")
        s_ln = sem("p1_ln_done")
        s_cor = sem("p1_correction")
        s_lc = sem("p1_log1p")
        s_dl = sem("p1_delta")
        s_du = sem("p1_du")
        s_st = sem("p1_delta_stored")
        s_ust = sem("p1_u_stored")
        s_xz = [sem(f"p1_xz_loaded{i}") for i in range(2)]
        s_z = sem("p1_z_stats")
        s_sz = sem("p1_gate")
        s_szst = [sem(f"p1_gate_stored{i}") for i in range(2)]
        s_ch = sem("p1_dve_steps")
        s_gate = sem("p1_dve_gate")
        s_a = sem("p1_a")
        s_a2 = sem("p1_a2")
        s_ast = sem("p1_a_stored")
        block = ctx.enter_context(nc.Block())

        @block.sync
        def _(sp):
            for dst, src in ((w_x[:], io["w_x"].rearrange("(t p) k -> p t k", p=P)), (w_dt[:], io["w_dt"]),
                             (conv_w[:], io["conv_w"].rearrange("(t p) k -> p t k", p=P)),
                             (conv_b[:], io["conv_b"]), (dt_b[:], io["dt_b"]),
                             (a_neg[:], io["a_log_d"].rearrange("(t p) k -> p t k", p=P))):
                sp.dma_start(dst, src).then_inc(s_w, 16)
            sp.dma_start(w_in[:], io["w_in"].rearrange("(k p) e -> p k e", p=P)).then_inc(s_w2, 16)
            sp.wait_ge(s_a2, 1)
            sp.dma_start(dr["a"].rearrange("t p n -> p t n"), a_neg[:]).then_inc(s_ast, 16)
            def batch(b):
                after(sp, s_psx, b * 2 * ET)
                sp.dma_start(ctxT[:], io["ctxT"][b].rearrange("(k p) l -> p k l", p=P)).then_inc(s_ctx, 16)
                for et in range(ET):
                    after(sp, s_szst[et % 2], (b * (ET // 2) + et // 2) * 16)
                    sp.dma_start(xz[:, et % 2, :], io["x"][b, et * P:(et + 1) * P, :]).then_inc(s_xz[et % 2], 16)
                    if et >= 1:
                        after(sp, s_u, b * ET + et)
                        sp.dma_start(dr["u"][b * ET + et - 1], u[:, et - 1, :]).then_inc(s_ust, 16)
                        after(sp, s_sz, b * ET + et)
                        sp.dma_start(dr["sz"][b * ET + et - 1], xz[:, (et - 1) % 2, :]).then_inc(s_szst[(et - 1) % 2], 16)
                after(sp, s_u, b * ET + ET)
                sp.dma_start(dr["u"][b * ET + ET - 1], u[:, ET - 1, :]).then_inc(s_ust, 16)
                after(sp, s_sz, b * ET + ET)
                sp.dma_start(dr["sz"][b * ET + ET - 1], xz[:, (ET - 1) % 2, :]).then_inc(s_szst[(ET - 1) % 2], 16)
                after(sp, s_xd, b + 1)
                for c in range(2):
                    sp.dma_start(dr["bc"][b, :, c, :], xd[DR + c * NST:DR + (c + 1) * NST, :]).then_inc(s_xdst, 16)
                for et in range(ET):
                    after(sp, s_dl, b * ET + et + 1)
                    sp.dma_start(dr["dl"][b * ET + et], rbuf[:, et, :]).then_inc(s_st, 16)
                    after(sp, s_du, b * ET + et + 1)
                    sp.dma_start(dr["du"][b * ET + et], ebuf[:, et, :]).then_inc(s_st, 16)
            turns(sp, B, batch)
            sp.wait_ge(s_ast, 16)
            sp.wait_ge(s_ust, 16 * B * ET)
            sp.wait_ge(s_xdst, 32 * B)
            sp.wait_ge(s_st, 16 * 2 * B * ET)
            for s in s_szst:
                sp.wait_ge(s, 16 * B * ET // 2)

        @block.tensor
        def _(pe):
            pe.wait_ge(s_w, 16 * 6)
            pe.wait_ge(s_w2, 16)

            def x_proj(b, et):
                after(pe, s_u, b * ET + et + 1)
                if et == 0:
                    after(pe, s_xd, b)
                for hb in range(2):
                    mm = pe.matmul(psD[:, hb * HB:(hb + 1) * HB], w_x[:, et, :], u[:, et, hb * HB:(hb + 1) * HB],
                                   start=(et == 0), stop=(et == ET - 1))
                mm.then_inc(s_xp, 1)

            def batch(b):
                after(pe, s_ctx, b * 16 + 16)
                for et in range(ET):
                    if et < 2:
                        after(pe, s_exp, b * 2 * ET)
                    else:
                        after(pe, s_pad, b * ET + et - 1)
                    for hb in range(2):
                        for k in range(KD):
                            mm = pe.matmul(psX[et % 2][:, hb * HB:(hb + 1) * HB], w_in[:, k, et * P:(et + 1) * P],
                                           ctxT[:, k, hb * HB:(hb + 1) * HB], start=(k == 0), stop=(k == KD - 1))
                    mm.then_inc(s_psx, 1)
                    if et >= 2:
                        x_proj(b, et - 2)
                x_proj(b, ET - 2)
                x_proj(b, ET - 1)
                after(pe, s_xd, b + 1)
                for et in range(ET):
                    if et < 2:
                        after(pe, s_pad, b * ET + ET)
                    else:
                        after(pe, s_exp, b * 2 * ET + 2 * (et - 2) + 1)
                    for hb in range(2):
                        mm = pe.matmul(psX[et % 2][:, hb * HB:(hb + 1) * HB], w_dt[:, et * P:(et + 1) * P],
                                       xd[0:DR, hb * HB:(hb + 1) * HB], start=True, stop=True)
                    mm.then_inc(s_psx, 1)

            turns(pe, B, batch)

        @block.scalar
        def _(act):
            act.wait_ge(s_w, 16 * 6)
            act.activation(a_neg[:, :, 0:NST], a_neg[:, :, 0:NST], ACT.Exp).then_inc(s_a, 1)
            act.wait_ge(s_pad0, 1)

            def u_silu(b, et):
                after(act, s_conv, b * ET + et + 1)
                if et == 0:
                    after(act, s_ust, b * ET * 16)
                    after(act, s_du, b * ET)
                act.activation(u[:, et, :], conv[:, et % 2, :], ACT.Silu).then_inc(s_u, 1)

            def z_silu(b, et):
                after(act, s_z, b * ET + et + 1)
                act.activation(xz[:, et % 2, :], xz[:, et % 2, :], ACT.Silu, bias=rstd[:, et % 2, 1:2],
                               scale=rstd[:, et % 2, 0:1]).then_inc(s_sz, 1)

            def batch(b):
                for et in range(ET):
                    after(act, s_psx, b * 2 * ET + et + 1)
                    if et < 2:
                        after(act, s_conv, b * ET)
                    else:
                        after(act, s_conv, b * ET + et - 1)
                    act.activation(xpad[:, et % 2, DC - 1:DC - 1 + L], psX[et % 2][:, :],
                                   ACT.Copy).then_inc(s_pad, 1)
                    if et >= 1:
                        u_silu(b, et - 1)
                        z_silu(b, et - 1)
                u_silu(b, ET - 1)
                z_silu(b, ET - 1)
                after(act, s_xp, b * ET + ET)
                after(act, s_xdst, b * 32)
                act.activation(xd[:, :], psD[:, :], ACT.Copy).then_inc(s_xd, 1)
                after(act, s_st, b * 2 * ET * 16)
                for et in range(ET):
                    after(act, s_psx, b * 2 * ET + ET + et + 1)
                    act.activation(rbuf[:, et, :], psX[et % 2][:, :], ACT.Relu, bias=dt_b[:, et:et + 1])
                    act.activation(ebuf[:, et, :], psX[et % 2][:, :], ACT.Abs,
                                   bias=dt_b[:, et:et + 1]).then_inc(s_exp, 1)
                    after(act, s_exp, b * 2 * ET + 2 * et + 1)
                    act.activation(ebuf[:, et, :], ebuf[:, et, :], ACT.Exp, scale=-1.0).then_inc(s_exp, 1)
                after(act, s_exp, b * 2 * ET + 2 * ET)
                for et in range(ET):
                    if et < 2:
                        after(act, s_dl, b * ET)
                    else:
                        after(act, s_dl, b * ET + et - 1)
                    act.activation(lbuf[:, et % 2, :], ebuf[:, et, :], ACT.Ln, bias=1.0).then_inc(s_ln, 1)

            turns(act, B, batch)

        @block.vector
        def _(dve):
            dve.memset(xpad[:, :, 0:DC - 1], 0.0).then_inc(s_pad0, 1)
            dve.wait_ge(s_a, 1)
            dve.tensor_scalar(a_neg[:, :, 0:NST], a_neg[:, :, 0:NST], -1.0, None, ALU.mult).then_inc(s_a2, 1)
            st = Steps(dve, s_ch, ET * (6 + ROOT))
            def batch(b):
                st.start(b)
                for et in range(ET):
                    after(dve, s_xz[et % 2], (b * (ET // 2) + et // 2) * 16 + 16)
                    dve.bn_stats(stats[:, 0:6], xz[:, et % 2, 0:HB])
                    st.then(dve.bn_stats(stats[:, 6:12], xz[:, et % 2, HB:L]), s_gate)
                    st.then(dve.bn_aggr(mv[:, :], stats[:, :]))
                    if et < 2:
                        after(dve, s_sz, b * ET)
                    else:
                        after(dve, s_sz, b * ET + et - 1)
                    inverse_root(st, dve, rstd[:, et % 2, 0:1], mv[:, 1:2], root)
                    dve.scalar_tensor_tensor(out=rstd[:, et % 2, 1:2], in0=mv[:, 0:1], scalar=-1.0,
                                             in1=rstd[:, et % 2, 0:1], op0=ALU.mult, op1=ALU.mult).then_inc(s_z, 1)
                    after(dve, s_pad, b * ET + et + 1)
                    if et < 2:
                        after(dve, s_u, b * ET)
                    else:
                        after(dve, s_u, b * ET + et - 1)
                    c = conv[:, et % 2, :]
                    st.then(dve.tensor_scalar(c, xpad[:, et % 2, 0:L], conv_w[:, et, 0:1], conv_b[:, et:et + 1],
                                              ALU.mult, ALU.add))
                    for k in range(1, DC - 1):
                        st.then(dve.scalar_tensor_tensor(out=c, in0=xpad[:, et % 2, k:k + L], scalar=conv_w[:, et, k:k + 1],
                                                         in1=c, op0=ALU.mult, op1=ALU.add))
                    dve.scalar_tensor_tensor(out=c, in0=xpad[:, et % 2, DC - 1:DC - 1 + L],
                                             scalar=conv_w[:, et, DC - 1:DC], in1=c, op0=ALU.mult,
                                             op1=ALU.add).then_inc(s_conv, 1)
                for et in range(ET):
                    after(dve, s_exp, b * 2 * ET + 2 * et + 2)
                    if et < 2:
                        after(dve, s_lc, b * ET)
                    else:
                        after(dve, s_lc, b * ET + et - 1)
                    c = cbuf[:, et % 2, :]
                    st.then(dve.tensor_scalar(c, ebuf[:, et, :], 1.0, 1.0, ALU.add, ALU.subtract))
                    dve.tensor_tensor(c, ebuf[:, et, :], c, ALU.subtract).then_inc(s_cor, 1)
                    if et >= 2:
                        after(dve, s_dl, b * ET + et - 1)
                        dve.tensor_tensor(ebuf[:, et - 2, :], rbuf[:, et - 2, :], u[:, et - 2, :],
                                          ALU.mult).then_inc(s_du, 1)
                for et in (ET - 2, ET - 1):
                    after(dve, s_dl, b * ET + et + 1)
                    dve.tensor_tensor(ebuf[:, et, :], rbuf[:, et, :], u[:, et, :], ALU.mult).then_inc(s_du, 1)
                st.end()

            turns(dve, B, batch)

        @block.gpsimd
        def _(pool):
            def batch(b):
                for et in range(ET):
                    after(pool, s_ln, b * ET + et + 1)
                    after(pool, s_cor, b * ET + et + 1)
                    pool.tensor_tensor(lbuf[:, et % 2, :], lbuf[:, et % 2, :], cbuf[:, et % 2, :], ALU.add).then_inc(s_lc, 1)
                    after(pool, s_lc, b * ET + et + 1)
                    pool.tensor_tensor(rbuf[:, et, :], rbuf[:, et, :], lbuf[:, et % 2, :], ALU.add).then_inc(s_dl, 1)

            turns(pool, B, batch)


def selective_scan(nc, io, dr):
    with ExitStack() as ctx:
        sb = lambda name, shape, dt=F32: ctx.enter_context(nc.sbuf_tensor(name, shape, dt))
        sem = lambda name: ctx.enter_context(nc.semaphore(name))
        NU = B * ET
        HR = 4
        ident = sb("ident2", [P, P])
        gate = sb("gate2", [P, 1])
        bc = sb("bc", [P, NST, 2, L])
        ad = sb("ad", [P, 2, NST + 1])
        dl = sb("dl", [P, 2, L])
        du = sb("du", [P, 2, L])
        ut = sb("ut", [P, 2, L])
        sz = sb("szt", [P, 2, L])
        xl = sb("xl", [P, 2, L])
        dbu = sb("dbu", [P, 2, L])
        h = sb("h", [P, HR, L])
        hc = sb("hc", [P, 2, L])
        yt = sb("yt", [P, L])
        da = [ctx.enter_context(nc.psum_tensor(f"da{i}", [P, L], F32)) for i in range(2)]
        psy = ctx.enter_context(nc.psum_tensor("psy", [P, L], F32))
        pst = ctx.enter_context(nc.psum_tensor("pst", [P, ET, P], F32))

        s_c = sem("p2_constants")
        s_gate = sem("p2_gate")
        s_bc = [sem(f"p2_bc_loaded{n}") for n in range(NST)]
        s_ld = [sem(f"p2_unit_loaded{i}") for i in range(2)]
        s_ul = [sem(f"p2_u_gate_loaded{i}") for i in range(2)]
        s_xl = [sem(f"p2_x_loaded{i}") for i in range(2)]
        s_xst = [sem(f"p2_x1_stored{i}") for i in range(2)]
        s_da = sem("p2_decay")
        s_dbu = sem("p2_input")
        s_scan = sem("p2_state")
        s_hc = sem("p2_state_times_c")
        s_ys = sem("p2_summed")
        s_t1 = sem("p2_skip_added")
        s_t2 = sem("p2_gated")
        s_tr = sem("p2_transposed")
        s_add = sem("p2_x1")
        block = ctx.enter_context(nc.Block())

        @block.sync
        def _(sp):
            def load(i, par):
                sp.dma_start(dl[:, par, :], dr["dl"][i]).then_inc(s_ld[par], 16)
                sp.dma_start(du[:, par, :], dr["du"][i]).then_inc(s_ld[par], 16)
                sp.dma_start(ad[:, par, :], dr["a"][i % ET]).then_inc(s_ld[par], 16)
                sp.dma_start(ut[:, par, :], dr["u"][i]).then_inc(s_ul[par], 16)
                sp.dma_start(sz[:, par, :], dr["sz"][i]).then_inc(s_ul[par], 16)

            def store(i, b, et):
                sp.dma_start(dr["x1"][b].rearrange("(t p) (e c) -> e p t c", p=P, c=P)[et],
                             xl[:, et % 2, :].rearrange("p (t c) -> p t c", c=P)).then_inc(s_xst[et % 2], 16)

            sp.dma_start(ident[:], io["ident"]).then_inc(s_c, 16)
            sp.dma_start(gate[:], io["g_x"].partition_broadcast(P)).then_inc(s_c, 16)
            load(0, 0)
            for n in range(NST):
                sp.dma_start(bc[:, n], dr["bc"][0, n].partition_broadcast(P)).then_inc(s_bc[n], 16)

            def batch(b):
                for et in range(ET):
                    i = b * ET + et
                    first = isinstance(b, int) and i == 0
                    final = isinstance(b, int) and i == NU - 1
                    after(sp, s_add, i if not first else 0)
                    if not first:
                        store(i - 1, b if et else b - 1, (et - 1) % ET)
                    if not final:
                        load(i + 1, (et + 1) % 2)
                    after(sp, s_xst[et % 2], (b * (ET // 2) + et // 2) * 16)
                    sp.dma_start(xl[:, et % 2, :].rearrange("p (t c) -> p t c", c=P),
                                 io["x"][b].rearrange("(t p) (e c) -> e p t c", p=P, c=P)[et]).then_inc(s_xl[et % 2], 16)
                if not (isinstance(b, int) and b == B - 1):
                    for n in range(NST):
                        sp.wait_ge(s_hc, b * ET * NST + (ET - 1) * NST + n + 1)
                        sp.dma_start(bc[:, n], dr["bc"][b + 1, n].partition_broadcast(P)).then_inc(s_bc[n], 16)

            turns(sp, B, batch, last=True)
            sp.wait_ge(s_add, NU)
            store(NU - 1, B - 1, ET - 1)
            for s in s_xst:
                sp.wait_ge(s, 16 * NU // 2)

        @block.scalar
        def _(act):
            act.wait_ge(s_c, 32)
            act.activation(gate[:], gate[:], ACT.Tanh).then_inc(s_gate, 1)

            def pair(j):
                for par in range(2):
                    i = j * 2 + par
                    act.wait_ge(s_ld[par], j * 48 + 48)
                    for n in range(NST):
                        after(act, s_scan, i * NST + n - 1)
                        act.activation(da[n % 2][:, :], dl[:, par, :], ACT.Exp, scale=ad[:, par, n:n + 1]).then_inc(s_da, 1)

            turns(act, NU // 2, pair)

        @block.gpsimd
        def _(pool):
            def pair(j):
                for par in range(2):
                    i = j * 2 + par
                    pool.wait_ge(s_ld[par], j * 48 + 48)
                    for n in range(NST):
                        pool.wait_ge(s_bc[n], (j // (ET // 2)) * 16 + 16)
                        after(pool, s_scan, i * NST + n - 1)
                        pool.tensor_tensor(dbu[:, n % 2, :], du[:, par, :], bc[:, n, 0, :], ALU.mult).then_inc(s_dbu, 1)

            turns(pool, NU // 2, pair)

        @block.vector
        def _(dve):
            def times_c(i, n):
                dve.wait_ge(s_scan, i * NST + n + 1)
                after(dve, s_ys, i * NST + n - 1)
                dve.tensor_tensor(hc[:, n % 2, :], h[:, n % HR, :], bc[:, n, 1, :], ALU.mult).then_inc(s_hc, 1)

            def skip_and_gate(i, j, par):
                dve.wait_ge(s_ul[par], j * 32 + 32)
                dve.wait_ge(s_ys, i * NST + NST)
                after(dve, s_tr, i)
                dve.scalar_tensor_tensor(out=yt[:, :], in0=ut[:, par, :], scalar=ad[:, par, NST:NST + 1],
                                         in1=psy[:, :], op0=ALU.mult, op1=ALU.add).then_inc(s_t1, 1)
                dve.wait_ge(s_t1, i + 1)
                dve.scalar_tensor_tensor(out=yt[:, :], in0=yt[:, :], scalar=gate[:, 0:1], in1=sz[:, par, :],
                                         op0=ALU.mult, op1=ALU.mult).then_inc(s_t2, 1)

            def residual(i, j, par):
                dve.wait_ge(s_xl[par], j * 16 + 16)
                dve.wait_ge(s_tr, i + 1)
                dve.tensor_tensor(xl[:, par, :], xl[:, par, :], pst[:, :, :].rearrange("p t c -> p (t c)"),
                                  ALU.add).then_inc(s_add, 1)

            def pair(j):
                for par in range(2):
                    i = j * 2 + par
                    first = isinstance(j, int) and i == 0
                    for n in range(NST):
                        dve.wait_ge(s_da, i * NST + n + 1)
                        dve.wait_ge(s_dbu, i * NST + n + 1)
                        after(dve, s_hc, i * NST + n - HR + 1)
                        dve.tensor_tensor_scan(h[:, n % HR, :], da[n % 2][:, :], dbu[:, n % 2, :], 0.0, ALU.mult,
                                               ALU.add).then_inc(s_scan, 1)
                        if n:
                            times_c(i, n - 1)
                        elif not first:
                            times_c(i - 1, NST - 1)
                        if n == 2 and not first:
                            skip_and_gate(i - 1, j - (par == 0), 1 - par)
                        if n == 5 and not first:
                            residual(i - 1, j - (par == 0), 1 - par)

            dve.wait_ge(s_gate, 1)
            turns(dve, NU // 2, pair)
            times_c(NU - 1, NST - 1)
            skip_and_gate(NU - 1, NU // 2 - 1, 1)
            residual(NU - 1, NU // 2 - 1, 1)

        @block.tensor
        def _(pe):
            pe.wait_ge(s_c, 32)

            def spread(i):
                pe.wait_ge(s_t2, i + 1)
                after(pe, s_add, i)
                for t in range(L // P):
                    mm = pe.transpose(pst[:, t, :], yt[:, t * P:(t + 1) * P], ident[:])
                mm.then_inc(s_tr, 1)

            def pair(j):
                for par in range(2):
                    i = j * 2 + par
                    first = isinstance(j, int) and i == 0
                    for n in range(NST):
                        if n == 0:
                            after(pe, s_t1, i)
                        pe.wait_ge(s_hc, i * NST + n + 1)
                        for hb in range(2):
                            mm = pe.matmul(psy[:, hb * HB:(hb + 1) * HB], ident[:], hc[:, n % 2, hb * HB:(hb + 1) * HB],
                                           start=(n == 0), stop=(n == NST - 1))
                        mm.then_inc(s_ys, 1)
                        if n == 1 and not first:
                            spread(i - 1)

            turns(pe, NU // 2, pair)
            spread(NU - 1)


def route_and_shared(nc, io, dr, slots, weights):
    with ExitStack() as ctx:
        sb = lambda name, shape, dt=F32: ctx.enter_context(nc.sbuf_tensor(name, shape, dt))
        ps = lambda name, shape: ctx.enter_context(nc.psum_tensor(name, shape, F32))
        sem = lambda name: ctx.enter_context(nc.semaphore(name))
        EG = NE // NG
        FC = FS // HB
        wg, wu = sb("wg", [P, KH, FS]), sb("wu", [P, KH, FS])
        wd = sb("wd", [P, FS // P, H])
        ident = sb("ident3", [P, P])
        tri = sb("tri", [P, P])
        ones = sb("ones3", [P, P])
        iota = sb("iota", [P, NE])
        lower = sb("lower", [P, NG, NG])
        bias = sb("bias", [P, NE])
        gw = sb("gw", [P, KH, NE])
        gate = sb("gate3", [P, 1])
        gate2 = sb("gate3_scaled", [P, 1])
        tok = sb("tok", [P, 2], I32)
        step = sb("token_step", [P, 1], I32)
        zero = sb("zero_table", [P, NE * CAP // P], I32)
        xt = sb("xt", [P, 2, H])
        xn = sb("xn", [P, 2, H])
        xT = sb("xT", [P, KH, P])
        sg = sb("sg", [P, FC, HB])
        hs = sb("hs", [P, FC, HB])
        hT = sb("hT", [P, FS // P, P])
        ac = sb("ac", [P, 2, H])
        stats = sb("stats3", [P, 12])
        mv = sb("mv3", [P, 2])
        root = sb("root3", [P, 2])
        rstd = sb("rstd3", [P, 1])
        th = sb("th", [P, NE])
        scores = sb("scores", [P, NE])
        sc = sb("sc", [P, NG, EG])
        gm = sb("gm", [P, NG, 8])
        gs = sb("gs", [P, NG])
        gt = sb("gt", [P, NG, NG])
        eq = sb("eq", [P, NG, NG])
        rank = sb("rank", [P, NG])
        m8 = sb("m8", [P, 8])
        i8 = sb("i8", [P, 8], U32)
        idx = sb("idx", [P, TOPK])
        oh = sb("oh", [P, TOPK, NE])
        ow = sb("ow", [P, TOPK, NE])
        mask = sb("mask", [P, NE])
        run = sb("run", [P, NE])
        w4 = sb("w4", [P, TOPK])
        ws = sb("ws", [P, 2])
        pos = sb("pos", [P, TOPK])
        over = sb("over", [P, TOPK])
        sf = sb("sf", [P, TOPK])
        si = sb("si", [P, 2, TOPK], I32)
        psG, psU, psR = ps("psG", [P, HB]), ps("psU", [P, HB]), ps("psR", [P, HB])
        psO, psX, psH = ps("psO", [P, H]), ps("psXT", [P, KH, P]), ps("psH", [P, HB // P, P])

        s_c = sem("p3_constants")
        s_w = sem("p3_weights")
        s_tanh = sem("p3_gate")
        s_init = sem("p3_initialised")
        s_tab = sem("p3_table_zero")
        s_x = [sem(f"p3_x1_loaded{i}") for i in range(2)]
        s_xnst = [sem(f"p3_xn_stored{i}") for i in range(2)]
        s_acst = [sem(f"p3_acc_stored{i}") for i in range(2)]
        s_sct = [sem(f"p3_tokens_scattered{i}") for i in range(2)]
        s_tok = sem("p3_token_ids")
        s_ch = sem("p3_dve_steps")
        s_ln = sem("p3_norm_steps")
        s_fence = sem("p3_dve_gate")
        s_xn = sem("p3_xn")
        s_xtr = sem("p3_xn_transposed")
        s_xT = sem("p3_xT_copied")
        s_lg = sem("p3_logits")
        s_th = sem("p3_logits_tanh")
        s_g = sem("p3_gate_product")
        s_u = sem("p3_up_product")
        s_sg = sem("p3_silu")
        s_h = sem("p3_hidden")
        s_htr = sem("p3_hidden_transposed")
        s_hT = sem("p3_hT_copied")
        s_d = sem("p3_down_product")
        s_ac = sem("p3_acc")
        s_mask = sem("p3_mask")
        s_pos = sem("p3_positions")
        s_posr = sem("p3_positions_read")
        s_slot = sem("p3_slots")
        s_carry = sem("p3_pool_carry")
        block = ctx.enter_context(nc.Block())
        x1 = dr["x1"].rearrange("b (t p) h -> (b t) p h", p=P)

        def split(j, par):
            t = j * 2 + par
            return t, isinstance(t, int) and t == 0, isinstance(t, int) and t == TT - 1

        @block.sync
        def _(sp):
            for dst, src in ((ident[:], io["ident"]), (tri[:], io["tri"]), (iota[:], io["iota"].partition_broadcast(P)),
                             (lower[:].rearrange("p a b -> p (a b)"), io["lower"].partition_broadcast(P)),
                             (bias[:], io["gate_b"].partition_broadcast(P)), (tok[:], io["tok"]),
                             (gw[:], io["gate_w"].rearrange("(k p) e -> p k e", p=P)),
                             (gate[:], io["g_f"].partition_broadcast(P))):
                sp.dma_start(dst, src).then_inc(s_c, 16)
            sp.dma_start(xt[:, 0, :], x1[0]).then_inc(s_x[0], 16)
            for dst, src in ((wg, io["w_sg"]), (wu, io["w_su"]), (wd, io["w_sd"])):
                sp.dma_start(dst[:], src.rearrange("(k p) f -> p k f", p=P)).then_inc(s_w, 16)
            sp.wait_ge(s_init, 1)
            sp.dma_start(dr["tab"].rearrange("(p s) o -> p (s o)", p=P), zero[:]).then_inc(s_tab, 16)

            def pair(j):
                for par in range(2):
                    t, first, last = split(j, par)
                    after(sp, s_ac, t)
                    if not last:
                        sp.dma_start(xt[:, 1 - par, :], x1[t + 1]).then_inc(s_x[1 - par], 16)
                    if not first:
                        sp.dma_start(dr["acc"][t - 1], ac[:, 1 - par, :]).then_inc(s_acst[1 - par], 16)
                    sp.wait_ge(s_xn, t + 1)
                    sp.dma_start(dr["xn"].rearrange("(t p) h -> t p h", p=P)[t], xn[:, par, :]).then_inc(s_xnst[par], 16)

            turns(sp, TT // 2, pair, last=True)
            sp.wait_ge(s_ac, TT)
            sp.dma_start(dr["acc"][TT - 1], ac[:, 1, :]).then_inc(s_acst[1], 16)
            for s in (*s_xnst, *s_acst):
                sp.wait_ge(s, 16 * TT // 2)

        @block.gpsimd
        def _(pool):
            pool.memset(ones[:], 1.0)
            pool.memset(run[:], 0.0)
            pool.memset(step[:], 2 * P)
            pool.memset(zero[:], 0).then_inc(s_init, 1)
            pool.wait_ge(s_tab, 16)
            pool.wait_ge(s_c, 128)

            def pair(j):
                for par in range(2):
                    t, first, last = split(j, par)
                    if not (isinstance(j, int) and j == 0):
                        pool.wait_ge(s_sct[par], j * 16 * TOPK)
                        pool.tensor_tensor(tok[:, par:par + 1], tok[:, par:par + 1], step[:], ALU.add).then_inc(s_tok, 1)
                        pool.wait_ge(s_tok, t - 1)
                    pool.wait_ge(s_slot, t + 1)
                    pool.sem_inc(s_carry, 1)
                    for k in range(TOPK):
                        pool.indirect_dma_start(dr["tab"], bass.IndirectOffsetOnAxis(ap=si[:, par, k:k + 1], axis=0),
                                                tok[:, par:par + 1], None, bounds_check=NE * CAP - 1,
                                                oob_is_err=False).then_inc(s_sct[par], 16)

            turns(pool, TT // 2, pair)
            for s in s_sct:
                pool.wait_ge(s, 16 * TOPK * TT // 2)

        @block.tensor
        def _(pe):
            pe.wait_ge(s_c, 128)
            pe.wait_ge(s_init, 1)

            def x_transpose(t, par):
                pe.wait_ge(s_xn, t + 1)
                after(pe, s_xT, 2 * t)
                for k in range(KH):
                    mm = pe.transpose(psX[:, k, :], xn[:, par, k * P:(k + 1) * P], ident[:])
                mm.then_inc(s_xtr, 1)

            def product(dst, w, c, done):
                for k in range(KH):
                    mm = pe.matmul(dst[:], xT[:, k, :], w[:, k, c * HB:(c + 1) * HB], start=(k == 0), stop=(k == KH - 1))
                mm.then_inc(done, 1)

            def h_transpose(t, c):
                pe.wait_ge(s_h, FC * t + c + 1)
                after(pe, s_hT, FC * t + c)
                for k in range(HB // P):
                    mm = pe.transpose(psH[:, k, :], hs[:, c, k * P:(k + 1) * P], ident[:])
                mm.then_inc(s_htr, 1)

            def tile(t, par, last):
                pe.wait_ge(s_xT, 2 * t + 2)
                after(pe, s_posr, t)
                for k in range(KH):
                    mm = pe.matmul(psR[:, 0:NE], xT[:, k, :], gw[:, k, :], start=(k == 0), stop=(k == KH - 1))
                mm.then_inc(s_lg, 1)
                if isinstance(t, int) and t == 0:
                    pe.wait_ge(s_w, 48)
                for c in range(FC):
                    after(pe, s_sg, FC * t + c)
                    product(psG, wg, c, s_g)
                    if c:
                        h_transpose(t, c - 1)
                    after(pe, s_h, FC * t + c)
                    product(psU, wu, c, s_u)
                pe.wait_ge(s_mask, t + 1)
                pe.matmul(psR[:, NE:2 * NE], tri[:], mask[:], start=True, stop=False)
                pe.matmul(psR[:, NE:2 * NE], ones[:], run[:], start=False, stop=True).then_inc(s_pos, 1)
                if not last:
                    x_transpose(t + 1, 1 - par)
                h_transpose(t, FC - 1)
                pe.wait_ge(s_hT, FC * t + FC)
                after(pe, s_ac, t)
                for hb in range(H // HB):
                    for k in range(FS // P):
                        mm = pe.matmul(psO[:, hb * HB:(hb + 1) * HB], hT[:, k, :], wd[:, k, hb * HB:(hb + 1) * HB],
                                       start=(k == 0), stop=(k == FS // P - 1))
                mm.then_inc(s_d, 1)

            def pair(j):
                for par in range(2):
                    t, first, last = split(j, par)
                    tile(t, par, last)

            x_transpose(0, 0)
            turns(pe, TT // 2, pair, last=True)

        @block.scalar
        def _(act):
            act.wait_ge(s_c, 128)
            act.activation(gate[:], gate[:], ACT.Tanh).then_inc(s_tanh, 1)

            def x_copy(t):
                act.wait_ge(s_xtr, t + 1)
                after(act, s_u, FC * t)
                for hb in range(2):
                    act.activation(xT[:, 4 * hb:4 * hb + 4, :], psX[:, 4 * hb:4 * hb + 4, :], ACT.Copy).then_inc(s_xT, 1)

            def h_copy(t, c):
                act.wait_ge(s_htr, FC * t + c + 1)
                after(act, s_d, t)
                act.activation(hT[:, 4 * c:4 * c + 4, :], psH[:, :, :], ACT.Copy).then_inc(s_hT, 1)

            def pair(j):
                for par in range(2):
                    t, first, last = split(j, par)
                    act.wait_ge(s_lg, t + 1)
                    after(act, s_ch, t * ROUTE)
                    act.activation(th[:], psR[:, 0:NE], ACT.Tanh, scale=0.5).then_inc(s_th, 1)
                    for c in range(FC):
                        act.wait_ge(s_g, FC * t + c + 1)
                        after(act, s_h, FC * (t - 1) + c + 1 if not first else 0)
                        act.activation(sg[:, c, :], psG[:], ACT.Silu).then_inc(s_sg, 1)
                        if c:
                            h_copy(t, c - 1)
                    if not last:
                        x_copy(t + 1)
                    h_copy(t, FC - 1)

            x_copy(0)
            turns(act, TT // 2, pair, last=True)

        @block.vector
        def _(dve):
            st = Steps(dve, s_ch, ROUTE)
            ln = Steps(dve, s_ln, ROOT + 2)

            def norm(t, par, first):
                ln.start(t)
                after(dve, s_xn, t)
                dve.wait_ge(s_x[par], (t // 2) * 16 + 16)
                dve.bn_stats(stats[:, 0:6], xt[:, par, 0:HB])
                ln.then(dve.bn_stats(stats[:, 6:12], xt[:, par, HB:H]), s_fence)
                ln.then(dve.bn_aggr(mv[:], stats[:]))
                inverse_root(ln, dve, rstd[:], mv[:, 1:2], root)
                if not first:
                    dve.wait_ge(s_xtr, t - 1)
                    dve.wait_ge(s_xnst[par], (t // 2) * 16)
                ins = dve.tensor_scalar(xn[:, par, :], xt[:, par, :], mv[:, 0:1], rstd[:], ALU.subtract, ALU.mult)
                ins.then_inc(s_xn, 1)
                ln.end()

            def residual(t, par):
                dve.wait_ge(s_d, t + 1)
                after(dve, s_acst[par], (t // 2) * 16)
                dve.scalar_tensor_tensor(out=ac[:, par, :], in0=psO[:], scalar=gate[:, 0:1], in1=xt[:, par, :],
                                         op0=ALU.mult, op1=ALU.add).then_inc(s_ac, 1)

            def choose(t):
                st.start(t)
                dve.wait_ge(s_th, t + 1)
                scf = sc[:].rearrange("p g e -> p (g e)")
                st.then(dve.tensor_scalar(scores[:], th[:], 0.5, 0.5, ALU.mult, ALU.add))
                st.then(dve.tensor_tensor(scf, scores[:], bias[:], ALU.add), s_fence)
                for g in range(NG):
                    ins = dve.max(gm[:, g, :], sc[:, g, :])
                st.then(ins)
                st.then(dve.tensor_tensor(gs[:], gm[:, :, 0], gm[:, :, 1], ALU.add))
                other = gs[:].unsqueeze(1).to_broadcast([P, NG, NG])
                mine = gs[:].unsqueeze(2).to_broadcast([P, NG, NG])
                st.then(dve.tensor_tensor(gt[:], other, mine, ALU.is_gt))
                st.then(dve.tensor_tensor(eq[:], other, mine, ALU.is_equal))
                st.then(dve.tensor_tensor(eq[:], eq[:], lower[:], ALU.mult))
                st.then(dve.tensor_tensor(gt[:], gt[:], eq[:], ALU.add))
                st.then(dve.tensor_reduce(rank[:], gt[:], AX, ALU.add))
                st.then(dve.tensor_scalar(rank[:], rank[:], float(TG), None, ALU.is_lt))
                st.then(dve.tensor_tensor(sc[:], sc[:], rank[:].unsqueeze(2).to_broadcast([P, NG, EG]), ALU.mult), s_fence)
                st.then(dve.max(m8[:], scf), s_fence)
                st.then(dve.max_index(i8[:], m8[:], scf))
                st.then(dve.tensor_copy(idx[:], i8[:, 0:TOPK]))
                st.then(dve.tensor_tensor(oh[:], iota[:].unsqueeze(1).to_broadcast([P, TOPK, NE]),
                                          idx[:].unsqueeze(2).to_broadcast([P, TOPK, NE]), ALU.is_equal))
                after(dve, s_pos, t)
                dve.tensor_reduce(mask[:], oh[:].rearrange("p k e -> p e k"), AX, ALU.add).then_inc(s_mask, 1)
                st.then(dve.tensor_tensor(ow[:], oh[:], scores[:].unsqueeze(1).to_broadcast([P, TOPK, NE]), ALU.mult))
                st.then(dve.tensor_reduce(w4[:], ow[:], AX, ALU.add))
                st.then(dve.tensor_reduce(ws[:, 0:1], w4[:], AX, ALU.add))
                st.then(dve.tensor_scalar(ws[:, 0:1], ws[:, 0:1], 1e-20, None, ALU.add))
                st.then(dve.reciprocal(ws[:, 1:2], ws[:, 0:1]))
                st.then(dve.tensor_scalar(w4[:], w4[:], ws[:, 1:2], gate2[:, 0:1], ALU.mult, ALU.mult))

            def queue(t, j, par):
                dve.wait_ge(s_pos, t + 1)
                dve.tensor_tensor(ow[:], oh[:], psR[:, NE:2 * NE].unsqueeze(1).to_broadcast([P, TOPK, NE]),
                                  ALU.mult).then_inc(s_posr, 1)
                dve.wait_ge(s_mask, t + 1)
                dve.wait_ge(s_posr, t + 1)
                st.then(dve.tensor_tensor(run[:], run[:], mask[:], ALU.add))
                st.then(dve.tensor_reduce(pos[:], ow[:], AX, ALU.add))
                st.then(dve.tensor_scalar(over[:], pos[:], float(CAP), float(DROPPED), ALU.is_ge, ALU.mult))
                st.then(dve.scalar_tensor_tensor(out=sf[:], in0=idx[:], scalar=float(CAP), in1=pos[:], op0=ALU.mult,
                                                 op1=ALU.add))
                st.then(dve.tensor_tensor(sf[:], sf[:], over[:], ALU.add))
                after(dve, s_sct[par], j * 16 * TOPK)
                dve.tensor_copy(si[:, par, :], sf[:]).then_inc(s_slot, 1)
                dve.scalar_tensor_tensor(out=weights[:, bass.ds(t * TOPK, TOPK)], in0=pos[:], scalar=float(CAP), in1=w4[:],
                                         op0=ALU.is_lt, op1=ALU.mult)
                st.then(dve.tensor_copy(slots[:, bass.ds(t * TOPK, TOPK)], sf[:]))
                st.end()

            def pair(j):
                for par in range(2):
                    t, first, last = split(j, par)
                    if not first:
                        residual(t - 1, 1 - par)
                    if not last:
                        norm(t + 1, 1 - par, first)
                    choose(t)
                    for c in range(FC):
                        dve.wait_ge(s_sg, FC * t + c + 1)
                        dve.wait_ge(s_u, FC * t + c + 1)
                        after(dve, s_htr, FC * (t - 1) + c + 1 if not first else 0)
                        dve.tensor_tensor(hs[:, c, :], sg[:, c, :], psU[:], ALU.mult).then_inc(s_h, 1)
                    queue(t, j, par)

            dve.wait_ge(s_c, 128)
            dve.wait_ge(s_tanh, 1)
            dve.wait_ge(s_init, 1)
            dve.tensor_scalar(gate2[:], gate[:], SCALE, None, ALU.mult)
            norm(0, 0, True)
            turns(dve, TT // 2, pair, last=True, first=2)
            residual(TT - 1, 1)


def experts(nc, io, dr):
    with ExitStack() as ctx:
        sb = lambda name, shape, dt=F32: ctx.enter_context(nc.sbuf_tensor(name, shape, dt))
        ps = lambda name, shape: ctx.enter_context(nc.psum_tensor(name, shape, F32))
        sem = lambda name: ctx.enter_context(nc.semaphore(name))
        KF = F // P
        IR = 4
        w1, w3 = sb("w1", [P, 2, KH, F]), sb("w3", [P, 2, KH, F])
        w2 = sb("w2", [P, 2, KF, H])
        ident = sb("ident4", [P, P])
        ids = sb("ids", [P, IR], I32)
        xg = sb("xg", [P, 2, H])
        xT = sb("xgT", [P, KH, P])
        sg = sb("sg4", [P, F])
        hs = sb("hs4", [P, F])
        hT = sb("hT4", [P, KF, P])
        ob = sb("ob", [P, 2, H])
        psG, psU = ps("psG4", [P, F]), ps("psU4", [P, F])
        psO, psX, psH = ps("psO4", [P, H]), ps("psX4", [P, KH, P]), ps("psH4", [P, KF, P])

        s_c = sem("p4_constants")
        s_w13 = [sem(f"p4_w1_w3_loaded{i}") for i in range(2)]
        s_w2 = [sem(f"p4_w2_loaded{i}") for i in range(2)]
        s_ids = [sem(f"p4_ids_loaded{i}") for i in range(IR)]
        s_gat = [sem(f"p4_rows_gathered{i}") for i in range(2)]
        s_obst = [sem(f"p4_rows_stored{i}") for i in range(2)]
        s_xtr = sem("p4_rows_transposed")
        s_xT = sem("p4_xT_copied")
        s_g = sem("p4_gate_product")
        s_u = sem("p4_up_product")
        s_sg = sem("p4_silu")
        s_h = sem("p4_hidden")
        s_htr = sem("p4_hidden_transposed")
        s_hT = sem("p4_hT_copied")
        s_d = sem("p4_down_product")
        s_oa = sem("p4_out_first_half")
        s_ob = sem("p4_out_second_half")
        s_carry = sem("p4_pool_carry")
        block = ctx.enter_context(nc.Block())

        def fixed(s):
            return s if isinstance(s, int) else None

        def four(body):
            def turn(j):
                for q in range(4):
                    body(j * 4 + q, j, q)
            return turn

        @block.sync
        def _(sp):
            tab = dr["tab"].rearrange("(s p) o -> s p o", p=P)

            def load_ids(s, r):
                sp.dma_start(ids[:, r:r + 1], tab[s]).then_inc(s_ids[r], 16)

            def load_up(e, par):
                for w, src in ((w1, io["w1"]), (w3, io["w3"])):
                    sp.dma_start(w[:, par], src[e].rearrange("(k p) f -> p k f", p=P)).then_inc(s_w13[par], 16)

            def load_down(e, par):
                sp.dma_start(w2[:, par], io["w2"][e].rearrange("(k p) h -> p k h", p=P)).then_inc(s_w2[par], 16)

            sp.dma_start(ident[:], io["ident"]).then_inc(s_c, 16)
            for r in range(IR - 1):
                load_ids(r, r)
            load_up(0, 0)
            load_down(0, 0)
            load_up(1, 1)
            load_down(1, 1)

            def tile(s, j, q):
                n = fixed(s)
                if n is None or n + IR - 1 < ST:
                    if n != 0:
                        sp.wait_ge(s_gat[(q - 1) % 2], ((s - 1) // 2) * 16 + 16)
                    load_ids(s + IR - 1, (q + IR - 1) % IR)
                if q % 2 == 0 and n != 0 and (n is None or n // 2 + 1 < NE):
                    sp.wait_ge(s_u, s)
                    load_up(s // 2 + 1, (q // 2 + 1) % 2)
                    sp.wait_ge(s_d, s)
                    load_down(s // 2 + 1, (q // 2 + 1) % 2)
                if n != 0:
                    sp.wait_ge(s_oa, s)
                    sp.wait_ge(s_ob, s)
                    sp.dma_start(dr["ob"].rearrange("(s p) h -> s p h", p=P)[s - 1], ob[:, (q - 1) % 2, :])\
                        .then_inc(s_obst[(q - 1) % 2], 16)

            turns(sp, ST // 4, four(tile), last=True)
            sp.wait_ge(s_oa, ST)
            sp.wait_ge(s_ob, ST)
            sp.dma_start(dr["ob"].rearrange("(s p) h -> s p h", p=P)[ST - 1], ob[:, 1, :]).then_inc(s_obst[1], 16)
            for s in s_obst:
                sp.wait_ge(s, 16 * ST // 2)

        @block.gpsimd
        def _(pool):
            def tile(s, j, q):
                pool.wait_ge(s_ids[q], j * 16 + 16)
                after(pool, s_xtr, s - 1)
                pool.sem_inc(s_carry, 1)
                pool.indirect_dma_start(xg[:, q % 2, :], None, dr["xn"],
                                        bass.IndirectOffsetOnAxis(ap=ids[:, q:q + 1], axis=0),
                                        bounds_check=NT - 1, oob_is_err=False).then_inc(s_gat[q % 2], 16)

            turns(pool, ST // 4, four(tile))

        @block.tensor
        def _(pe):
            pe.wait_ge(s_c, 16)

            def x_transpose(s, q):
                pe.wait_ge(s_gat[q % 2], (s // 2) * 16 + 16)
                after(pe, s_xT, 2 * s)
                for k in range(KH):
                    mm = pe.transpose(psX[:, k, :], xg[:, q % 2, k * P:(k + 1) * P], ident[:])
                mm.then_inc(s_xtr, 1)

            def down(s, q):
                e = s // 2
                pe.wait_ge(s_hT, s + 1)
                pe.wait_ge(s_w2[(q // 2) % 2], (e // 2) * 16 + 16)
                after(pe, s_oa, s)
                after(pe, s_ob, s)
                for hb in range(H // HB):
                    for k in range(KF):
                        mm = pe.matmul(psO[:, hb * HB:(hb + 1) * HB], hT[:, k, :],
                                       w2[:, (q // 2) % 2, k, hb * HB:(hb + 1) * HB], start=(k == 0), stop=(k == KF - 1))
                mm.then_inc(s_d, 1)

            def tile(s, j, q):
                par = q // 2
                pe.wait_ge(s_xT, 2 * s + 2)
                pe.wait_ge(s_w13[par], j * 32 + 32)
                after(pe, s_sg, s)
                for k in range(KH):
                    mm = pe.matmul(psG[:], xT[:, k, :], w1[:, par, k, :], start=(k == 0), stop=(k == KH - 1))
                mm.then_inc(s_g, 1)
                after(pe, s_h, s)
                for k in range(KH):
                    mm = pe.matmul(psU[:], xT[:, k, :], w3[:, par, k, :], start=(k == 0), stop=(k == KH - 1))
                mm.then_inc(s_u, 1)
                if fixed(s) != ST - 1:
                    x_transpose(s + 1, q + 1)
                if fixed(s) != 0:
                    down(s - 1, (q - 1) % 4)
                pe.wait_ge(s_h, s + 1)
                after(pe, s_hT, s)
                for k in range(KF):
                    mm = pe.transpose(psH[:, k, :], hs[:, k * P:(k + 1) * P], ident[:])
                mm.then_inc(s_htr, 1)

            x_transpose(0, 0)
            turns(pe, ST // 4, four(tile), last=True)
            down(ST - 1, 3)

        @block.scalar
        def _(act):
            def x_copy(s):
                act.wait_ge(s_xtr, s + 1)
                after(act, s_u, s)
                for hb in range(2):
                    act.activation(xT[:, 4 * hb:4 * hb + 4, :], psX[:, 4 * hb:4 * hb + 4, :], ACT.Copy).then_inc(s_xT, 1)

            def out_half(s, par):
                act.wait_ge(s_d, s + 1)
                after(act, s_obst[par], (s // 2) * 16)
                act.activation(ob[:, par, 0:HB], psO[:, 0:HB], ACT.Copy).then_inc(s_oa, 1)

            def tile(s, j, q):
                act.wait_ge(s_g, s + 1)
                after(act, s_h, s)
                act.activation(sg[:], psG[:], ACT.Silu).then_inc(s_sg, 1)
                if fixed(s) != ST - 1:
                    x_copy(s + 1)
                if fixed(s) != 0:
                    out_half(s - 1, (q - 1) % 2)
                act.wait_ge(s_htr, s + 1)
                after(act, s_d, s)
                act.activation(hT[:], psH[:], ACT.Copy).then_inc(s_hT, 1)

            x_copy(0)
            turns(act, ST // 4, four(tile), last=True)
            out_half(ST - 1, 1)

        @block.vector
        def _(dve):
            def out_half(s, par):
                dve.wait_ge(s_d, s + 1)
                after(dve, s_obst[par], (s // 2) * 16)
                dve.tensor_copy(ob[:, par, HB:H], psO[:, HB:H]).then_inc(s_ob, 1)

            def tile(s, j, q):
                dve.wait_ge(s_sg, s + 1)
                dve.wait_ge(s_u, s + 1)
                after(dve, s_htr, s)
                dve.tensor_tensor(hs[:], sg[:], psU[:], ALU.mult).then_inc(s_h, 1)
                if fixed(s) != 0:
                    out_half(s - 1, (q - 1) % 2)

            turns(dve, ST // 4, four(tile))
            out_half(ST - 1, 1)


def combine(nc, io, dr, out, slots, weights):
    with ExitStack() as ctx:
        sb = lambda name, shape, dt=F32: ctx.enter_context(nc.sbuf_tensor(name, shape, dt))
        sem = lambda name: ctx.enter_context(nc.semaphore(name))
        CR = 4
        y = sb("y", [P, CR, TOPK, H])
        ac = sb("ac5", [P, CR, H])
        si = sb("si5", [P, CR, TOPK], I32)
        s_zero = sem("p5_rows_zero")
        s_si = sem("p5_slots")
        s_y = [sem(f"p5_rows_gathered{i}") for i in range(CR)]
        s_ac = [sem(f"p5_acc_loaded{i}") for i in range(CR)]
        s_out = [sem(f"p5_out_stored{i}") for i in range(CR)]
        s_sum = sem("p5_sum_steps")
        s_carry = sem("p5_pool_carry")
        block = ctx.enter_context(nc.Block())
        o = out.rearrange("b (t p) h -> (b t) p h", p=P)

        def group(body):
            def turn(j):
                for r in range(CR):
                    body(j * CR + r, j, r)
            return turn

        @block.sync
        def _(sp):
            def tile(t, j, r):
                if not (isinstance(t, int) and t < 2):
                    sp.wait_ge(s_sum, (t - 2) * TOPK + TOPK)
                    sp.dma_start(o[t - 2], ac[:, (r - 2) % CR, :]).then_inc(s_out[(r - 2) % CR], 16)
                after(sp, s_out[r], j * 16)
                sp.dma_start(ac[:, r, :], dr["acc"][t]).then_inc(s_ac[r], 16)

            turns(sp, TT // CR, group(tile))
            for t in (TT - 2, TT - 1):
                sp.wait_ge(s_sum, t * TOPK + TOPK)
                sp.dma_start(o[t], ac[:, t % CR, :]).then_inc(s_out[t % CR], 16)
            for s in s_out:
                sp.wait_ge(s, 16 * TT // CR)

        @block.gpsimd
        def _(pool):
            pool.wait_ge(s_zero, CR)

            def tile(t, j, r):
                after(pool, s_sum, (j - 1) * CR * TOPK + (r + 1) * TOPK if not (isinstance(j, int) and j == 0) else 0)
                pool.tensor_copy(si[:, r, :], slots[:, bass.ds(t * TOPK, TOPK)]).then_inc(s_si, 1)
                pool.wait_ge(s_si, t + 1)
                pool.sem_inc(s_carry, 1)
                for k in range(TOPK):
                    pool.indirect_dma_start(y[:, r, k, :], None, dr["ob"],
                                            bass.IndirectOffsetOnAxis(ap=si[:, r, k:k + 1], axis=0),
                                            bounds_check=NE * CAP - 1, oob_is_err=False).then_inc(s_y[r], 16)

            turns(pool, TT // CR, group(tile))

        @block.vector
        def _(dve):
            for r in range(CR):
                dve.memset(y[:, r], 0.0).then_inc(s_zero, 1)

            def tile(t, j, r):
                dve.wait_ge(s_ac[r], j * 16 + 16)
                dve.wait_ge(s_y[r], j * 16 * TOPK + 16 * TOPK)
                for k in range(TOPK):
                    if k:
                        dve.wait_ge(s_sum, t * TOPK + k)
                    dve.scalar_tensor_tensor(out=ac[:, r, :], in0=y[:, r, k, :], scalar=weights[:, bass.ds(t * TOPK + k, 1)],
                                             in1=ac[:, r, :], op0=ALU.mult, op1=ALU.add).then_inc(s_sum, 1)

            turns(dve, TT // CR, group(tile))


def program(nc, io, out):
    dt = lambda name, shape, t=F32: nc.dram_tensor(name, shape, t, kind="Internal").ap()
    dr = {k: dt("scratch_" + k, s) for k, s in dict(
        a=(ET, P, NST + 1), x1=(B, L, H), u=(B * ET, P, L), dl=(B * ET, P, L), du=(B * ET, P, L), sz=(B * ET, P, L),
        bc=(B, NST, 2, L), xn=(NT, H), acc=(TT, P, H), ob=(NE * CAP, H)).items()}
    dr["tab"] = dt("scratch_tab", (NE * CAP, 1), I32)
    mamba_inputs(nc, io, dr)
    selective_scan(nc, io, dr)
    with (nc.sbuf_tensor("slots", [P, TT * TOPK], I32) as slots, nc.sbuf_tensor("weights", [P, TT * TOPK], F32) as weights):
        route_and_shared(nc, io, dr, slots, weights)
        experts(nc, io, dr)
        combine(nc, io, dr, out, slots, weights)


def kernel(x, ctx_1024, g_xattn, g_ffn, L0_xattn_in_proj_w, L0_xattn_conv_w, L0_xattn_conv_b, L0_xattn_x_proj_w,
           L0_xattn_dt_proj_w, L0_xattn_dt_proj_b, L0_xattn_A_log, L0_xattn_D, L0_ffn_gate_w, L0_ffn_gate_bias,
           L0_ffn_w1, L0_ffn_w2, L0_ffn_w3, L0_ffn_shared_gate, L0_ffn_shared_up, L0_ffn_shared_down):
    import numpy as np
    import concourse.bacc as bacc
    from concourse.bass_utils import run_bass_kernel_spmd

    per_tile = lambda v: np.ascontiguousarray(np.asarray(v).reshape(-1, P).T)
    t = lambda v: np.ascontiguousarray(np.asarray(v).T)
    arrays = dict(
        x=np.asarray(x), ctxT=np.ascontiguousarray(np.asarray(ctx_1024).transpose(0, 2, 1)),
        w_in=t(L0_xattn_in_proj_w), w_x=t(L0_xattn_x_proj_w), w_dt=t(L0_xattn_dt_proj_w),
        conv_w=np.asarray(L0_xattn_conv_w), conv_b=per_tile(L0_xattn_conv_b), dt_b=per_tile(L0_xattn_dt_proj_b),
        a_log_d=np.concatenate([np.asarray(L0_xattn_A_log), np.asarray(L0_xattn_D)[:, None]], 1), g_x=np.asarray(g_xattn), g_f=np.asarray(g_ffn),
        ident=np.eye(P, dtype=np.float32), tri=np.triu(np.ones((P, P), np.float32), 1),
        iota=np.arange(NE, dtype=np.float32), lower=np.tril(np.ones((NG, NG), np.float32), -1).reshape(-1),
        tok=(np.arange(P)[:, None] + P * np.arange(2)[None, :]).astype(np.int32), gate_w=t(L0_ffn_gate_w),
        gate_b=np.asarray(L0_ffn_gate_bias), w1=np.asarray(L0_ffn_w1), w2=np.asarray(L0_ffn_w2), w3=np.asarray(L0_ffn_w3),
        w_sg=np.asarray(L0_ffn_shared_gate), w_su=np.asarray(L0_ffn_shared_up), w_sd=np.asarray(L0_ffn_shared_down))
    nc = bacc.Bacc("TRN2", target_bir_lowering=False, num_devices=1)
    io = {k: nc.dram_tensor("in_" + k, a.shape, mybir.dt.from_np(a.dtype), kind="ExternalInput").ap()
          for k, a in arrays.items()}
    out = nc.dram_tensor("out", (B, L, H), F32, kind="ExternalOutput").ap()
    program(nc, io, out)
    r = run_bass_kernel_spmd(nc, [{"in_" + k: a for k, a in arrays.items()}], core_ids=[0])
    return r.results[0]["out"]
```

```python
from contextlib import ExitStack

import concourse.bass as bass
from concourse import mybir

P = 128
B, L, DM = 4, 1024, 512
DI, NST, DR, DC = 1024, 16, 32, 4
H, F, FS = 1024, 512, 1024
NE, TOPK, NG, TG = 32, 4, 4, 2
CAP = 2 * (2 * 512 * TOPK // NE)
NT = B * L
SCALE, EPS = 2.0, 1e-5
ET = DI // P
KD = DM // P
KH = H // P
TT = NT // P
ST = NE * CAP // P
TPE = CAP // P
HB = 512
NEWTON = 4
ROOT = 3 + 3 * NEWTON
CHOICE = 21
ROUTE = CHOICE + 5
DROPPED = 1 << 16

ALU = mybir.AluOpType
ACT = mybir.ActivationFunctionType
F32 = mybir.dt.float32
F32R = mybir.dt.float32r
I32 = mybir.dt.int32
U32 = mybir.dt.uint32
AX = mybir.AxisListType.X


def after(eng, sem, value):
    if isinstance(value, int):
        if value > 0:
            eng.wait_ge(sem, value)
    else:
        assert value.min_val > 0
        eng.wait_ge(sem, value)


def turns(eng, n, body, last=False, first=1):
    for i in range(first):
        body(i)
    with eng.Fori(first, n - last) as i:
        body(i)
    if last:
        body(n - 1)


class Semaphores(list):

    def __init__(self, nc, ctx):
        self.nc = nc
        ctx.callback(self.give_back)

    def give_back(self):
        self.nc.clear_and_free_semaphores(self)
        self.nc.all_engine_barrier()

    def __call__(self, name):
        self.append(self.nc.alloc_semaphore(name))
        return self[-1]


class Steps:

    def __init__(self, eng, sem, per):
        self.eng, self.sem, self.per, self.n, self.turn = eng, sem, per, 0, 0

    def start(self, turn):
        self.turn, self.n = turn, 0

    def resume(self, turn, n):
        self.turn, self.n = turn, n

    def end(self):
        assert self.n == self.per, (self.n, self.per)

    def then(self, ins, gate=None):
        ins.then_inc(self.sem, 1)
        self.n += 1
        self.eng.wait_ge(self.sem, self.turn * self.per + self.n)
        if gate is not None:
            self.eng.sem_inc(gate, 1)


def inverse_root(st, dve, y, var, tmp):
    st.then(dve.tensor_scalar(tmp[:, 0:1], var, EPS, None, ALU.add))
    st.then(dve.tensor_scalar(tmp[:, 1:2].bitcast(I32), tmp[:, 0:1].bitcast(I32), 1, None, ALU.arith_shift_right))
    st.then(dve.tensor_scalar(y.bitcast(I32), tmp[:, 1:2].bitcast(I32), -1.0, float(0x5F3759DF), ALU.mult, ALU.add))
    for _ in range(NEWTON):
        st.then(dve.scalar_tensor_tensor(out=tmp[:, 1:2], in0=y, scalar=y, in1=tmp[:, 0:1], op0=ALU.mult, op1=ALU.mult))
        st.then(dve.tensor_scalar(tmp[:, 1:2], tmp[:, 1:2], -0.5, 1.5, ALU.mult, ALU.add))
        st.then(dve.tensor_tensor(y, y, tmp[:, 1:2], ALU.mult))


def mamba_inputs(nc, io, dr):
    with ExitStack() as ctx:
        sb = lambda name, shape, dt=F32: ctx.enter_context(nc.sbuf_tensor(name, shape, dt))
        sem = Semaphores(nc, ctx)
        w_in = sb("w_in", [P, KD, DI])
        w_x = sb("w_x", [P, ET, DR + 2 * NST])
        w_dt = sb("w_dt", [DR, DI])
        conv_w = sb("conv_w", [P, ET, DC])
        conv_b = sb("conv_b", [P, ET])
        dt_b = sb("dt_b", [P, ET])
        a_neg = sb("a_neg", [P, ET, NST + 1])
        ctxT = sb("ctxT", [P, KD, L])
        xpad = sb("xpad", [P, 2, L + DC])
        conv = sb("conv", [P, 2, L])
        u = sb("u", [P, ET, L])
        xd = sb("xd", [DR + 2 * NST, L])
        ebuf = sb("ebuf", [P, ET, L])
        rbuf = sb("rbuf", [P, ET, L])
        lbuf = sb("lbuf", [P, 2, L])
        cbuf = sb("cbuf", [P, 2, L])
        xz = sb("xz", [P, 2, L])
        stats = sb("stats", [P, 12])
        mv = sb("mv", [P, 2])
        rstd = sb("rstd", [P, 2, 2])
        root = sb("root", [P, 2])
        psX = [ctx.enter_context(nc.psum_tensor(f"psX{i}", [P, L], F32)) for i in range(2)]
        psD = ctx.enter_context(nc.psum_tensor("psD", [DR + 2 * NST, L], F32))

        s_w = sem("p1_weights")
        s_w2 = sem("p1_weights_ctx")
        s_ctx = sem("p1_ctx_loaded")
        s_pad0 = sem("p1_padding_zero")
        s_psx = sem("p1_psum_full")
        s_pad = sem("p1_xpad_full")
        s_conv = sem("p1_conv_done")
        s_u = sem("p1_u_ready")
        s_xp = sem("p1_xproj_done")
        s_xd = sem("p1_xd_ready")
        s_xdst = sem("p1_xd_stored")
        s_exp = sem("p1_exp_done")
        s_ln = sem("p1_ln_done")
        s_cor = sem("p1_correction")
        s_lc = sem("p1_log1p")
        s_dl = sem("p1_delta")
        s_du = sem("p1_du")
        s_st = sem("p1_delta_stored")
        s_ust = sem("p1_u_stored")
        s_xz = [sem(f"p1_xz_loaded{i}") for i in range(2)]
        s_z = sem("p1_z_stats")
        s_sz = sem("p1_gate")
        s_szst = [sem(f"p1_gate_stored{i}") for i in range(2)]
        s_ch = sem("p1_dve_steps")
        s_gate = sem("p1_dve_gate")
        s_a = sem("p1_a")
        s_a2 = sem("p1_a2")
        s_ast = sem("p1_a_stored")
        block = ctx.enter_context(nc.Block())

        @block.sync
        def _(sp):
            for dst, src in ((w_x[:], io["w_x"].rearrange("(t p) k -> p t k", p=P)), (w_dt[:], io["w_dt"]),
                             (conv_w[:], io["conv_w"].rearrange("(t p) k -> p t k", p=P)),
                             (conv_b[:], io["conv_b"]), (dt_b[:], io["dt_b"]),
                             (a_neg[:], io["a_log_d"].rearrange("(t p) k -> p t k", p=P))):
                sp.dma_start(dst, src).then_inc(s_w, 16)
            sp.dma_start(w_in[:], io["w_in"].rearrange("(k p) e -> p k e", p=P)).then_inc(s_w2, 16)
            sp.wait_ge(s_a2, 1)
            sp.dma_start(dr["a"].rearrange("t p n -> p t n"), a_neg[:]).then_inc(s_ast, 16)
            def batch(b):
                after(sp, s_psx, b * 2 * ET)
                sp.dma_start(ctxT[:], io["ctxT"][b].rearrange("(k p) l -> p k l", p=P)).then_inc(s_ctx, 16)
                for et in range(ET):
                    after(sp, s_szst[et % 2], (b * (ET // 2) + et // 2) * 16)
                    sp.dma_start(xz[:, et % 2, :], io["x"][b, et * P:(et + 1) * P, :]).then_inc(s_xz[et % 2], 16)
                    if et >= 1:
                        after(sp, s_u, b * ET + et)
                        sp.dma_start(dr["u"][b * ET + et - 1], u[:, et - 1, :]).then_inc(s_ust, 16)
                        after(sp, s_sz, b * ET + et)
                        sp.dma_start(dr["sz"][b * ET + et - 1], xz[:, (et - 1) % 2, :]).then_inc(s_szst[(et - 1) % 2], 16)
                after(sp, s_u, b * ET + ET)
                sp.dma_start(dr["u"][b * ET + ET - 1], u[:, ET - 1, :]).then_inc(s_ust, 16)
                after(sp, s_sz, b * ET + ET)
                sp.dma_start(dr["sz"][b * ET + ET - 1], xz[:, (ET - 1) % 2, :]).then_inc(s_szst[(ET - 1) % 2], 16)
                after(sp, s_xd, b + 1)
                for c in range(2):
                    sp.dma_start(dr["bc"][b, :, c, :], xd[DR + c * NST:DR + (c + 1) * NST, :]).then_inc(s_xdst, 16)
                for et in range(ET):
                    after(sp, s_dl, b * ET + et + 1)
                    sp.dma_start(dr["dl"][b * ET + et], rbuf[:, et, :]).then_inc(s_st, 16)
                    after(sp, s_du, b * ET + et + 1)
                    sp.dma_start(dr["du"][b * ET + et], ebuf[:, et, :]).then_inc(s_st, 16)
            turns(sp, B, batch)
            sp.wait_ge(s_ast, 16)
            sp.wait_ge(s_ust, 16 * B * ET)
            sp.wait_ge(s_xdst, 32 * B)
            sp.wait_ge(s_st, 16 * 2 * B * ET)
            for s in s_szst:
                sp.wait_ge(s, 16 * B * ET // 2)

        @block.tensor
        def _(pe):
            pe.wait_ge(s_w, 16 * 6)
            pe.wait_ge(s_w2, 16)

            def x_proj(b, et):
                after(pe, s_u, b * ET + et + 1)
                if et == 0:
                    after(pe, s_xd, b)
                for hb in range(2):
                    mm = pe.matmul(psD[:, hb * HB:(hb + 1) * HB], w_x[:, et, :], u[:, et, hb * HB:(hb + 1) * HB],
                                   start=(et == 0), stop=(et == ET - 1))
                mm.then_inc(s_xp, 1)

            def batch(b):
                after(pe, s_ctx, b * 16 + 16)
                for et in range(ET):
                    if et < 2:
                        after(pe, s_exp, b * 2 * ET)
                    else:
                        after(pe, s_pad, b * ET + et - 1)
                    for hb in range(2):
                        for k in range(KD):
                            mm = pe.matmul(psX[et % 2][:, hb * HB:(hb + 1) * HB], w_in[:, k, et * P:(et + 1) * P],
                                           ctxT[:, k, hb * HB:(hb + 1) * HB], start=(k == 0), stop=(k == KD - 1))
                    mm.then_inc(s_psx, 1)
                    if et >= 2:
                        x_proj(b, et - 2)
                x_proj(b, ET - 2)
                x_proj(b, ET - 1)
                after(pe, s_xd, b + 1)
                for et in range(ET):
                    if et < 2:
                        after(pe, s_pad, b * ET + ET)
                    else:
                        after(pe, s_exp, b * 2 * ET + 2 * (et - 2) + 1)
                    for hb in range(2):
                        mm = pe.matmul(psX[et % 2][:, hb * HB:(hb + 1) * HB], w_dt[:, et * P:(et + 1) * P],
                                       xd[0:DR, hb * HB:(hb + 1) * HB], start=True, stop=True)
                    mm.then_inc(s_psx, 1)

            turns(pe, B, batch)

        @block.scalar
        def _(act):
            act.wait_ge(s_w, 16 * 6)
            act.activation(a_neg[:, :, 0:NST], a_neg[:, :, 0:NST], ACT.Exp).then_inc(s_a, 1)
            act.wait_ge(s_pad0, 1)

            def u_silu(b, et):
                after(act, s_conv, b * ET + et + 1)
                if et == 0:
                    after(act, s_ust, b * ET * 16)
                    after(act, s_du, b * ET)
                act.activation(u[:, et, :], conv[:, et % 2, :], ACT.Silu).then_inc(s_u, 1)

            def z_silu(b, et):
                after(act, s_z, b * ET + et + 1)
                act.activation(xz[:, et % 2, :], xz[:, et % 2, :], ACT.Silu, bias=rstd[:, et % 2, 1:2],
                               scale=rstd[:, et % 2, 0:1]).then_inc(s_sz, 1)

            def batch(b):
                for et in range(ET):
                    after(act, s_psx, b * 2 * ET + et + 1)
                    if et < 2:
                        after(act, s_conv, b * ET)
                    else:
                        after(act, s_conv, b * ET + et - 1)
                    act.activation(xpad[:, et % 2, DC - 1:DC - 1 + L], psX[et % 2][:, :],
                                   ACT.Copy).then_inc(s_pad, 1)
                    if et >= 1:
                        u_silu(b, et - 1)
                        z_silu(b, et - 1)
                u_silu(b, ET - 1)
                z_silu(b, ET - 1)
                after(act, s_xp, b * ET + ET)
                after(act, s_xdst, b * 32)
                act.activation(xd[:, :], psD[:, :], ACT.Copy).then_inc(s_xd, 1)
                after(act, s_st, b * 2 * ET * 16)
                for et in range(ET):
                    after(act, s_psx, b * 2 * ET + ET + et + 1)
                    act.activation(rbuf[:, et, :], psX[et % 2][:, :], ACT.Relu, bias=dt_b[:, et:et + 1])
                    act.activation(ebuf[:, et, :], psX[et % 2][:, :], ACT.Abs,
                                   bias=dt_b[:, et:et + 1]).then_inc(s_exp, 1)
                    after(act, s_exp, b * 2 * ET + 2 * et + 1)
                    act.activation(ebuf[:, et, :], ebuf[:, et, :], ACT.Exp, scale=-1.0).then_inc(s_exp, 1)
                after(act, s_exp, b * 2 * ET + 2 * ET)
                for et in range(ET):
                    if et < 2:
                        after(act, s_dl, b * ET)
                    else:
                        after(act, s_dl, b * ET + et - 1)
                    act.activation(lbuf[:, et % 2, :], ebuf[:, et, :], ACT.Ln, bias=1.0).then_inc(s_ln, 1)

            turns(act, B, batch)

        @block.vector
        def _(dve):
            dve.memset(xpad[:, :, 0:DC - 1], 0.0).then_inc(s_pad0, 1)
            dve.wait_ge(s_a, 1)
            dve.tensor_scalar(a_neg[:, :, 0:NST], a_neg[:, :, 0:NST], -1.0, None, ALU.mult).then_inc(s_a2, 1)
            st = Steps(dve, s_ch, ET * (6 + ROOT))
            def batch(b):
                st.start(b)
                for et in range(ET):
                    after(dve, s_xz[et % 2], (b * (ET // 2) + et // 2) * 16 + 16)
                    dve.bn_stats(stats[:, 0:6], xz[:, et % 2, 0:HB])
                    st.then(dve.bn_stats(stats[:, 6:12], xz[:, et % 2, HB:L]), s_gate)
                    st.then(dve.bn_aggr(mv[:, :], stats[:, :]))
                    if et < 2:
                        after(dve, s_sz, b * ET)
                    else:
                        after(dve, s_sz, b * ET + et - 1)
                    inverse_root(st, dve, rstd[:, et % 2, 0:1], mv[:, 1:2], root)
                    dve.scalar_tensor_tensor(out=rstd[:, et % 2, 1:2], in0=mv[:, 0:1], scalar=-1.0,
                                             in1=rstd[:, et % 2, 0:1], op0=ALU.mult, op1=ALU.mult).then_inc(s_z, 1)
                    after(dve, s_pad, b * ET + et + 1)
                    if et < 2:
                        after(dve, s_u, b * ET)
                    else:
                        after(dve, s_u, b * ET + et - 1)
                    c = conv[:, et % 2, :]
                    st.then(dve.tensor_scalar(c, xpad[:, et % 2, 0:L], conv_w[:, et, 0:1], conv_b[:, et:et + 1],
                                              ALU.mult, ALU.add))
                    for k in range(1, DC - 1):
                        st.then(dve.scalar_tensor_tensor(out=c, in0=xpad[:, et % 2, k:k + L], scalar=conv_w[:, et, k:k + 1],
                                                         in1=c, op0=ALU.mult, op1=ALU.add))
                    dve.scalar_tensor_tensor(out=c, in0=xpad[:, et % 2, DC - 1:DC - 1 + L],
                                             scalar=conv_w[:, et, DC - 1:DC], in1=c, op0=ALU.mult,
                                             op1=ALU.add).then_inc(s_conv, 1)
                for et in range(ET):
                    after(dve, s_exp, b * 2 * ET + 2 * et + 2)
                    if et < 2:
                        after(dve, s_lc, b * ET)
                    else:
                        after(dve, s_lc, b * ET + et - 1)
                    c = cbuf[:, et % 2, :]
                    st.then(dve.tensor_scalar(c, ebuf[:, et, :], 1.0, 1.0, ALU.add, ALU.subtract))
                    dve.tensor_tensor(c, ebuf[:, et, :], c, ALU.subtract).then_inc(s_cor, 1)
                    if et >= 2:
                        after(dve, s_dl, b * ET + et - 1)
                        dve.tensor_tensor(ebuf[:, et - 2, :], rbuf[:, et - 2, :], u[:, et - 2, :],
                                          ALU.mult).then_inc(s_du, 1)
                for et in (ET - 2, ET - 1):
                    after(dve, s_dl, b * ET + et + 1)
                    dve.tensor_tensor(ebuf[:, et, :], rbuf[:, et, :], u[:, et, :], ALU.mult).then_inc(s_du, 1)
                st.end()

            turns(dve, B, batch)

        @block.gpsimd
        def _(pool):
            def batch(b):
                for et in range(ET):
                    after(pool, s_ln, b * ET + et + 1)
                    after(pool, s_cor, b * ET + et + 1)
                    pool.tensor_tensor(lbuf[:, et % 2, :], lbuf[:, et % 2, :], cbuf[:, et % 2, :], ALU.add).then_inc(s_lc, 1)
                    after(pool, s_lc, b * ET + et + 1)
                    pool.tensor_tensor(rbuf[:, et, :], rbuf[:, et, :], lbuf[:, et % 2, :], ALU.add).then_inc(s_dl, 1)

            turns(pool, B, batch)


def selective_scan(nc, io, dr):
    with ExitStack() as ctx:
        sb = lambda name, shape, dt=F32: ctx.enter_context(nc.sbuf_tensor(name, shape, dt))
        sem = Semaphores(nc, ctx)
        NU = B * ET
        HR = 4
        ident = sb("ident2", [P, P])
        gate = sb("gate2", [P, 1])
        bc = sb("bc", [P, NST, 2, L])
        ad = sb("ad", [P, 2, NST + 1])
        dl = sb("dl", [P, 2, L])
        du = sb("du", [P, 2, L])
        ut = sb("ut", [P, 2, L])
        sz = sb("szt", [P, 2, L])
        xl = sb("xl", [P, 2, L])
        dbu = sb("dbu", [P, 2, L])
        h = sb("h", [P, HR, L])
        hc = sb("hc", [P, 2, L])
        yt = sb("yt", [P, L])
        da = [ctx.enter_context(nc.psum_tensor(f"da{i}", [P, L], F32)) for i in range(2)]
        psy = ctx.enter_context(nc.psum_tensor("psy", [P, L], F32))
        pst = ctx.enter_context(nc.psum_tensor("pst", [P, ET, P], F32))

        s_c = sem("p2_constants")
        s_gate = sem("p2_gate")
        s_bc = [sem(f"p2_bc_loaded{n}") for n in range(NST)]
        s_ld = [sem(f"p2_unit_loaded{i}") for i in range(2)]
        s_ul = [sem(f"p2_u_gate_loaded{i}") for i in range(2)]
        s_xl = [sem(f"p2_x_loaded{i}") for i in range(2)]
        s_xst = [sem(f"p2_x1_stored{i}") for i in range(2)]
        s_da = sem("p2_decay")
        s_dbu = sem("p2_input")
        s_scan = sem("p2_state")
        s_hc = sem("p2_state_times_c")
        s_ys = sem("p2_summed")
        s_t1 = sem("p2_skip_added")
        s_t2 = sem("p2_gated")
        s_tr = sem("p2_transposed")
        s_add = sem("p2_x1")
        block = ctx.enter_context(nc.Block())

        @block.sync
        def _(sp):
            def load(i, par):
                sp.dma_start(dl[:, par, :], dr["dl"][i]).then_inc(s_ld[par], 16)
                sp.dma_start(du[:, par, :], dr["du"][i]).then_inc(s_ld[par], 16)
                sp.dma_start(ad[:, par, :], dr["a"][i % ET]).then_inc(s_ld[par], 16)
                sp.dma_start(ut[:, par, :], dr["u"][i]).then_inc(s_ul[par], 16)
                sp.dma_start(sz[:, par, :], dr["sz"][i]).then_inc(s_ul[par], 16)

            def store(i, b, et):
                sp.dma_start(dr["x1"][b].rearrange("(t p) (e c) -> e p t c", p=P, c=P)[et],
                             xl[:, et % 2, :].rearrange("p (t c) -> p t c", c=P)).then_inc(s_xst[et % 2], 16)

            sp.dma_start(ident[:], io["ident"]).then_inc(s_c, 16)
            sp.dma_start(gate[:], io["g_x"].partition_broadcast(P)).then_inc(s_c, 16)
            load(0, 0)
            for n in range(NST):
                sp.dma_start(bc[:, n], dr["bc"][0, n].partition_broadcast(P)).then_inc(s_bc[n], 16)

            def batch(b):
                for et in range(ET):
                    i = b * ET + et
                    first = isinstance(b, int) and i == 0
                    final = isinstance(b, int) and i == NU - 1
                    after(sp, s_add, i if not first else 0)
                    if not first:
                        store(i - 1, b if et else b - 1, (et - 1) % ET)
                    if not final:
                        load(i + 1, (et + 1) % 2)
                    after(sp, s_xst[et % 2], (b * (ET // 2) + et // 2) * 16)
                    sp.dma_start(xl[:, et % 2, :].rearrange("p (t c) -> p t c", c=P),
                                 io["x"][b].rearrange("(t p) (e c) -> e p t c", p=P, c=P)[et]).then_inc(s_xl[et % 2], 16)
                if not (isinstance(b, int) and b == B - 1):
                    for n in range(NST):
                        sp.wait_ge(s_hc, b * ET * NST + (ET - 1) * NST + n + 1)
                        sp.dma_start(bc[:, n], dr["bc"][b + 1, n].partition_broadcast(P)).then_inc(s_bc[n], 16)

            turns(sp, B, batch, last=True)
            sp.wait_ge(s_add, NU)
            store(NU - 1, B - 1, ET - 1)
            for s in s_xst:
                sp.wait_ge(s, 16 * NU // 2)

        @block.scalar
        def _(act):
            act.wait_ge(s_c, 32)
            act.activation(gate[:], gate[:], ACT.Tanh).then_inc(s_gate, 1)

            def pair(j):
                for par in range(2):
                    i = j * 2 + par
                    act.wait_ge(s_ld[par], j * 48 + 48)
                    for n in range(NST):
                        after(act, s_scan, i * NST + n - 1)
                        act.activation(da[n % 2][:, :], dl[:, par, :], ACT.Exp, scale=ad[:, par, n:n + 1]).then_inc(s_da, 1)

            turns(act, NU // 2, pair)

        @block.gpsimd
        def _(pool):
            def pair(j):
                for par in range(2):
                    i = j * 2 + par
                    pool.wait_ge(s_ld[par], j * 48 + 48)
                    for n in range(NST):
                        pool.wait_ge(s_bc[n], (j // (ET // 2)) * 16 + 16)
                        after(pool, s_scan, i * NST + n - 1)
                        pool.tensor_tensor(dbu[:, n % 2, :], du[:, par, :], bc[:, n, 0, :], ALU.mult).then_inc(s_dbu, 1)

            turns(pool, NU // 2, pair)

        @block.vector
        def _(dve):
            def times_c(i, n):
                dve.wait_ge(s_scan, i * NST + n + 1)
                after(dve, s_ys, i * NST + n - 1)
                dve.tensor_tensor(hc[:, n % 2, :], h[:, n % HR, :], bc[:, n, 1, :], ALU.mult).then_inc(s_hc, 1)

            def skip_and_gate(i, j, par):
                dve.wait_ge(s_ul[par], j * 32 + 32)
                dve.wait_ge(s_ys, i * NST + NST)
                after(dve, s_tr, i)
                dve.scalar_tensor_tensor(out=yt[:, :], in0=ut[:, par, :], scalar=ad[:, par, NST:NST + 1],
                                         in1=psy[:, :], op0=ALU.mult, op1=ALU.add).then_inc(s_t1, 1)
                dve.wait_ge(s_t1, i + 1)
                dve.scalar_tensor_tensor(out=yt[:, :], in0=yt[:, :], scalar=gate[:, 0:1], in1=sz[:, par, :],
                                         op0=ALU.mult, op1=ALU.mult).then_inc(s_t2, 1)

            def residual(i, j, par):
                dve.wait_ge(s_xl[par], j * 16 + 16)
                dve.wait_ge(s_tr, i + 1)
                dve.tensor_tensor(xl[:, par, :], xl[:, par, :], pst[:, :, :].rearrange("p t c -> p (t c)"),
                                  ALU.add).then_inc(s_add, 1)

            def pair(j):
                for par in range(2):
                    i = j * 2 + par
                    first = isinstance(j, int) and i == 0
                    for n in range(NST):
                        dve.wait_ge(s_da, i * NST + n + 1)
                        dve.wait_ge(s_dbu, i * NST + n + 1)
                        after(dve, s_hc, i * NST + n - HR + 1)
                        dve.tensor_tensor_scan(h[:, n % HR, :], da[n % 2][:, :], dbu[:, n % 2, :], 0.0, ALU.mult,
                                               ALU.add).then_inc(s_scan, 1)
                        if n:
                            times_c(i, n - 1)
                        elif not first:
                            times_c(i - 1, NST - 1)
                        if n == 2 and not first:
                            skip_and_gate(i - 1, j - (par == 0), 1 - par)
                        if n == 5 and not first:
                            residual(i - 1, j - (par == 0), 1 - par)

            dve.wait_ge(s_gate, 1)
            turns(dve, NU // 2, pair)
            times_c(NU - 1, NST - 1)
            skip_and_gate(NU - 1, NU // 2 - 1, 1)
            residual(NU - 1, NU // 2 - 1, 1)

        @block.tensor
        def _(pe):
            pe.wait_ge(s_c, 32)

            def spread(i):
                pe.wait_ge(s_t2, i + 1)
                after(pe, s_add, i)
                for t in range(L // P):
                    mm = pe.transpose(pst[:, t, :], yt[:, t * P:(t + 1) * P], ident[:])
                mm.then_inc(s_tr, 1)

            def pair(j):
                for par in range(2):
                    i = j * 2 + par
                    first = isinstance(j, int) and i == 0
                    for n in range(NST):
                        if n == 0:
                            after(pe, s_t1, i)
                        pe.wait_ge(s_hc, i * NST + n + 1)
                        for hb in range(2):
                            mm = pe.matmul(psy[:, hb * HB:(hb + 1) * HB], ident[:], hc[:, n % 2, hb * HB:(hb + 1) * HB],
                                           start=(n == 0), stop=(n == NST - 1))
                        mm.then_inc(s_ys, 1)
                        if n == 1 and not first:
                            spread(i - 1)

            turns(pe, NU // 2, pair)
            spread(NU - 1)


def shared_pass(nc, io, dr, part, slots, weights, out=None):
    route = part == 0
    with ExitStack() as ctx:
        nm = lambda name: f"{name}_s{part}"
        sb = lambda name, shape, dt=F32: ctx.enter_context(nc.sbuf_tensor(nm(name), shape, dt))
        ps = lambda name, shape: ctx.enter_context(nc.psum_tensor(nm(name), shape, F32))
        named = Semaphores(nc, ctx)
        sem = lambda name: named(nm(name))
        EG = NE // NG
        KF = HB // P
        WN = KH * HB
        raw = sb("raw", [P, 2, WN])
        wsp = sb("wsp", [P, 3, 2, WN], F32R)
        ident = sb("ident", [P, P])
        gate = sb("gate", [P, 1])
        xt = sb("xt", [P, 2, H])
        xn = sb("xn", [P, 2, H]) if route else xt
        xT = sb("xT", [P, 2, 2, KH, P], F32R)
        sg = sb("sg", [P, HB])
        hT = sb("hT", [P, 2, KF, P], F32R)
        ac = sb("ac", [P, 2, H])
        psG, psU = ps("psG", [P, HB]), ps("psU", [P, HB])
        psO, psX, psH = ps("psO", [P, H]), ps("psXT", [P, 2, 4, P]), ps("psH", [P, KF, P])
        if route:
            psR = ps("psR", [P, HB])
            tri = sb("tri", [P, P])
            ones = sb("ones", [P, P])
            iota = sb("iota", [P, NE])
            lower = sb("lower", [P, NG, NG])
            bias = sb("bias", [P, NE])
            gw = sb("gw", [P, KH, NE])
            xTf = sb("xTf", [P, 2, KH, P])
            gate2 = sb("gate_scaled", [P, 1])
            tok = sb("tok", [P, 2], I32)
            step = sb("token_step", [P, 1], I32)
            zero = sb("zero_table", [P, NE * CAP // P], I32)
            stats, mv, root, rstd = sb("stats", [P, 12]), sb("mv", [P, 2]), sb("root", [P, 2]), sb("rstd", [P, 1])
            th, scores, sc = sb("th", [P, NE]), sb("scores", [P, NE]), sb("sc", [P, NG, EG])
            gm, gs = sb("gm", [P, NG, 8]), sb("gs", [P, NG])
            gt, eq, rank = sb("gt", [P, NG, NG]), sb("eq", [P, NG, NG]), sb("rank", [P, NG])
            m8, i8, idx = sb("m8", [P, 8]), sb("i8", [P, 8], U32), sb("idx", [P, TOPK])
            oh, ow = sb("oh", [P, TOPK, NE]), sb("ow", [P, TOPK, NE])
            mask, run = sb("mask", [P, NE]), sb("run", [P, NE])
            w4, ws = sb("w4", [P, TOPK]), sb("ws", [P, 2])
            pos, over, sf = sb("pos", [P, TOPK]), sb("over", [P, TOPK]), sb("sf", [P, TOPK])
            si = sb("si", [P, 2, TOPK], I32)
        else:
            x1t = sb("x1t", [P, 2, H])
            y = raw[:].rearrange("p r (k h) -> p r k h", h=H)
            si = sb("si", [P, 2, TOPK], I32)

        SUMS = TOPK + 1
        NC = 8 if route else 2
        s_c = sem("constants")
        s_raw = [sem(f"matrix_loaded{i}") for i in range(2)]
        s_whi, s_wlo = sem("matrix_heads"), sem("matrix_rests")
        s_tanh = sem("gate_tanh")
        s_x = [sem(f"x_loaded{i}") for i in range(2)]
        s_acl = [sem(f"acc_loaded{i}") for i in range(2)]
        s_xnst = [sem(f"xn_stored{i}") for i in range(2)]
        s_acst = [sem(f"acc_stored{i}") for i in range(2)]
        s_xn, s_xtr, s_xhi, s_xlo = sem("xn"), sem("x_transposed"), sem("x_heads"), sem("x_rests")
        s_g, s_u, s_sg, s_h = sem("gate_product"), sem("up_product"), sem("silu"), sem("hidden")
        s_htr, s_hhi, s_hlo = sem("hidden_transposed"), sem("hidden_heads"), sem("hidden_rests")
        s_d = sem("down_product")
        if route:
            s_ac = sem("acc")
        if route:
            s_init, s_tab = sem("initialised"), sem("table_zero")
            s_sct = [sem(f"tokens_scattered{i}") for i in range(2)]
            s_tok, s_ch, s_ln, s_fence = sem("token_ids"), sem("dve_steps"), sem("norm_steps"), sem("dve_gate")
            s_lg, s_th, s_mask, s_pos, s_posr = sem("logits"), sem("logits_tanh"), sem("mask"), sem("positions"), sem("pos_read")
            s_run = sem("queue_lengths")
            s_slot, s_carry = sem("slots"), sem("pool_carry")
        else:
            s_zero, s_si, s_carry = sem("rows_zero"), sem("gather_slots"), sem("pool_carry")
            s_y = [sem(f"rows_gathered{i}") for i in range(2)]
            s_half, s_sum = sem("half_added"), sem("sum_steps")
        block = ctx.enter_context(nc.Block())
        x1 = dr["x1"].rearrange("b (t p) h -> (b t) p h", p=P)
        if out is not None:
            o = out.rearrange("b (t p) h -> (b t) p h", p=P)
        xnd = dr["xn"].rearrange("(t p) h -> t p h", p=P)

        def split(j, par):
            t = j * 2 + par
            i = isinstance(t, int)
            return t, i and t == 0, i and t < 2, i and t == TT - 1

        @block.sync
        def _(sp):
            consts = [(ident[:], io["ident"]), (gate[:], io["g_f"].partition_broadcast(P))]
            if route:
                consts += [(tri[:], io["tri"]), (iota[:], io["iota"].partition_broadcast(P)),
                           (lower[:].rearrange("p a b -> p (a b)"), io["lower"].partition_broadcast(P)),
                           (bias[:], io["gate_b"].partition_broadcast(P)), (tok[:], io["tok"]),
                           (gw[:], io["gate_w"].rearrange("(k p) e -> p k e", p=P))]
            for dst, src in consts:
                sp.dma_start(dst, src).then_inc(s_c, 16)

            def load(t, par):
                sp.dma_start(xt[:, par, :], x1[t] if route else xnd[t]).then_inc(s_x[par], 16)

            def store(t, par):
                sp.wait_ge(*((s_ac, t + 1) if route else (s_sum, t * SUMS + SUMS)))
                sp.dma_start(dr["acc"][t] if route else o[t], ac[:, par, :]).then_inc(s_acst[par], 16)

            load(0, 0)
            cols = slice(part * HB, (part + 1) * HB)
            for m, src in enumerate((io["w_sg"][:, cols], io["w_su"][:, cols], io["w_sd"][cols, :])):
                if m == 2:
                    sp.wait_ge(s_wlo, 1)
                sp.dma_start(raw[:, m % 2, :].rearrange("p (k f) -> p k f", k=KF if m == 2 else KH),
                             src.rearrange("(k p) f -> p k f", p=P)).then_inc(s_raw[m % 2], 16)
            if route:
                sp.wait_ge(s_init, 1)
                sp.dma_start(dr["tab"].rearrange("(p s) o -> p (s o)", p=P), zero[:]).then_inc(s_tab, 16)

            def pair(j):
                for par in range(2):
                    t, first, early, last = split(j, par)
                    if not last:
                        after(sp, s_xn if route else s_xtr, t)
                        load(t + 1, 1 - par)
                    if route:
                        sp.wait_ge(s_xn, t + 1)
                        sp.dma_start(xnd[t], xn[:, par, :]).then_inc(s_xnst[par], 16)
                    if not early:
                        store(t - 2, par)
                    if not route:
                        after(sp, s_acst[par], j * 16)
                        sp.dma_start(ac[:, par, :], dr["acc"][t]).then_inc(s_acl[par], 16)
                        sp.dma_start(x1t[:, par, :], x1[t]).then_inc(s_acl[par], 16)

            turns(sp, TT // 2, pair, last=True)
            store(TT - 2, 0)
            store(TT - 1, 1)
            for s in (*(s_xnst if route else ()), *s_acst):
                sp.wait_ge(s, 16 * TT // 2)

        if route:
            @block.gpsimd
            def _(pool):
                pool.memset(ones[:], 1.0)
                pool.memset(run[:], 0.0)
                pool.memset(step[:], 2 * P)
                pool.memset(zero[:], 0).then_inc(s_init, 1)
                pool.wait_ge(s_tab, 16)
                pool.wait_ge(s_c, 16 * NC)

                def pair(j):
                    for par in range(2):
                        t, first, early, last = split(j, par)
                        if not (isinstance(j, int) and j == 0):
                            pool.wait_ge(s_sct[par], j * 16 * TOPK)
                            pool.tensor_tensor(tok[:, par:par + 1], tok[:, par:par + 1], step[:], ALU.add).then_inc(s_tok, 1)
                            pool.wait_ge(s_tok, t - 1)
                        pool.wait_ge(s_slot, t + 1)
                        pool.sem_inc(s_carry, 1)
                        for k in range(TOPK):
                            pool.indirect_dma_start(dr["tab"], bass.IndirectOffsetOnAxis(ap=si[:, par, k:k + 1], axis=0),
                                                    tok[:, par:par + 1], None, bounds_check=NE * CAP - 1,
                                                    oob_is_err=False).then_inc(s_sct[par], 16)

                turns(pool, TT // 2, pair)
                for s in s_sct:
                    pool.wait_ge(s, 16 * TOPK * TT // 2)

        else:
            @block.gpsimd
            def _(pool):
                pool.wait_ge(s_zero, 1)

                def pair(j):
                    for par in range(2):
                        t = j * 2 + par
                        after(pool, s_sum, (t - 2) * SUMS + TOPK if not isinstance(t, int) or t >= 2 else 0)
                        pool.tensor_copy(si[:, par, :], slots[:, bass.ds(t * TOPK, TOPK)]).then_inc(s_si, 1)
                        pool.wait_ge(s_si, t + 1)
                        pool.sem_inc(s_carry, 1)
                        for k in range(TOPK):
                            pool.indirect_dma_start(y[:, par, k, :], None, dr["ob"],
                                                    bass.IndirectOffsetOnAxis(ap=si[:, par, k:k + 1], axis=0),
                                                    bounds_check=NE * CAP - 1, oob_is_err=False).then_inc(s_y[par], 16)

                turns(pool, TT // 2, pair)

        @block.tensor
        def _(pe):
            pe.wait_ge(s_c, 16 * NC)
            if route:
                pe.wait_ge(s_init, 1)

            def x_transpose(t, par, j):
                if route:
                    pe.wait_ge(s_xn, t + 1)
                else:
                    pe.wait_ge(s_x[par], j * 16 + 16)
                after(pe, s_xlo, 2 * t)
                for k in range(KH):
                    mm = pe.transpose(psX[:, k // 4, k % 4, :], xn[:, par, k * P:(k + 1) * P], ident[:])
                mm.then_inc(s_xtr, 1)

            def product(dst, lhs, rhs, done):
                for n, (l, r) in enumerate(zip(lhs, rhs)):
                    pe.matmul(dst, l[0], r[0], start=(n == 0), stop=False)
                    pe.matmul(dst, l[0], r[1], start=False, stop=False)
                    mm = pe.matmul(dst, l[1], r[0], start=False, stop=(n == len(lhs) - 1))
                if done is not None:
                    mm.then_inc(done, 1)

            def up(dst, m, par, done):
                product(dst[:], [[xT[:, par, c, k, :] for c in range(2)] for k in range(KH)],
                        [[wsp[:, m, c, k * HB:(k + 1) * HB] for c in range(2)] for k in range(KH)], done)

            def down(t):
                pe.wait_ge(s_hlo, t + 1)
                after(pe, s_ac if route else s_half, t)
                for hb in range(H // HB):
                    product(psO[:, hb * HB:(hb + 1) * HB], [[hT[:, c, k, :] for c in range(2)] for k in range(KF)],
                            [[wsp[:, 2, c, k * H + hb * HB:k * H + (hb + 1) * HB] for c in range(2)] for k in range(KF)],
                            s_d if hb else None)

            def pair(j):
                for par in range(2):
                    t, first, early, last = split(j, par)
                    pe.wait_ge(s_xlo, 2 * t + 2)
                    if first:
                        pe.wait_ge(s_wlo, 1)
                    after(pe, s_sg, t)
                    up(psG, 0, par, s_g)
                    if route:
                        after(pe, s_posr, t)
                        for k in range(KH):
                            mm = pe.matmul(psR[:, 0:NE], xTf[:, par, k, :], gw[:, k, :], start=(k == 0), stop=(k == KH - 1))
                        mm.then_inc(s_lg, 1)
                    if first:
                        pe.wait_ge(s_wlo, 2)
                    else:
                        h_transpose(t - 1)
                    after(pe, s_h, t)
                    up(psU, 1, par, s_u)
                    if not last:
                        x_transpose(t + 1, 1 - par, j + par)
                    if first:
                        pe.wait_ge(s_wlo, 3)
                    else:
                        down(t - 1)
                    if route:
                        pe.wait_ge(s_mask, t + 1)
                        if not first:
                            pe.wait_ge(s_run, t)
                        pe.matmul(psR[:, NE:2 * NE], tri[:], mask[:], start=True, stop=False)
                        pe.matmul(psR[:, NE:2 * NE], ones[:], run[:], start=False, stop=True).then_inc(s_pos, 1)

            def h_transpose(t):
                pe.wait_ge(s_h, t + 1)
                after(pe, s_hlo, t)
                for k in range(KF):
                    mm = pe.transpose(psH[:, k, :], sg[:, k * P:(k + 1) * P], ident[:])
                mm.then_inc(s_htr, 1)

            x_transpose(0, 0, 0)
            turns(pe, TT // 2, pair, last=True)
            h_transpose(TT - 1)
            down(TT - 1)

        @block.scalar
        def _(act):
            act.wait_ge(s_c, 16 * NC)
            act.activation(gate[:], gate[:], ACT.Tanh).then_inc(s_tanh, 1)

            def x_head(t, par):
                act.wait_ge(s_xtr, t + 1)
                after(act, s_u, t - 1)
                for hb in range(2):
                    ks = slice(4 * hb, 4 * hb + 4)
                    act.activation(xT[:, par, 0, ks, :], psX[:, hb], ACT.Copy).then_inc(s_xhi, 1)
                    if route:
                        act.activation(xTf[:, par, ks, :], psX[:, hb], ACT.Copy).then_inc(s_xhi, 1)

            def pair(j):
                for par in range(2):
                    t, first, early, last = split(j, par)
                    if route and not early:
                        scaled_out(t - 2, j - 1, par)
                    if route:
                        act.wait_ge(s_lg, t + 1)
                        if not first:
                            act.wait_ge(s_ch, (t - 1) * ROUTE + 1)
                        act.activation(th[:], psR[:, 0:NE], ACT.Tanh, scale=0.5).then_inc(s_th, 1)
                    if not first:
                        h_head(t - 1)
                    act.wait_ge(s_g, t + 1)
                    after(act, s_htr, t)
                    act.activation(sg[:], psG[:], ACT.Silu).then_inc(s_sg, 1)
                    if not last:
                        x_head(t + 1, 1 - par)

            def h_head(t):
                act.wait_ge(s_htr, t + 1)
                after(act, s_d, t)
                act.activation(hT[:, 0], psH[:], ACT.Copy).then_inc(s_hhi, 1)

            def scaled_out(t, j, par):
                act.wait_ge(s_d, t + 1)
                after(act, s_acst[par], j * 16)
                act.activation(ac[:, par, :], psO[:], ACT.Copy, scale=gate[:, 0:1]).then_inc(s_ac, 1)

            x_head(0, 0)
            for m in range(3):
                act.wait_ge(s_raw[m % 2], 16 * (m // 2 + 1))
                act.activation(wsp[:, m, 0, :], raw[:, m % 2, :], ACT.Copy).then_inc(s_whi, 1)
            act.wait_ge(s_tanh, 1)
            turns(act, TT // 2, pair, last=True, first=2)
            if route:
                scaled_out(TT - 2, TT // 2 - 1, 0)
            h_head(TT - 1)
            if route:
                scaled_out(TT - 1, TT // 2 - 1, 1)

        @block.vector
        def _(dve):
            f32 = lambda ap: ap.bitcast(F32)
            XH = 4 if route else 2

            def x_rest(t, par):
                for hb in range(2):
                    ks = slice(4 * hb, 4 * hb + 4)
                    dve.wait_ge(s_xhi, XH * t + XH // 2 * (hb + 1))
                    dve.tensor_tensor(xT[:, par, 1, ks, :], psX[:, hb], f32(xT[:, par, 0, ks, :]), ALU.subtract)\
                        .then_inc(s_xlo, 1)

            def h_rest(t):
                dve.wait_ge(s_hhi, t + 1)
                dve.tensor_tensor(hT[:, 1], psH[:], f32(hT[:, 0]), ALU.subtract).then_inc(s_hlo, 1)

            def multiply(t):
                dve.wait_ge(s_sg, t + 1)
                dve.wait_ge(s_u, t + 1)
                dve.tensor_tensor(sg[:], sg[:], psU[:], ALU.mult).then_inc(s_h, 1)

            def finish(t, j, par):
                dve.wait_ge(s_d, t + 1)
                dve.wait_ge(s_acl[par], j * 32 + 32)
                dve.scalar_tensor_tensor(out=x1t[:, par, :], in0=psO[:], scalar=gate[:, 0:1], in1=x1t[:, par, :],
                                         op0=ALU.mult, op1=ALU.add).then_inc(s_half, 1)
                dve.wait_ge(s_y[par], j * 16 * TOPK + 16 * TOPK)
                for k in range(TOPK):
                    if k:
                        dve.wait_ge(s_sum, t * SUMS + k)
                    dve.scalar_tensor_tensor(out=ac[:, par, :], in0=y[:, par, k, :], scalar=weights[:, bass.ds(t * TOPK + k, 1)],
                                             in1=ac[:, par, :], op0=ALU.mult, op1=ALU.add).then_inc(s_sum, 1)
                dve.wait_ge(s_half, t + 1)
                dve.wait_ge(s_sum, t * SUMS + TOPK)
                dve.tensor_tensor(ac[:, par, :], ac[:, par, :], x1t[:, par, :], ALU.add).then_inc(s_sum, 1)

            dve.wait_ge(s_c, 16 * NC)
            dve.wait_ge(s_tanh, 1)
            if route:
                st = Steps(dve, s_ch, ROUTE)
                ln = Steps(dve, s_ln, ROOT + 2)

            def norm(t, j, par):
                ln.start(t)
                after(dve, s_xn, t)
                dve.wait_ge(s_x[par], j * 16 + 16)
                dve.bn_stats(stats[:, 0:6], xt[:, par, 0:HB])
                ln.then(dve.bn_stats(stats[:, 6:12], xt[:, par, HB:H]), s_fence)
                ln.then(dve.bn_aggr(mv[:], stats[:]))
                inverse_root(ln, dve, rstd[:], mv[:, 1:2], root)
                after(dve, s_xtr, t - 1)
                after(dve, s_xnst[par], j * 16)
                dve.tensor_scalar(xn[:, par, :], xt[:, par, :], mv[:, 0:1], rstd[:], ALU.subtract,
                                  ALU.mult).then_inc(s_xn, 1)
                ln.end()

            def choose(t):
                st.start(t)
                dve.wait_ge(s_th, t + 1)
                scf = sc[:].rearrange("p g e -> p (g e)")
                st.then(dve.tensor_scalar(scores[:], th[:], 0.5, 0.5, ALU.mult, ALU.add))
                st.then(dve.tensor_tensor(scf, scores[:], bias[:], ALU.add), s_fence)
                for g in range(NG):
                    ins = dve.max(gm[:, g, :], sc[:, g, :])
                st.then(ins)
                st.then(dve.tensor_tensor(gs[:], gm[:, :, 0], gm[:, :, 1], ALU.add))
                other = gs[:].unsqueeze(1).to_broadcast([P, NG, NG])
                mine = gs[:].unsqueeze(2).to_broadcast([P, NG, NG])
                st.then(dve.tensor_tensor(gt[:], other, mine, ALU.is_gt))
                st.then(dve.tensor_tensor(eq[:], other, mine, ALU.is_equal))
                st.then(dve.tensor_tensor(eq[:], eq[:], lower[:], ALU.mult))
                st.then(dve.tensor_tensor(gt[:], gt[:], eq[:], ALU.add))
                st.then(dve.tensor_reduce(rank[:], gt[:], AX, ALU.add))
                st.then(dve.tensor_scalar(rank[:], rank[:], float(TG), None, ALU.is_lt))
                st.then(dve.tensor_tensor(sc[:], sc[:], rank[:].unsqueeze(2).to_broadcast([P, NG, EG]), ALU.mult), s_fence)
                st.then(dve.max(m8[:], scf), s_fence)
                st.then(dve.max_index(i8[:], m8[:], scf))
                st.then(dve.tensor_copy(idx[:], i8[:, 0:TOPK]))
                st.then(dve.tensor_tensor(oh[:], iota[:].unsqueeze(1).to_broadcast([P, TOPK, NE]),
                                          idx[:].unsqueeze(2).to_broadcast([P, TOPK, NE]), ALU.is_equal))
                after(dve, s_pos, t)
                dve.tensor_reduce(mask[:], oh[:].rearrange("p k e -> p e k"), AX, ALU.add).then_inc(s_mask, 1)
                st.then(dve.tensor_tensor(ow[:], oh[:], scores[:].unsqueeze(1).to_broadcast([P, TOPK, NE]), ALU.mult))
                st.then(dve.tensor_reduce(w4[:], ow[:], AX, ALU.add))
                st.then(dve.tensor_reduce(ws[:, 0:1], w4[:], AX, ALU.add))
                st.then(dve.tensor_scalar(ws[:, 0:1], ws[:, 0:1], 1e-20, None, ALU.add))
                st.then(dve.reciprocal(ws[:, 1:2], ws[:, 0:1]))
                st.then(dve.tensor_scalar(w4[:], w4[:], ws[:, 1:2], gate2[:, 0:1], ALU.mult, ALU.mult))
                assert st.n == CHOICE

            def queue(t, j, par):
                st.resume(t, CHOICE)
                dve.wait_ge(s_pos, t + 1)
                dve.tensor_tensor(ow[:], oh[:], psR[:, NE:2 * NE].unsqueeze(1).to_broadcast([P, TOPK, NE]),
                                  ALU.mult).then_inc(s_posr, 1)
                dve.wait_ge(s_mask, t + 1)
                dve.wait_ge(s_posr, t + 1)
                dve.tensor_tensor(run[:], run[:], mask[:], ALU.add).then_inc(s_run, 1)
                dve.wait_ge(s_run, t + 1)
                st.then(dve.tensor_reduce(pos[:], ow[:], AX, ALU.add))
                st.then(dve.tensor_scalar(over[:], pos[:], float(CAP), float(DROPPED), ALU.is_ge, ALU.mult))
                st.then(dve.scalar_tensor_tensor(out=sf[:], in0=idx[:], scalar=float(CAP), in1=pos[:], op0=ALU.mult,
                                                 op1=ALU.add))
                st.then(dve.tensor_tensor(sf[:], sf[:], over[:], ALU.add))
                after(dve, s_sct[par], j * 16 * TOPK)
                dve.tensor_copy(si[:, par, :], sf[:]).then_inc(s_slot, 1)
                dve.scalar_tensor_tensor(out=weights[:, bass.ds(t * TOPK, TOPK)], in0=pos[:], scalar=float(CAP), in1=w4[:],
                                         op0=ALU.is_lt, op1=ALU.mult)
                st.then(dve.tensor_copy(slots[:, bass.ds(t * TOPK, TOPK)], sf[:]))
                st.end()

            def pair(j):
                for par in range(2):
                    t, first, early, last = split(j, par)
                    if route and not last:
                        norm(t + 1, j + par, 1 - par)
                    if route and not first:
                        queue(t - 1, j - (par == 0), 1 - par)
                    if not route and not early:
                        finish(t - 2, j - 1, par)
                    if not first:
                        h_rest(t - 1)
                    if route:
                        choose(t)
                    if not last:
                        x_rest(t + 1, 1 - par)
                    multiply(t)

            if route:
                dve.wait_ge(s_init, 1)
                dve.tensor_scalar(gate2[:], gate[:], SCALE, None, ALU.mult)
                norm(0, 0, 0)
            x_rest(0, 0)
            for m in range(3):
                dve.wait_ge(s_whi, m + 1)
                dve.tensor_tensor(wsp[:, m, 1, :], raw[:, m % 2, :], f32(wsp[:, m, 0, :]), ALU.subtract).then_inc(s_wlo, 1)
            if not route:
                dve.wait_ge(s_wlo, 3)
                dve.memset(y, 0.0).then_inc(s_zero, 1)
            turns(dve, TT // 2, pair, last=True, first=2)
            if route:
                queue(TT - 1, TT // 2 - 1, 1)
            else:
                finish(TT - 2, TT // 2 - 1, 0)
            h_rest(TT - 1)
            if not route:
                finish(TT - 1, TT // 2 - 1, 1)


def experts(nc, io, dr):
    with ExitStack() as ctx:
        sb = lambda name, shape, dt=F32: ctx.enter_context(nc.sbuf_tensor(name, shape, dt))
        ps = lambda name, shape: ctx.enter_context(nc.psum_tensor(name, shape, F32))
        sem = Semaphores(nc, ctx)
        KF = F // P
        WN = KH * F
        IR, WR, XT = 4, 4, 4
        raw = sb("raw", [P, 2, WN])
        wsp = sb("wsp", [P, WR, 2, WN], F32R)
        ident = sb("ident4", [P, P])
        ids = sb("ids", [P, IR], I32)
        xg = sb("xg", [P, TPE, H])
        xT = sb("xgT", [P, TPE, 2, KH, P], F32R)
        sg = sb("sg4", [P, TPE, F])
        hT = sb("hT4", [P, TPE, 2, KF, P], F32R)
        ob = sb("ob", [P, TPE, H])
        psG = [ps(f"psG4{t}", [P, F]) for t in range(TPE)]
        psU = [ps(f"psU4{t}", [P, F]) for t in range(TPE)]
        psO = [ps(f"psO4{t}", [P, HB]) for t in range(2)]
        psT = [ps(f"psT4{t}", [P, 4, P]) for t in range(2)]

        s_c = sem("p4_constants")
        s_raw = [sem(f"p4_matrix_loaded{i}") for i in range(2)]
        s_ids = [sem(f"p4_ids_loaded{i}") for i in range(IR)]
        s_gat = [sem(f"p4_rows_gathered{i}") for i in range(TPE)]
        s_obst = [sem(f"p4_rows_stored{i}") for i in range(TPE)]
        s_whi = sem("p4_matrix_heads")
        s_wlo = sem("p4_matrix_rests")
        s_tr = sem("p4_transposed")
        s_thi = sem("p4_transposed_heads")
        s_tlo = sem("p4_transposed_rests")
        s_g = sem("p4_gate_product")
        s_u = sem("p4_up_product")
        s_sg = sem("p4_silu")
        s_h = sem("p4_hidden")
        s_d = sem("p4_down_product")
        s_oa = sem("p4_out_first_half")
        s_ob = sem("p4_out_second_half")
        s_carry = sem("p4_pool_carry")
        block = ctx.enter_context(nc.Block())
        f32 = lambda ap: ap.bitcast(F32)

        ROUNDS = [("h", 0, 0), ("x", 0, 0), ("x", 0, 1), ("h", 1, 0), ("x", 1, 0), ("x", 1, 1)]
        NR = len(ROUNDS)
        HEAD = 2 * TPE

        def rounds(e):
            last = isinstance(e, int) and e == NE - 1
            kept = [r for r in ROUNDS if r[0] == "h" or not last]
            return [(kind, t, hb, HEAD + e * NR + n, n % 2) for n, (kind, t, hb) in enumerate(kept)]

        def four(body):
            def turn(j):
                for x in range(XT):
                    body(j * XT + x, j, x)
            return turn

        @block.sync
        def _(sp):
            tab = dr["tab"].rearrange("(s p) o -> s p o", p=P)

            def load_ids(s, r):
                sp.dma_start(ids[:, r:r + 1], tab[s]).then_inc(s_ids[r], 16)

            def load_matrix(e, j, x, m):
                c = (3 * x + m) % 2
                after(sp, s_wlo, 3 * e + m - 1)
                src = (io["w1"], io["w3"], io["w2"])[m][e]
                sp.dma_start(raw[:, c, :].rearrange("p (k f) -> p k f", k=KF if m == 2 else KH),
                             src.rearrange("(k p) f -> p k f", p=P)).then_inc(s_raw[c], 16)

            sp.dma_start(ident[:], io["ident"]).then_inc(s_c, 16)
            for r in range(IR):
                load_ids(r, r)
            load_matrix(0, 0, 0, 0)
            load_matrix(0, 0, 0, 1)

            def expert(e, j, x):
                first, last = isinstance(e, int) and e == 0, isinstance(e, int) and e == NE - 1
                load_matrix(e, j, x, 2)
                if not last:
                    nj, nx = (j, x + 1) if x + 1 < XT else (j + 1, 0)
                    load_matrix(e + 1, nj, nx, 0)
                for t in range(TPE):
                    if not first:
                        sp.wait_ge(s_oa, TPE * (e - 1) + t + 1)
                        sp.wait_ge(s_ob, TPE * (e - 1) + t + 1)
                        sp.dma_start(dr["ob"].rearrange("(s p) h -> s p h", p=P)[TPE * (e - 1) + t], ob[:, t, :])\
                            .then_inc(s_obst[t], 16)
                if not (isinstance(e, int) and e + 2 >= NE):
                    for t in range(TPE):
                        sp.wait_ge(s_gat[t], e * 16 + 16)
                        load_ids(TPE * (e + 2) + t, (TPE * x + t) % IR)
                if not last:
                    load_matrix(e + 1, nj, nx, 1)

            turns(sp, NE // XT, four(expert), last=True)
            for t in range(TPE):
                sp.wait_ge(s_oa, TPE * (NE - 1) + t + 1)
                sp.wait_ge(s_ob, TPE * (NE - 1) + t + 1)
                sp.dma_start(dr["ob"].rearrange("(s p) h -> s p h", p=P)[TPE * (NE - 1) + t], ob[:, t, :])\
                    .then_inc(s_obst[t], 16)
            for s in s_obst:
                sp.wait_ge(s, 16 * NE)

        @block.gpsimd
        def _(pool):
            def expert(e, j, x):
                for t in range(TPE):
                    pool.wait_ge(s_ids[(TPE * x + t) % IR], (e // 2) * 16 + 16)
                    if isinstance(e, int) and e < 2:
                        pool.wait_ge(s_tr, 2 * t + 2) if e else None
                    else:
                        pool.wait_ge(s_tr, HEAD + (e - 2) * NR + (3 if t == 0 else 6))
                    pool.sem_inc(s_carry, 1)
                    r = (TPE * x + t) % IR
                    pool.indirect_dma_start(xg[:, t, :], None, dr["xn"],
                                            bass.IndirectOffsetOnAxis(ap=ids[:, r:r + 1], axis=0),
                                            bounds_check=NT - 1, oob_is_err=False).then_inc(s_gat[t], 16)

            turns(pool, NE // XT, four(expert))

        @block.tensor
        def _(pe):
            pe.wait_ge(s_c, 16)

            def transpose_round(kind, t, hb, n, bank, e):
                if kind == "h":
                    pe.wait_ge(s_h, TPE * e + t + 1)
                else:
                    pe.wait_ge(s_gat[t], e * 16 + 16)
                after(pe, s_tlo, n - 1)
                src = sg[:, t, :] if kind == "h" else xg[:, t, hb * HB:(hb + 1) * HB]
                for k in range(4):
                    mm = pe.transpose(psT[bank][:, k, :], src[:, k * P:(k + 1) * P], ident[:])
                mm.then_inc(s_tr, 1)

            def product(dst, lhs, rhs, done):
                for n, (l, r) in enumerate(zip(lhs, rhs)):
                    pe.matmul(dst, l[0], r[0], start=(n == 0), stop=False)
                    pe.matmul(dst, l[0], r[1], start=False, stop=False)
                    mm = pe.matmul(dst, l[1], r[0], start=False, stop=(n == len(lhs) - 1))
                mm.then_inc(done, 1)

            def weights_of(x, m, k, c0):
                slot = (3 * x + m) % WR
                width = H if m == 2 else F
                return [wsp[:, slot, part, k * width + c0:k * width + c0 + HB] for part in range(2)]

            def expert(e, j, x):
                for m, dst, done, read in ((0, psG, s_g, s_sg), (1, psU, s_u, s_h)):
                    pe.wait_ge(s_wlo, 3 * e + m + 1)
                    for t in range(TPE):
                        if m == 0:
                            pe.wait_ge(s_tlo, (HEAD + (e - 1) * NR + (3 if t == 0 else 6)) if not (isinstance(e, int) and e == 0)
                                       else 2 * t + 2)
                        after(pe, read, TPE * (e - 1) + t + 1 if not (isinstance(e, int) and e == 0) else 0)
                        product(dst[t][:], [[xT[:, t, part, k, :] for part in range(2)] for k in range(KH)],
                                [weights_of(x, m, k, 0) for k in range(KH)], done)
                for kind, t, hb, n, bank in rounds(e):
                    transpose_round(kind, t, hb, n, bank, e if kind == "h" else e + 1)
                pe.wait_ge(s_wlo, 3 * e + 3)
                rest = {(kind, t): n for kind, t, hb, n, bank in rounds(e)}
                for t in range(TPE):
                    pe.wait_ge(s_tlo, rest["h", t] + 1)
                    for hb in range(2):
                        after(pe, (s_oa, s_ob)[hb], TPE * e + t)
                        product(psO[hb][:], [[hT[:, t, part, k, :] for part in range(2)] for k in range(KF)],
                                [weights_of(x, 2, k, hb * HB) for k in range(KF)], s_d)

            for n in range(HEAD):
                transpose_round("x", n // 2, n % 2, n, n % 2, 0)
            turns(pe, NE // XT, four(expert), last=True)

        def splits(eng, e, step):
            for kind, t, hb, n, bank in rounds(e):
                dst = hT[:, t, :, :, :] if kind == "h" else xT[:, t, :, 4 * hb:4 * hb + 4, :]
                step(kind, t, n, bank, dst, e)

        @block.scalar
        def _(act):
            def head(kind, t, n, bank, dst, e):
                act.wait_ge(s_tr, n + 1)
                if kind == "h":
                    after(act, s_d, 4 * (e - 1) + 2 * t + 2 if not (isinstance(e, int) and e == 0) else 0)
                elif e is not None:
                    act.wait_ge(s_u, TPE * e + TPE)
                act.activation(dst[:, 0], psT[bank][:], ACT.Copy).then_inc(s_thi, 1)

            def matrix_head(e, j, x, m):
                c, slot = (3 * x + m) % 2, (3 * x + m) % WR
                act.wait_ge(s_raw[c], ((3 * e + m) // 2) * 16 + 16)
                if m == 0:
                    after(act, s_d, 4 * (e - 1) if not (isinstance(e, int) and e < 2) else 0)
                else:
                    after(act, (s_g, s_u)[m - 1], TPE * e)
                act.activation(wsp[:, slot, 0, :], raw[:, c, :], ACT.Copy).then_inc(s_whi, 1)

            def out_half(e, t):
                act.wait_ge(s_d, 4 * e + 2 * t + 1)
                after(act, s_obst[t], e * 16)
                act.activation(ob[:, t, 0:HB], psO[0][:], ACT.Copy).then_inc(s_oa, 1)

            def silu(e, t):
                act.wait_ge(s_g, TPE * e + t + 1)
                if not (isinstance(e, int) and e == 0):
                    act.wait_ge(s_tr, HEAD + (e - 1) * NR + (1 if t == 0 else 4))
                act.activation(sg[:, t, :], psG[t][:], ACT.Silu).then_inc(s_sg, 1)

            def expert(e, j, x):
                last = isinstance(e, int) and e == NE - 1
                nj, nx = (j, x + 1) if x + 1 < XT else (j + 1, 0)
                matrix_head(e, j, x, 2)
                for t in range(TPE):
                    silu(e, t)
                if not last:
                    matrix_head(e + 1, nj, nx, 0)
                splits(act, e, head)
                out_half(e, 0)
                if not last:
                    matrix_head(e + 1, nj, nx, 1)
                out_half(e, 1)

            for n in range(HEAD):
                head("x", n // 2, n, n % 2, xT[:, n // 2, :, 4 * (n % 2):4 * (n % 2) + 4, :], None)
            matrix_head(0, 0, 0, 0)
            matrix_head(0, 0, 0, 1)
            turns(act, NE // XT, four(expert), last=True)

        @block.vector
        def _(dve):
            def rest(kind, t, n, bank, dst, e):
                dve.wait_ge(s_thi, n + 1)
                dve.tensor_tensor(dst[:, 1], psT[bank][:], f32(dst[:, 0]), ALU.subtract).then_inc(s_tlo, 1)

            def matrix_rest(e, j, x, m):
                c, slot = (3 * x + m) % 2, (3 * x + m) % WR
                dve.wait_ge(s_whi, 3 * e + m + 1)
                dve.tensor_tensor(wsp[:, slot, 1, :], raw[:, c, :], f32(wsp[:, slot, 0, :]), ALU.subtract).then_inc(s_wlo, 1)

            def out_half(e, t):
                dve.wait_ge(s_d, 4 * e + 2 * t + 2)
                after(dve, s_obst[t], e * 16)
                dve.tensor_copy(ob[:, t, HB:H], psO[1][:]).then_inc(s_ob, 1)

            def expert(e, j, x):
                last = isinstance(e, int) and e == NE - 1
                nj, nx = (j, x + 1) if x + 1 < XT else (j + 1, 0)
                matrix_rest(e, j, x, 2)
                if not last:
                    matrix_rest(e + 1, nj, nx, 0)
                for t in range(TPE):
                    dve.wait_ge(s_sg, TPE * e + t + 1)
                    dve.wait_ge(s_u, TPE * e + t + 1)
                    dve.tensor_tensor(sg[:, t, :], sg[:, t, :], psU[t][:], ALU.mult).then_inc(s_h, 1)
                splits(dve, e, rest)
                out_half(e, 0)
                if not last:
                    matrix_rest(e + 1, nj, nx, 1)
                out_half(e, 1)

            for n in range(HEAD):
                rest("x", n // 2, n, n % 2, xT[:, n // 2, :, 4 * (n % 2):4 * (n % 2) + 4, :], None)
            matrix_rest(0, 0, 0, 0)
            matrix_rest(0, 0, 0, 1)
            turns(dve, NE // XT, four(expert), last=True)


def program(nc, io, out):
    dt = lambda name, shape, t=F32: nc.dram_tensor(name, shape, t, kind="Internal").ap()
    dr = {k: dt("scratch_" + k, s) for k, s in dict(
        a=(ET, P, NST + 1), x1=(B, L, H), u=(B * ET, P, L), dl=(B * ET, P, L), du=(B * ET, P, L), sz=(B * ET, P, L),
        bc=(B, NST, 2, L), xn=(NT, H), acc=(TT, P, H), ob=(NE * CAP, H)).items()}
    dr["tab"] = dt("scratch_tab", (NE * CAP, 1), I32)
    mamba_inputs(nc, io, dr)
    selective_scan(nc, io, dr)
    with (nc.sbuf_tensor("slots", [P, TT * TOPK], I32) as slots, nc.sbuf_tensor("weights", [P, TT * TOPK], F32) as weights):
        shared_pass(nc, io, dr, 0, slots, weights)
        experts(nc, io, dr)
        shared_pass(nc, io, dr, 1, slots, weights, out)


def kernel(x, ctx_1024, g_xattn, g_ffn, L0_xattn_in_proj_w, L0_xattn_conv_w, L0_xattn_conv_b, L0_xattn_x_proj_w,
           L0_xattn_dt_proj_w, L0_xattn_dt_proj_b, L0_xattn_A_log, L0_xattn_D, L0_ffn_gate_w, L0_ffn_gate_bias,
           L0_ffn_w1, L0_ffn_w2, L0_ffn_w3, L0_ffn_shared_gate, L0_ffn_shared_up, L0_ffn_shared_down):
    import numpy as np
    import concourse.bacc as bacc
    from concourse.bass_utils import run_bass_kernel_spmd

    per_tile = lambda v: np.ascontiguousarray(np.asarray(v).reshape(-1, P).T)
    t = lambda v: np.ascontiguousarray(np.asarray(v).T)
    arrays = dict(
        x=np.asarray(x), ctxT=np.ascontiguousarray(np.asarray(ctx_1024).transpose(0, 2, 1)),
        w_in=t(L0_xattn_in_proj_w), w_x=t(L0_xattn_x_proj_w), w_dt=t(L0_xattn_dt_proj_w),
        conv_w=np.asarray(L0_xattn_conv_w), conv_b=per_tile(L0_xattn_conv_b), dt_b=per_tile(L0_xattn_dt_proj_b),
        a_log_d=np.concatenate([np.asarray(L0_xattn_A_log), np.asarray(L0_xattn_D)[:, None]], 1), g_x=np.asarray(g_xattn), g_f=np.asarray(g_ffn),
        ident=np.eye(P, dtype=np.float32), tri=np.triu(np.ones((P, P), np.float32), 1),
        iota=np.arange(NE, dtype=np.float32), lower=np.tril(np.ones((NG, NG), np.float32), -1).reshape(-1),
        tok=(np.arange(P)[:, None] + P * np.arange(2)[None, :]).astype(np.int32), gate_w=t(L0_ffn_gate_w),
        gate_b=np.asarray(L0_ffn_gate_bias), w1=np.asarray(L0_ffn_w1), w2=np.asarray(L0_ffn_w2), w3=np.asarray(L0_ffn_w3),
        w_sg=np.asarray(L0_ffn_shared_gate), w_su=np.asarray(L0_ffn_shared_up), w_sd=np.asarray(L0_ffn_shared_down))
    nc = bacc.Bacc("TRN2", target_bir_lowering=False, num_devices=1)
    io = {k: nc.dram_tensor("in_" + k, a.shape, mybir.dt.from_np(a.dtype), kind="ExternalInput").ap()
          for k, a in arrays.items()}
    out = nc.dram_tensor("out", (B, L, H), F32, kind="ExternalOutput").ap()
    program(nc, io, out)
    r = run_bass_kernel_spmd(nc, [{"in_" + k: a for k, a in arrays.items()}], core_ids=[0])
    return r.results[0]["out"]
```

```python
from contextlib import ExitStack

import concourse.bass as bass
from concourse import mybir

P = 128
B, L, DM = 4, 1024, 512
DI, NST, DR, DC = 1024, 16, 32, 4
H, F, FS = 1024, 512, 1024
NE, TOPK, NG, TG = 32, 4, 4, 2
CAP = 2 * (2 * 512 * TOPK // NE)
NT = B * L
SCALE, EPS = 2.0, 1e-5
ET = DI // P
KD = DM // P
KH = H // P
TT = NT // P
ST = NE * CAP // P
TPE = CAP // P
HB = 512
NEWTON = 3
ROOT = 3 + 3 * NEWTON
CHOICE = 21
ROUTE = CHOICE + 5
DROPPED = 1 << 16

ALU = mybir.AluOpType
ACT = mybir.ActivationFunctionType
F32 = mybir.dt.float32
F32R = mybir.dt.float32r
I32 = mybir.dt.int32
U32 = mybir.dt.uint32
AX = mybir.AxisListType.X


def after(eng, sem, value):
    if isinstance(value, int):
        if value > 0:
            eng.wait_ge(sem, value)
    else:
        assert value.min_val > 0
        eng.wait_ge(sem, value)


def turns(eng, n, body, last=False, first=1):
    for i in range(first):
        body(i)
    with eng.Fori(first, n - last) as i:
        body(i)
    if last:
        body(n - 1)


class Semaphores(list):

    def __init__(self, nc, ctx):
        self.nc = nc
        ctx.callback(self.give_back)

    def give_back(self):
        self.nc.clear_and_free_semaphores(self)
        self.nc.all_engine_barrier()

    def __call__(self, name):
        self.append(self.nc.alloc_semaphore(name))
        return self[-1]


class Steps:

    def __init__(self, eng, sem, per):
        self.eng, self.sem, self.per, self.n, self.turn = eng, sem, per, 0, 0

    def start(self, turn):
        self.turn, self.n = turn, 0

    def resume(self, turn, n):
        self.turn, self.n = turn, n

    def end(self):
        assert self.n == self.per, (self.n, self.per)

    def then(self, ins, gate=None):
        ins.then_inc(self.sem, 1)
        self.n += 1
        self.eng.wait_ge(self.sem, self.turn * self.per + self.n)
        if gate is not None:
            self.eng.sem_inc(gate, 1)


def inverse_root(st, dve, y, var, tmp):
    st.then(dve.tensor_scalar(tmp[:, 0:1], var, EPS, None, ALU.add))
    st.then(dve.tensor_scalar(tmp[:, 1:2].bitcast(I32), tmp[:, 0:1].bitcast(I32), 1, None, ALU.arith_shift_right))
    st.then(dve.tensor_scalar(y.bitcast(I32), tmp[:, 1:2].bitcast(I32), -1.0, float(0x5F3759DF), ALU.mult, ALU.add))
    for _ in range(NEWTON):
        st.then(dve.scalar_tensor_tensor(out=tmp[:, 1:2], in0=y, scalar=y, in1=tmp[:, 0:1], op0=ALU.mult, op1=ALU.mult))
        st.then(dve.tensor_scalar(tmp[:, 1:2], tmp[:, 1:2], -0.5, 1.5, ALU.mult, ALU.add))
        st.then(dve.tensor_tensor(y, y, tmp[:, 1:2], ALU.mult))


def mamba_inputs(nc, io, dr):
    with ExitStack() as ctx:
        sb = lambda name, shape, dt=F32: ctx.enter_context(nc.sbuf_tensor(name, shape, dt))
        sem = Semaphores(nc, ctx)
        DT, LOG, SR = ET + 2, ET + 4, 4
        w_in = sb("w_in", [P, KD, DI])
        w_x = sb("w_x", [P, ET, DR + 2 * NST])
        w_dt = sb("w_dt", [DR, DI])
        conv_w = sb("conv_w", [P, ET, DC])
        conv_b = sb("conv_b", [P, ET])
        dt_b = sb("dt_b", [P, ET])
        a_neg = sb("a_neg", [P, ET, NST + 1])
        ctxT = sb("ctxT", [P, 2 * KD * L])
        xpad = sb("xpad", [P, 2, L + DC])
        conv = sb("conv", [P, 2, L])
        u = sb("u", [P, 2 * ET * L])
        xd = sb("xd", [DR + 2 * NST, L])
        ebuf = sb("ebuf", [P, SR, L])
        rbuf = sb("rbuf", [P, SR, L])
        lbuf = sb("lbuf", [P, SR, L])
        cbuf = sb("cbuf", [P, 2, L])
        xz = sb("xz", [P, 2, L])
        stats = sb("stats", [P, 12])
        mv = sb("mv", [P, 2])
        rstd = sb("rstd", [P, 2, 2])
        root = sb("root", [P, 2])
        psX = [ctx.enter_context(nc.psum_tensor(f"psX{i}", [P, L], F32)) for i in range(2)]
        psT = ctx.enter_context(nc.psum_tensor("psT", [P, L], F32))
        psD = ctx.enter_context(nc.psum_tensor("psD", [DR + 2 * NST, L], F32))

        s_w = sem("p1_weights")
        s_first = sem("p1_first_operands")
        s_w2 = sem("p1_in_proj_rest")
        s_ctx = sem("p1_ctx_loaded")
        s_pad0 = sem("p1_padding_zero")
        s_psx = sem("p1_psum_full")
        s_pad = sem("p1_xpad_full")
        s_conv = sem("p1_conv_done")
        s_u = sem("p1_u_ready")
        s_xp = sem("p1_xproj_done")
        s_xd = sem("p1_xd_ready")
        s_xdst = sem("p1_xd_stored")
        s_dt = sem("p1_step_sizes")
        s_abs = sem("p1_abs_done")
        s_exp = sem("p1_exp_done")
        s_ln = sem("p1_ln_done")
        s_cor = sem("p1_correction")
        s_lc = sem("p1_log1p")
        s_dl = sem("p1_delta")
        s_du = sem("p1_du")
        s_st = [sem(f"p1_delta_stored{i}") for i in range(SR)]
        s_ust = [sem(f"p1_u_stored{i}") for i in range(ET)]
        s_xz = [sem(f"p1_xz_loaded{i}") for i in range(2)]
        s_z = sem("p1_z_stats")
        s_sz = sem("p1_gate")
        s_szst = [sem(f"p1_gate_stored{i}") for i in range(2)]
        s_ch = sem("p1_dve_steps")
        s_gate = sem("p1_dve_gate")
        s_a = sem("p1_a")
        s_a2 = sem("p1_a2")
        s_ast = sem("p1_a_stored")
        s_cst = sem("p1_correction_steps")
        block = ctx.enter_context(nc.Block())

        def behind(b, et, lag):
            b, et = b + (et - lag) // ET, (et - lag) % ET
            if isinstance(b, int) and not 0 <= b < B:
                return None
            return b, et, b * ET + et

        def steps(eng, body, ahead=0):
            def batch(b):
                for et in range(ET):
                    body(b, et)
            batch(0)
            batch(1)
            with eng.Fori(2, B - ahead) as b:
                batch(b)
            for b in range(B - ahead, B):
                batch(b)
            batch(B)
            batch(B + 1)

        def on_tile(b, et, lag, do):
            tile = behind(b, et, lag)
            if tile is not None:
                do(*tile)

        def u_at(b, et, start=0, size=L):
            return u[:, bass.ds(((b % 2) * ET + et) * L + start, size)]

        def tail(q):
            return isinstance(q, int) and q >= B * ET - LOG

        def times_u(eng, b, et, q):
            eng.wait_ge(s_dl, q + 1)
            after(eng, s_du, q)
            eng.tensor_tensor(ebuf[:, et % SR, :], rbuf[:, et % SR, :], u_at(b, et), ALU.mult).then_inc(s_du, 1)

        @block.sync
        def _(sp):
            w_src = io["w_in"].rearrange("(k p) e -> p k e", p=P)
            ctx_src = io["ctxT"].rearrange("b (k p) l -> b p k l", p=P)
            ctx_at = lambda b: ctxT[:, bass.ds((b % 2) * KD * L, KD * L)].rearrange("p (k l) -> p k l", k=KD)
            sp.dma_start(w_in[:, :, 0:HB], w_src[:, :, 0:HB]).then_inc(s_first, 16)
            sp.dma_start(ctx_at(0)[:, :, 0:HB], ctx_src[0][:, :, 0:HB]).then_inc(s_first, 16)

            def load_x(b, et, q):
                after(sp, s_szst[et % 2], (b * (ET // 2) + et // 2) * 16)
                sp.dma_start(xz[:, et % 2, :], io["x"][b, et * P:(et + 1) * P, :]).then_inc(s_xz[et % 2], 16)

            load_x(0, 0, 0)

            def load_ctx(b):
                after(sp, s_psx, (b - 1) * ET)
                sp.wait_ge(s_ctx, b * 16)
                sp.dma_start(ctx_at(b), ctx_src[b]).then_inc(s_ctx, 16)

            for dst, src in ((w_x[:], io["w_x"].rearrange("(t p) k -> p t k", p=P)), (w_dt[:], io["w_dt"]),
                             (conv_w[:], io["conv_w"].rearrange("(t p) k -> p t k", p=P)),
                             (conv_b[:], io["conv_b"]), (dt_b[:], io["dt_b"]),
                             (a_neg[:], io["a_log_d"].rearrange("(t p) k -> p t k", p=P))):
                sp.dma_start(dst, src).then_inc(s_w, 16)
            sp.dma_start(ctx_at(0)[:, :, HB:L], ctx_src[0][:, :, HB:L]).then_inc(s_ctx, 16)
            sp.dma_start(w_in[:, :, HB:DI], w_src[:, :, HB:DI]).then_inc(s_w2, 16)

            def store_gate(b, et, q):
                sp.wait_ge(s_sz, q + 1)
                sp.dma_start(dr["sz"][q], xz[:, et % 2, :]).then_inc(s_szst[et % 2], 16)

            def store_u(b, et, q):
                sp.wait_ge(s_u, q + 1)
                sp.dma_start(dr["u"][q], u_at(b, et)).then_inc(s_ust[et], 16)

            def store_bc(b):
                sp.wait_ge(s_xd, b + 1)
                for c in range(2):
                    sp.dma_start(dr["bc"][b, :, c, :], xd[DR + c * NST:DR + (c + 1) * NST, :]).then_inc(s_xdst, 16)

            def store_steps(b, et, q):
                sp.wait_ge(s_dl, q + 1)
                sp.dma_start(dr["dl"][q], rbuf[:, et % SR, :]).then_inc(s_st[et % SR], 16)
                sp.wait_ge(s_du, q + 1)
                sp.dma_start(dr["du"][q], ebuf[:, et % SR, :]).then_inc(s_st[et % SR], 16)

            def step(b, et):
                if not (isinstance(b, int) and b == 0 and et == 0):
                    on_tile(b, et, 0, load_x)
                if et == 1 and not (isinstance(b, int) and b + 1 >= B):
                    load_ctx(b + 1)
                on_tile(b, et, 1, store_gate)
                on_tile(b, et, 2, store_u)
                if et == 4 and not (isinstance(b, int) and not 0 < b <= B):
                    store_bc(b - 1)
                on_tile(b, et, LOG + 2, store_steps)

            steps(sp, step, ahead=1)
            sp.wait_ge(s_a2, 1)
            sp.dma_start(dr["a"].rearrange("t p n -> p t n"), a_neg[:]).then_inc(s_ast, 16)
            sp.wait_ge(s_ast, 16)
            sp.wait_ge(s_xdst, 32 * B)
            for s in s_ust:
                sp.wait_ge(s, 16 * B)
            for s in s_st:
                sp.wait_ge(s, 32 * B * ET // SR)
            for s in s_szst:
                sp.wait_ge(s, 16 * B * ET // 2)

        @block.tensor
        def _(pe):
            pe.wait_ge(s_first, 32)

            def in_proj(b, et, q):
                start = isinstance(b, int) and b == 0
                if et == 0 and not start:
                    pe.wait_ge(s_ctx, b * 16 + 16)
                if start and et == HB // P:
                    pe.wait_ge(s_w2, 16)
                after(pe, s_pad, q - 1)
                for hb in range(2):
                    if start and et == 0 and hb == 1:
                        pe.wait_ge(s_ctx, 16)
                    for k in range(KD):
                        mm = pe.matmul(psX[et % 2][:, hb * HB:(hb + 1) * HB], w_in[:, k, et * P:(et + 1) * P],
                                       ctxT[:, bass.ds((b % 2) * KD * L + k * L + hb * HB, HB)],
                                       start=(k == 0), stop=(k == KD - 1))
                mm.then_inc(s_psx, 1)

            def dt_proj(b, et, q):
                if et == 0:
                    pe.wait_ge(s_xd, b + 1)
                after(pe, s_abs, q)
                for hb in range(2):
                    mm = pe.matmul(psT[:, hb * HB:(hb + 1) * HB], w_dt[:, et * P:(et + 1) * P],
                                   xd[0:DR, hb * HB:(hb + 1) * HB], start=True, stop=True)
                mm.then_inc(s_dt, 1)

            def x_proj(b, et, q):
                pe.wait_ge(s_u, q + 1)
                if et == 0:
                    after(pe, s_xd, b)
                for hb in range(2):
                    mm = pe.matmul(psD[:, hb * HB:(hb + 1) * HB], w_x[:, et, :], u_at(b, et, hb * HB, HB),
                                   start=(et == 0), stop=(et == ET - 1))
                mm.then_inc(s_xp, 1)

            def step(b, et):
                on_tile(b, et, 0, in_proj)
                if isinstance(b, int) and b == 0 and et == 1:
                    pe.wait_ge(s_w, 16 * 6)
                on_tile(b, et, DT, dt_proj)
                on_tile(b, et, 2, x_proj)

            steps(pe, step)

        @block.scalar
        def _(act):
            act.wait_ge(s_w, 16 * 6)
            act.activation(a_neg[:, :, 0:NST], a_neg[:, :, 0:NST], ACT.Exp).then_inc(s_a, 1)
            act.wait_ge(s_pad0, 1)

            def low_rank(b):
                act.wait_ge(s_xp, b * ET + ET)
                after(act, s_xdst, b * 32)
                act.activation(xd[:, :], psD[:, :], ACT.Copy).then_inc(s_xd, 1)

            def u_silu(b, et, q):
                act.wait_ge(s_conv, q + 1)
                after(act, s_ust[et], b * 16)
                after(act, s_du, q - 2 * ET + 2)
                act.activation(u_at(b, et), conv[:, et % 2, :], ACT.Silu).then_inc(s_u, 1)

            def z_silu(b, et, q):
                act.wait_ge(s_z, q + 1)
                act.activation(xz[:, et % 2, :], xz[:, et % 2, :], ACT.Silu, bias=rstd[:, et % 2, 1:2],
                               scale=rstd[:, et % 2, 0:1]).then_inc(s_sz, 1)

            def pad(b, et, q):
                act.wait_ge(s_psx, q + 1)
                after(act, s_conv, q - 1)
                act.activation(xpad[:, et % 2, DC - 1:DC - 1 + L], psX[et % 2][:, :], ACT.Copy).then_inc(s_pad, 1)

            def softplus(b, et, q):
                act.wait_ge(s_dt, q + 1)
                after(act, s_st[et % SR], (b * (ET // SR) + et // SR) * 32)
                act.activation(rbuf[:, et % SR, :], psT[:, :], ACT.Relu, bias=dt_b[:, et:et + 1])
                act.activation(ebuf[:, et % SR, :], psT[:, :], ACT.Abs, bias=dt_b[:, et:et + 1]).then_inc(s_abs, 1)
                if et % 2:
                    act.wait_ge(s_abs, q + 1)
                    for e in (et - 1, et):
                        act.activation(ebuf[:, e % SR, :], ebuf[:, e % SR, :], ACT.Exp, scale=-1.0).then_inc(s_exp, 1)
                    act.wait_ge(s_exp, q + 1)
                    after(act, s_dl, q - SR + 1)
                    for e in (et - 1, et):
                        act.activation(lbuf[:, e % SR, :], ebuf[:, e % SR, :], ACT.Ln, bias=1.0).then_inc(s_ln, 1)

            def step(b, et):
                if et == 2 and not (isinstance(b, int) and not 0 < b <= B):
                    low_rank(b - 1)
                on_tile(b, et, 0, pad)
                on_tile(b, et, 1, u_silu)
                on_tile(b, et, 0, z_silu)
                on_tile(b, et, DT, softplus)

            steps(act, step)

        @block.vector
        def _(dve):
            dve.memset(xpad[:, :, 0:DC - 1], 0.0).then_inc(s_pad0, 1)
            st = Steps(dve, s_ch, 5 + ROOT)
            cs = Steps(dve, s_cst, 1)

            def gate_stats(b, et, q):
                st.start(q)
                dve.wait_ge(s_xz[et % 2], (b * (ET // 2) + et // 2) * 16 + 16)
                dve.bn_stats(stats[:, 0:6], xz[:, et % 2, 0:HB])
                st.then(dve.bn_stats(stats[:, 6:12], xz[:, et % 2, HB:L]), s_gate)
                st.then(dve.bn_aggr(mv[:, :], stats[:, :]))
                after(dve, s_sz, q - 1)
                inverse_root(st, dve, rstd[:, et % 2, 0:1], mv[:, 1:2], root)
                dve.scalar_tensor_tensor(out=rstd[:, et % 2, 1:2], in0=mv[:, 0:1], scalar=-1.0,
                                         in1=rstd[:, et % 2, 0:1], op0=ALU.mult, op1=ALU.mult).then_inc(s_z, 1)

            def convolve(b, et, q):
                dve.wait_ge(s_pad, q + 1)
                after(dve, s_u, q - 1)
                c = conv[:, et % 2, :]
                st.then(dve.tensor_scalar(c, xpad[:, et % 2, 0:L], conv_w[:, et, 0:1], conv_b[:, et:et + 1],
                                          ALU.mult, ALU.add))
                for k in range(1, DC - 1):
                    st.then(dve.scalar_tensor_tensor(out=c, in0=xpad[:, et % 2, k:k + L], scalar=conv_w[:, et, k:k + 1],
                                                     in1=c, op0=ALU.mult, op1=ALU.add))
                dve.scalar_tensor_tensor(out=c, in0=xpad[:, et % 2, DC - 1:DC - 1 + L],
                                         scalar=conv_w[:, et, DC - 1:DC], in1=c, op0=ALU.mult,
                                         op1=ALU.add).then_inc(s_conv, 1)
                st.end()

            def correction(b, et, q):
                cs.start(q)
                dve.wait_ge(s_exp, q + 1)
                after(dve, s_lc, q - 1)
                c = cbuf[:, et % 2, :]
                cs.then(dve.tensor_scalar(c, ebuf[:, et % SR, :], 1.0, 1.0, ALU.add, ALU.subtract))
                dve.tensor_tensor(c, ebuf[:, et % SR, :], c, ALU.subtract).then_inc(s_cor, 1)

            def step(b, et):
                on_tile(b, et, 0, gate_stats)
                if isinstance(b, int) and b == 0 and et == 0:
                    dve.wait_ge(s_a, 1)
                    dve.tensor_scalar(a_neg[:, :, 0:NST], a_neg[:, :, 0:NST], -1.0, None, ALU.mult).then_inc(s_a2, 1)
                on_tile(b, et, LOG, correction)
                on_tile(b, et, LOG + 1, lambda b, et, q: times_u(dve, b, et, q) if tail(q) else None)
                on_tile(b, et, 0, convolve)

            steps(dve, step)

        @block.gpsimd
        def _(pool):
            def delta(b, et, q):
                pool.wait_ge(s_ln, q + 1)
                pool.wait_ge(s_cor, q + 1)
                e = et % SR
                pool.tensor_tensor(lbuf[:, e, :], lbuf[:, e, :], cbuf[:, et % 2, :], ALU.add).then_inc(s_lc, 1)
                pool.wait_ge(s_lc, q + 1)
                pool.tensor_tensor(rbuf[:, e, :], rbuf[:, e, :], lbuf[:, e, :], ALU.add).then_inc(s_dl, 1)
                if not tail(q):
                    times_u(pool, b, et, q)

            steps(pool, lambda b, et: on_tile(b, et, LOG, delta))


def selective_scan(nc, io, dr):
    with ExitStack() as ctx:
        sb = lambda name, shape, dt=F32: ctx.enter_context(nc.sbuf_tensor(name, shape, dt))
        sem = Semaphores(nc, ctx)
        NU = B * ET
        HR, IR = 4, 4
        HALF = ET // 2
        GATED, SPREAD, COPIED, SKIPPED = 1, (3, 6), 10, 10
        ident = sb("ident2", [P, P])
        skip = sb("skip", [P, P])
        gate = sb("gate2", [P, 1])
        bc = sb("bc", [P, NST, 2, L])
        ad = sb("ad", [P, 2, NST + 1])
        dl = sb("dl", [P, 2, L])
        du = sb("du", [P, 2, L])
        ut = sb("ut", [P, L])
        sz = sb("szt", [P, L])
        xl = sb("xl", [P, ET, P])
        xo = sb("xo", [P, ET, P])
        dbu = sb("dbu", [P, IR, L])
        h = sb("h", [P, HR, L])
        hc = sb("hc", [P, 2, L])
        yt = sb("yt", [P, L])
        da = [ctx.enter_context(nc.psum_tensor(f"da{i}", [P, L], F32)) for i in range(2)]
        psy = ctx.enter_context(nc.psum_tensor("psy", [P, L], F32))
        pst = ctx.enter_context(nc.psum_tensor("pst", [P, ET, P], F32))

        s_c = sem("p2_constants")
        s_gate = sem("p2_gate")
        s_bc = [sem(f"p2_bc_loaded{n}") for n in range(NST)]
        s_ld = [sem(f"p2_unit_loaded{i}") for i in range(2)]
        s_ut = sem("p2_u_loaded")
        s_szl = sem("p2_silu_loaded")
        s_xl = sem("p2_x_loaded")
        s_xst = sem("p2_x1_stored")
        s_da = sem("p2_decay")
        s_dbu = sem("p2_input")
        s_scan = sem("p2_state")
        s_hc = sem("p2_state_times_c")
        s_ys = sem("p2_summed")
        s_skip = sem("p2_skip_matrix")
        s_gated = sem("p2_gated")
        s_tr = sem("p2_transposed")
        s_x1 = sem("p2_x1")
        block = ctx.enter_context(nc.Block())

        @block.sync
        def _(sp):
            def load_steps(i, par):
                sp.dma_start(dl[:, par, :], dr["dl"][i]).then_inc(s_ld[par], 16)
                sp.dma_start(du[:, par, :], dr["du"][i]).then_inc(s_ld[par], 16)
                sp.dma_start(ad[:, par, :], dr["a"][i % ET]).then_inc(s_ld[par], 16)

            def load_bc(b, n):
                sp.dma_start(bc[:, n], dr["bc"][b, n].partition_broadcast(P)).then_inc(s_bc[n], 16)

            def store(i, b, et):
                sp.wait_ge(s_x1, i + 1)
                sp.dma_start(dr["x1"][b].rearrange("(t p) (e c) -> e p t c", p=P, c=P)[et], xo[:]).then_inc(s_xst, 16)

            load_steps(0, 0)
            for n in range(NST):
                load_bc(0, n)
                if n == NST // 2:
                    sp.dma_start(ut[:], dr["u"][0]).then_inc(s_ut, 16)

            def batch(b):
                for et in range(ET):
                    i = b * ET + et
                    known = isinstance(b, int)
                    first, final, last_batch = known and i == 0, known and i == NU - 1, known and b == B - 1
                    after(sp, s_scan, i * NST)
                    if not final:
                        load_steps(i + 1, (et + 1) % 2)
                    for n in range(NST):
                        if n == GATED:
                            after(sp, s_gated, i)
                            sp.dma_start(sz[:], dr["sz"][i]).then_inc(s_szl, 16)
                        if n == SPREAD[1]:
                            after(sp, s_tr, 2 * i)
                            sp.dma_start(xl[:], io["x"][b].rearrange("(t p) (e c) -> e p t c", p=P, c=P)[et])\
                                .then_inc(s_xl, 16)
                        if n == COPIED and not first:
                            store(i - 1, b if et else b - 1, (et - 1) % ET)
                        if n == SKIPPED + 1 and not final:
                            sp.wait_ge(s_ys, i * NST + n + 1)
                            sp.dma_start(ut[:], dr["u"][i + 1]).then_inc(s_ut, 16)
                        if et == ET - 1 and not last_batch:
                            sp.wait_ge(s_hc, i * NST + n + 1)
                            load_bc(b + 1, n)

            turns(sp, B, batch, last=True)
            store(NU - 1, B - 1, ET - 1)
            sp.wait_ge(s_xst, 16 * NU)

        @block.scalar
        def _(act):
            act.dma_start(gate[:], io["g_x"].partition_broadcast(P)).then_inc(s_c, 16)
            act.dma_start(ident[:], io["ident"]).then_inc(s_c, 16)
            act.wait_ge(s_c, 32)
            act.activation(gate[:], gate[:], ACT.Tanh).then_inc(s_gate, 1)

            def copy_out(i):
                act.wait_ge(s_tr, 2 * i + 2)
                after(act, s_xst, i * 16)
                act.activation(xo[:], pst[:], ACT.Copy).then_inc(s_x1, 1)

            def pair(j):
                for par in range(2):
                    i = j * 2 + par
                    first = isinstance(j, int) and i == 0
                    act.wait_ge(s_ld[par], j * 48 + 48)
                    for n in range(NST):
                        after(act, s_scan, i * NST + n - 1)
                        act.activation(da[n % 2][:, :], dl[:, par, :], ACT.Exp, scale=ad[:, par, n:n + 1]).then_inc(s_da, 1)
                        if n == 2:
                            if not first:
                                act.wait_ge(s_ys, (i - 1) * NST + SKIPPED + 2)
                            act.activation(skip[:], ident[:], ACT.Copy, scale=ad[:, par, NST:NST + 1]).then_inc(s_skip, 1)
                        if n == COPIED and not first:
                            copy_out(i - 1)

            turns(act, NU // 2, pair)
            copy_out(NU - 1)

        @block.gpsimd
        def _(pool):
            def pair(j):
                for par in range(2):
                    i = j * 2 + par
                    pool.wait_ge(s_ld[par], j * 48 + 48)
                    for n in range(NST):
                        pool.wait_ge(s_bc[n], (j // (ET // 2)) * 16 + 16)
                        after(pool, s_scan, i * NST + n - IR + 1)
                        pool.tensor_tensor(dbu[:, n % IR, :], du[:, par, :], bc[:, n, 0, :], ALU.mult).then_inc(s_dbu, 1)

            turns(pool, NU // 2, pair)

        @block.vector
        def _(dve):
            def times_c(i, n):
                dve.wait_ge(s_scan, i * NST + n + 1)
                after(dve, s_ys, i * NST + n - 1)
                dve.tensor_tensor(hc[:, n % 2, :], h[:, n % HR, :], bc[:, n, 1, :], ALU.mult).then_inc(s_hc, 1)

            def gate_unit(i):
                dve.wait_ge(s_szl, i * 16 + 16)
                dve.wait_ge(s_ys, i * NST + NST)
                after(dve, s_tr, 2 * i)
                dve.scalar_tensor_tensor(out=yt[:, :], in0=psy[:, :], scalar=gate[:, 0:1], in1=sz[:],
                                         op0=ALU.mult, op1=ALU.mult).then_inc(s_gated, 1)

            def pair(j):
                for par in range(2):
                    i = j * 2 + par
                    first = isinstance(j, int) and i == 0
                    for n in range(NST):
                        dve.wait_ge(s_da, i * NST + n + 1)
                        dve.wait_ge(s_dbu, i * NST + n + 1)
                        after(dve, s_hc, i * NST + n - HR + 1)
                        dve.tensor_tensor_scan(h[:, n % HR, :], da[n % 2][:, :], dbu[:, n % IR, :], 0.0, ALU.mult,
                                               ALU.add).then_inc(s_scan, 1)
                        if n:
                            times_c(i, n - 1)
                        elif not first:
                            times_c(i - 1, NST - 1)
                        if n == GATED and not first:
                            gate_unit(i - 1)

            dve.wait_ge(s_gate, 1)
            turns(dve, NU // 2, pair)
            times_c(NU - 1, NST - 1)
            gate_unit(NU - 1)

        @block.tensor
        def _(pe):
            pe.wait_ge(s_c, 32)

            def spread(i, half):
                if half == 0:
                    pe.wait_ge(s_gated, i + 1)
                    pe.wait_ge(s_xl, i * 16 + 16)
                    after(pe, s_x1, i)
                for t in range(half * HALF, (half + 1) * HALF):
                    pe.matmul(pst[:, t, :], yt[:, t * P:(t + 1) * P], ident[:], start=True, stop=False)
                    mm = pe.matmul(pst[:, t, :], ident[:], xl[:, t, :], start=False, stop=True)
                mm.then_inc(s_tr, 1)

            def pair(j):
                for par in range(2):
                    i = j * 2 + par
                    first = isinstance(j, int) and i == 0
                    for n in range(NST):
                        if n == 0:
                            after(pe, s_gated, i)
                        pe.wait_ge(s_hc, i * NST + n + 1)
                        for hb in range(2):
                            mm = pe.matmul(psy[:, hb * HB:(hb + 1) * HB], ident[:], hc[:, n % 2, hb * HB:(hb + 1) * HB],
                                           start=(n == 0), stop=(n == NST - 1))
                        mm.then_inc(s_ys, 1)
                        if n in SPREAD and not first:
                            spread(i - 1, SPREAD.index(n))
                        if n == SKIPPED:
                            pe.wait_ge(s_skip, i + 1)
                            pe.wait_ge(s_ut, i * 16 + 16)
                            for hb in range(2):
                                pe.matmul(psy[:, hb * HB:(hb + 1) * HB], skip[:], ut[:, hb * HB:(hb + 1) * HB],
                                          start=False, stop=False)

            turns(pe, NU // 2, pair)
            spread(NU - 1, 0)
            spread(NU - 1, 1)


def shared_pass(nc, io, dr, part, slots, weights, out=None):
    route = part == 0
    with ExitStack() as ctx:
        nm = lambda name: f"{name}_s{part}"
        sb = lambda name, shape, dt=F32: ctx.enter_context(nc.sbuf_tensor(nm(name), shape, dt))
        ps = lambda name, shape: ctx.enter_context(nc.psum_tensor(nm(name), shape, F32))
        named = Semaphores(nc, ctx)
        sem = lambda name: named(nm(name))
        EG = NE // NG
        KF = HB // P
        WN = KH * HB
        raw = sb("raw", [P, 2, WN])
        wsp = sb("wsp", [P, 3, 2, WN], F32R)
        ident = sb("ident", [P, P])
        gate = sb("gate", [P, 1])
        xt = sb("xt", [P, 2, H])
        xn = sb("xn", [P, 2, H]) if route else xt
        xT = sb("xT", [P, 2, 2, KH, P], F32R)
        sg = sb("sg", [P, HB])
        hT = sb("hT", [P, 2, KF, P], F32R)
        ac = sb("ac", [P, 2, H])
        psG, psU = ps("psG", [P, HB]), ps("psU", [P, HB])
        psO, psX, psH = ps("psO", [P, H]), ps("psXT", [P, 2, 4, P]), ps("psH", [P, KF, P])
        if route:
            psR = ps("psR", [P, HB])
            tri = sb("tri", [P, P])
            ones = sb("ones", [P, P])
            iota = sb("iota", [P, NE])
            lower = sb("lower", [P, NG, NG])
            bias = sb("bias", [P, NE])
            gw = sb("gw", [P, KH, NE])
            xTf = sb("xTf", [P, 2, KH, P])
            gate2 = sb("gate_scaled", [P, 1])
            tok = sb("tok", [P, 2], I32)
            step = sb("token_step", [P, 1], I32)
            zero = sb("zero_table", [P, NE * CAP // P], I32)
            stats, mv, root, rstd = sb("stats", [P, 12]), sb("mv", [P, 2]), sb("root", [P, 2]), sb("rstd", [P, 1])
            th, scores, sc = sb("th", [P, NE]), sb("scores", [P, NE]), sb("sc", [P, NG, EG])
            gm, gs = sb("gm", [P, NG, 8]), sb("gs", [P, NG])
            gt, eq, rank = sb("gt", [P, NG, NG]), sb("eq", [P, NG, NG]), sb("rank", [P, NG])
            m8, i8, idx = sb("m8", [P, 8]), sb("i8", [P, 8], U32), sb("idx", [P, TOPK])
            oh, ow = sb("oh", [P, TOPK, NE]), sb("ow", [P, TOPK, NE])
            mask, run = sb("mask", [P, NE]), sb("run", [P, NE])
            w4, ws = sb("w4", [P, TOPK]), sb("ws", [P, 2])
            pos, over, sf = sb("pos", [P, TOPK]), sb("over", [P, TOPK]), sb("sf", [P, TOPK])
            si = sb("si", [P, 2, TOPK], I32)
        else:
            x1t = sb("x1t", [P, 2, H])
            y = raw[:].rearrange("p r (k h) -> p r k h", h=H)
            si = sb("si", [P, 2, TOPK], I32)

        SUMS = TOPK + 1
        halves = (slice(0, WN // 2), slice(WN // 2, WN))
        NC = 8 if route else 2
        s_c = sem("constants")
        s_raw = [[sem(f"matrix_loaded{i}_half{half}") for half in range(2)] for i in range(2)]
        s_whi, s_wlo = sem("matrix_heads"), sem("matrix_rests")
        s_tanh = sem("gate_tanh")
        s_x = [sem(f"x_loaded{i}") for i in range(2)]
        s_acl = [sem(f"acc_loaded{i}") for i in range(2)]
        s_xnst = [sem(f"xn_stored{i}") for i in range(2)]
        s_acst = [sem(f"acc_stored{i}") for i in range(2)]
        s_xn, s_xtr, s_xhi, s_xlo = sem("xn"), sem("x_transposed"), sem("x_heads"), sem("x_rests")
        s_g, s_u, s_sg, s_h = sem("gate_product"), sem("up_product"), sem("silu"), sem("hidden")
        s_htr, s_hhi, s_hlo = sem("hidden_transposed"), sem("hidden_heads"), sem("hidden_rests")
        s_d = sem("down_product")
        if route:
            s_ac = sem("acc")
        if route:
            s_init, s_tab = sem("initialised"), sem("table_zero")
            s_sct = [sem(f"tokens_scattered{i}") for i in range(2)]
            s_tok, s_ch, s_ln, s_fence = sem("token_ids"), sem("dve_steps"), sem("norm_steps"), sem("dve_gate")
            s_lg, s_th, s_mask, s_pos, s_posr = sem("logits"), sem("logits_tanh"), sem("mask"), sem("positions"), sem("pos_read")
            s_run = sem("queue_lengths")
            s_slot, s_carry = sem("slots"), sem("pool_carry")
        else:
            s_zero, s_si, s_carry = sem("rows_zero"), sem("gather_slots"), sem("pool_carry")
            s_y = [sem(f"rows_gathered{i}") for i in range(2)]
            s_half, s_sum = sem("half_added"), sem("sum_steps")
        block = ctx.enter_context(nc.Block())
        x1 = dr["x1"].rearrange("b (t p) h -> (b t) p h", p=P)
        if out is not None:
            o = out.rearrange("b (t p) h -> (b t) p h", p=P)
        xnd = dr["xn"].rearrange("(t p) h -> t p h", p=P)

        def split(j, par):
            t = j * 2 + par
            i = isinstance(t, int)
            return t, i and t == 0, i and t < 2, i and t == TT - 1

        @block.sync
        def _(sp):
            consts = [(gate[:], io["g_f"].partition_broadcast(P)), (ident[:], io["ident"])]
            if route:
                consts += [(tri[:], io["tri"]), (iota[:], io["iota"].partition_broadcast(P)),
                           (lower[:].rearrange("p a b -> p (a b)"), io["lower"].partition_broadcast(P)),
                           (bias[:], io["gate_b"].partition_broadcast(P)), (tok[:], io["tok"]),
                           (gw[:], io["gate_w"].rearrange("(k p) e -> p k e", p=P))]
            for dst, src in consts:
                sp.dma_start(dst, src).then_inc(s_c, 16)

            def load(t, par):
                sp.dma_start(xt[:, par, :], x1[t] if route else xnd[t]).then_inc(s_x[par], 16)

            def store(t, par):
                sp.wait_ge(*((s_ac, t + 1) if route else (s_sum, t * SUMS + SUMS)))
                sp.dma_start(dr["acc"][t] if route else o[t], ac[:, par, :]).then_inc(s_acst[par], 16)

            load(0, 0)
            cols = slice(part * HB, (part + 1) * HB)
            for m, src in enumerate((io["w_sg"][:, cols], io["w_su"][:, cols], io["w_sd"][cols, :])):
                blocks = (KF if m == 2 else KH) // 2
                for half in range(2):
                    if m == 2:
                        sp.wait_ge(s_wlo, half + 1)
                    sp.dma_start(raw[:, m % 2, halves[half]].rearrange("p (k f) -> p k f", k=blocks),
                                 src.rearrange("(h k p) f -> h p k f", h=2, p=P)[half]).then_inc(s_raw[m % 2][half], 16)
            if route:
                sp.wait_ge(s_init, 1)
                sp.dma_start(dr["tab"].rearrange("(p s) o -> p (s o)", p=P), zero[:]).then_inc(s_tab, 16)

            def pair(j):
                for par in range(2):
                    t, first, early, last = split(j, par)
                    if not last:
                        after(sp, s_xn if route else s_xtr, t)
                        load(t + 1, 1 - par)
                    if route:
                        sp.wait_ge(s_xn, t + 1)
                        sp.dma_start(xnd[t], xn[:, par, :]).then_inc(s_xnst[par], 16)
                    if not early:
                        store(t - 2, par)
                    if not route:
                        after(sp, s_acst[par], j * 16)
                        sp.dma_start(ac[:, par, :], dr["acc"][t]).then_inc(s_acl[par], 16)
                        sp.dma_start(x1t[:, par, :], x1[t]).then_inc(s_acl[par], 16)

            turns(sp, TT // 2, pair, last=True)
            store(TT - 2, 0)
            store(TT - 1, 1)
            for s in (*(s_xnst if route else ()), *s_acst):
                sp.wait_ge(s, 16 * TT // 2)

        if route:
            @block.gpsimd
            def _(pool):
                pool.memset(ones[:], 1.0)
                pool.memset(run[:], 0.0)
                pool.memset(step[:], 2 * P)
                pool.memset(zero[:], 0).then_inc(s_init, 1)
                pool.wait_ge(s_tab, 16)
                pool.wait_ge(s_c, 16 * NC)

                def pair(j):
                    for par in range(2):
                        t, first, early, last = split(j, par)
                        if not (isinstance(j, int) and j == 0):
                            pool.wait_ge(s_sct[par], j * 16 * TOPK)
                            pool.tensor_tensor(tok[:, par:par + 1], tok[:, par:par + 1], step[:], ALU.add).then_inc(s_tok, 1)
                            pool.wait_ge(s_tok, t - 1)
                        pool.wait_ge(s_slot, t + 1)
                        pool.sem_inc(s_carry, 1)
                        for k in range(TOPK):
                            pool.indirect_dma_start(dr["tab"], bass.IndirectOffsetOnAxis(ap=si[:, par, k:k + 1], axis=0),
                                                    tok[:, par:par + 1], None, bounds_check=NE * CAP - 1,
                                                    oob_is_err=False).then_inc(s_sct[par], 16)

                turns(pool, TT // 2, pair)
                for s in s_sct:
                    pool.wait_ge(s, 16 * TOPK * TT // 2)

        else:
            @block.gpsimd
            def _(pool):
                pool.wait_ge(s_wlo, 6)
                pool.memset(y, 0.0).then_inc(s_zero, 1)
                pool.wait_ge(s_zero, 1)

                def pair(j):
                    for par in range(2):
                        t = j * 2 + par
                        after(pool, s_sum, (t - 2) * SUMS + TOPK if not isinstance(t, int) or t >= 2 else 0)
                        pool.tensor_copy(si[:, par, :], slots[:, bass.ds(t * TOPK, TOPK)]).then_inc(s_si, 1)
                        pool.wait_ge(s_si, t + 1)
                        pool.sem_inc(s_carry, 1)
                        for k in range(TOPK):
                            pool.indirect_dma_start(y[:, par, k, :], None, dr["ob"],
                                                    bass.IndirectOffsetOnAxis(ap=si[:, par, k:k + 1], axis=0),
                                                    bounds_check=NE * CAP - 1, oob_is_err=False).then_inc(s_y[par], 16)

                turns(pool, TT // 2, pair)

        @block.tensor
        def _(pe):
            pe.wait_ge(s_c, 16 * NC)
            if route:
                pe.wait_ge(s_init, 1)

            def x_transpose(t, par, j):
                if route:
                    pe.wait_ge(s_xn, t + 1)
                else:
                    pe.wait_ge(s_x[par], j * 16 + 16)
                after(pe, s_xlo, 2 * t)
                for k in range(KH):
                    mm = pe.transpose(psX[:, k // 4, k % 4, :], xn[:, par, k * P:(k + 1) * P], ident[:])
                mm.then_inc(s_xtr, 1)

            def product(dst, lhs, rhs, done):
                for n, (l, r) in enumerate(zip(lhs, rhs)):
                    pe.matmul(dst, l[0], r[0], start=(n == 0), stop=False)
                    pe.matmul(dst, l[0], r[1], start=False, stop=False)
                    mm = pe.matmul(dst, l[1], r[0], start=False, stop=(n == len(lhs) - 1))
                if done is not None:
                    mm.then_inc(done, 1)

            def up(dst, m, par, done):
                product(dst[:], [[xT[:, par, c, k, :] for c in range(2)] for k in range(KH)],
                        [[wsp[:, m, c, k * HB:(k + 1) * HB] for c in range(2)] for k in range(KH)], done)

            def down(t):
                pe.wait_ge(s_hlo, t + 1)
                after(pe, s_ac if route else s_half, t)
                for hb in range(H // HB):
                    product(psO[:, hb * HB:(hb + 1) * HB], [[hT[:, c, k, :] for c in range(2)] for k in range(KF)],
                            [[wsp[:, 2, c, k * H + hb * HB:k * H + (hb + 1) * HB] for c in range(2)] for k in range(KF)],
                            s_d if hb else None)

            def pair(j):
                for par in range(2):
                    t, first, early, last = split(j, par)
                    pe.wait_ge(s_xlo, 2 * t + 2)
                    if first:
                        pe.wait_ge(s_wlo, 2)
                    after(pe, s_sg, t)
                    up(psG, 0, par, s_g)
                    if route:
                        after(pe, s_posr, t)
                        for k in range(KH):
                            mm = pe.matmul(psR[:, 0:NE], xTf[:, par, k, :], gw[:, k, :], start=(k == 0), stop=(k == KH - 1))
                        mm.then_inc(s_lg, 1)
                    if first:
                        pe.wait_ge(s_wlo, 4)
                    else:
                        h_transpose(t - 1)
                    after(pe, s_h, t)
                    up(psU, 1, par, s_u)
                    if not last:
                        x_transpose(t + 1, 1 - par, j + par)
                    if first:
                        pe.wait_ge(s_wlo, 6)
                    else:
                        down(t - 1)
                    if route:
                        pe.wait_ge(s_mask, t + 1)
                        if not first:
                            pe.wait_ge(s_run, t)
                        pe.matmul(psR[:, NE:2 * NE], tri[:], mask[:], start=True, stop=False)
                        pe.matmul(psR[:, NE:2 * NE], ones[:], run[:], start=False, stop=True).then_inc(s_pos, 1)

            def h_transpose(t):
                pe.wait_ge(s_h, t + 1)
                after(pe, s_hlo, t)
                for k in range(KF):
                    mm = pe.transpose(psH[:, k, :], sg[:, k * P:(k + 1) * P], ident[:])
                mm.then_inc(s_htr, 1)

            x_transpose(0, 0, 0)
            turns(pe, TT // 2, pair, last=True)
            h_transpose(TT - 1)
            down(TT - 1)

        @block.scalar
        def _(act):
            act.wait_ge(s_c, 16 * NC)
            act.activation(gate[:], gate[:], ACT.Tanh).then_inc(s_tanh, 1)

            def x_head(t, par):
                act.wait_ge(s_xtr, t + 1)
                after(act, s_u, t - 1)
                for hb in range(2):
                    ks = slice(4 * hb, 4 * hb + 4)
                    act.activation(xT[:, par, 0, ks, :], psX[:, hb], ACT.Copy).then_inc(s_xhi, 1)
                    if route:
                        act.activation(xTf[:, par, ks, :], psX[:, hb], ACT.Copy).then_inc(s_xhi, 1)

            def pair(j):
                for par in range(2):
                    t, first, early, last = split(j, par)
                    if route and not early:
                        scaled_out(t - 2, j - 1, par)
                    if route:
                        act.wait_ge(s_lg, t + 1)
                        if not first:
                            act.wait_ge(s_ch, (t - 1) * ROUTE + 1)
                        act.activation(th[:], psR[:, 0:NE], ACT.Tanh, scale=0.5).then_inc(s_th, 1)
                    if not first:
                        h_head(t - 1)
                    act.wait_ge(s_g, t + 1)
                    after(act, s_htr, t)
                    act.activation(sg[:], psG[:], ACT.Silu).then_inc(s_sg, 1)
                    if not last:
                        x_head(t + 1, 1 - par)

            def h_head(t):
                act.wait_ge(s_htr, t + 1)
                after(act, s_d, t)
                act.activation(hT[:, 0], psH[:], ACT.Copy).then_inc(s_hhi, 1)

            def scaled_out(t, j, par):
                act.wait_ge(s_d, t + 1)
                after(act, s_acst[par], j * 16)
                act.activation(ac[:, par, :], psO[:], ACT.Copy, scale=gate[:, 0:1]).then_inc(s_ac, 1)

            x_head(0, 0)
            for m in range(3):
                for half in range(2):
                    act.wait_ge(s_raw[m % 2][half], 16 * (m // 2 + 1))
                    act.activation(wsp[:, m, 0, halves[half]], raw[:, m % 2, halves[half]], ACT.Copy).then_inc(s_whi, 1)
            act.wait_ge(s_tanh, 1)
            turns(act, TT // 2, pair, last=True, first=2)
            if route:
                scaled_out(TT - 2, TT // 2 - 1, 0)
            h_head(TT - 1)
            if route:
                scaled_out(TT - 1, TT // 2 - 1, 1)

        @block.vector
        def _(dve):
            f32 = lambda ap: ap.bitcast(F32)
            XH = 4 if route else 2

            def x_rest(t, par):
                for hb in range(2):
                    ks = slice(4 * hb, 4 * hb + 4)
                    dve.wait_ge(s_xhi, XH * t + XH // 2 * (hb + 1))
                    dve.tensor_tensor(xT[:, par, 1, ks, :], psX[:, hb], f32(xT[:, par, 0, ks, :]), ALU.subtract)\
                        .then_inc(s_xlo, 1)

            def h_rest(t):
                dve.wait_ge(s_hhi, t + 1)
                dve.tensor_tensor(hT[:, 1], psH[:], f32(hT[:, 0]), ALU.subtract).then_inc(s_hlo, 1)

            def multiply(t):
                dve.wait_ge(s_sg, t + 1)
                dve.wait_ge(s_u, t + 1)
                dve.tensor_tensor(sg[:], sg[:], psU[:], ALU.mult).then_inc(s_h, 1)

            def finish(t, j, par):
                dve.wait_ge(s_acl[par], j * 32 + 32)
                dve.wait_ge(s_y[par], j * 16 * TOPK + 16 * TOPK)
                for k in range(TOPK):
                    if k:
                        dve.wait_ge(s_sum, t * SUMS + k)
                    dve.scalar_tensor_tensor(out=ac[:, par, :], in0=y[:, par, k, :], scalar=weights[:, bass.ds(t * TOPK + k, 1)],
                                             in1=ac[:, par, :], op0=ALU.mult, op1=ALU.add).then_inc(s_sum, 1)
                dve.wait_ge(s_d, t + 1)
                dve.scalar_tensor_tensor(out=x1t[:, par, :], in0=psO[:], scalar=gate[:, 0:1], in1=x1t[:, par, :],
                                         op0=ALU.mult, op1=ALU.add).then_inc(s_half, 1)
                dve.wait_ge(s_half, t + 1)
                dve.wait_ge(s_sum, t * SUMS + TOPK)
                dve.tensor_tensor(ac[:, par, :], ac[:, par, :], x1t[:, par, :], ALU.add).then_inc(s_sum, 1)

            dve.wait_ge(s_c, 16 * NC)
            dve.wait_ge(s_tanh, 1)
            if route:
                st = Steps(dve, s_ch, ROUTE)
                ln = Steps(dve, s_ln, ROOT + 2)

            def norm(t, j, par):
                ln.start(t)
                after(dve, s_xn, t)
                dve.wait_ge(s_x[par], j * 16 + 16)
                dve.bn_stats(stats[:, 0:6], xt[:, par, 0:HB])
                ln.then(dve.bn_stats(stats[:, 6:12], xt[:, par, HB:H]), s_fence)
                ln.then(dve.bn_aggr(mv[:], stats[:]))
                inverse_root(ln, dve, rstd[:], mv[:, 1:2], root)
                after(dve, s_xtr, t - 1)
                after(dve, s_xnst[par], j * 16)
                dve.tensor_scalar(xn[:, par, :], xt[:, par, :], mv[:, 0:1], rstd[:], ALU.subtract,
                                  ALU.mult).then_inc(s_xn, 1)
                ln.end()

            def choose(t):
                st.start(t)
                dve.wait_ge(s_th, t + 1)
                scf = sc[:].rearrange("p g e -> p (g e)")
                st.then(dve.tensor_scalar(scores[:], th[:], 0.5, 0.5, ALU.mult, ALU.add))
                st.then(dve.tensor_tensor(scf, scores[:], bias[:], ALU.add), s_fence)
                for g in range(NG):
                    ins = dve.max(gm[:, g, :], sc[:, g, :])
                st.then(ins)
                st.then(dve.tensor_tensor(gs[:], gm[:, :, 0], gm[:, :, 1], ALU.add))
                other = gs[:].unsqueeze(1).to_broadcast([P, NG, NG])
                mine = gs[:].unsqueeze(2).to_broadcast([P, NG, NG])
                st.then(dve.tensor_tensor(gt[:], other, mine, ALU.is_gt))
                st.then(dve.tensor_tensor(eq[:], other, mine, ALU.is_equal))
                st.then(dve.tensor_tensor(eq[:], eq[:], lower[:], ALU.mult))
                st.then(dve.tensor_tensor(gt[:], gt[:], eq[:], ALU.add))
                st.then(dve.tensor_reduce(rank[:], gt[:], AX, ALU.add))
                st.then(dve.tensor_scalar(rank[:], rank[:], float(TG), None, ALU.is_lt))
                st.then(dve.tensor_tensor(sc[:], sc[:], rank[:].unsqueeze(2).to_broadcast([P, NG, EG]), ALU.mult), s_fence)
                st.then(dve.max(m8[:], scf), s_fence)
                st.then(dve.max_index(i8[:], m8[:], scf))
                st.then(dve.tensor_copy(idx[:], i8[:, 0:TOPK]))
                st.then(dve.tensor_tensor(oh[:], iota[:].unsqueeze(1).to_broadcast([P, TOPK, NE]),
                                          idx[:].unsqueeze(2).to_broadcast([P, TOPK, NE]), ALU.is_equal))
                after(dve, s_pos, t)
                dve.tensor_reduce(mask[:], oh[:].rearrange("p k e -> p e k"), AX, ALU.add).then_inc(s_mask, 1)
                st.then(dve.tensor_tensor(ow[:], oh[:], scores[:].unsqueeze(1).to_broadcast([P, TOPK, NE]), ALU.mult))
                st.then(dve.tensor_reduce(w4[:], ow[:], AX, ALU.add))
                st.then(dve.tensor_reduce(ws[:, 0:1], w4[:], AX, ALU.add))
                st.then(dve.tensor_scalar(ws[:, 0:1], ws[:, 0:1], 1e-20, None, ALU.add))
                st.then(dve.reciprocal(ws[:, 1:2], ws[:, 0:1]))
                st.then(dve.tensor_scalar(w4[:], w4[:], ws[:, 1:2], gate2[:, 0:1], ALU.mult, ALU.mult))
                assert st.n == CHOICE

            def queue(t, j, par):
                st.resume(t, CHOICE)
                dve.wait_ge(s_pos, t + 1)
                dve.tensor_tensor(ow[:], oh[:], psR[:, NE:2 * NE].unsqueeze(1).to_broadcast([P, TOPK, NE]),
                                  ALU.mult).then_inc(s_posr, 1)
                dve.wait_ge(s_mask, t + 1)
                dve.wait_ge(s_posr, t + 1)
                dve.tensor_tensor(run[:], run[:], mask[:], ALU.add).then_inc(s_run, 1)
                dve.wait_ge(s_run, t + 1)
                st.then(dve.tensor_reduce(pos[:], ow[:], AX, ALU.add))
                st.then(dve.tensor_scalar(over[:], pos[:], float(CAP), float(DROPPED), ALU.is_ge, ALU.mult))
                st.then(dve.scalar_tensor_tensor(out=sf[:], in0=idx[:], scalar=float(CAP), in1=pos[:], op0=ALU.mult,
                                                 op1=ALU.add))
                st.then(dve.tensor_tensor(sf[:], sf[:], over[:], ALU.add))
                after(dve, s_sct[par], j * 16 * TOPK)
                dve.tensor_copy(si[:, par, :], sf[:]).then_inc(s_slot, 1)
                dve.scalar_tensor_tensor(out=weights[:, bass.ds(t * TOPK, TOPK)], in0=pos[:], scalar=float(CAP), in1=w4[:],
                                         op0=ALU.is_lt, op1=ALU.mult)
                st.then(dve.tensor_copy(slots[:, bass.ds(t * TOPK, TOPK)], sf[:]))
                st.end()

            def pair(j):
                for par in range(2):
                    t, first, early, last = split(j, par)
                    if route and not last:
                        norm(t + 1, j + par, 1 - par)
                    if route and not first:
                        queue(t - 1, j - (par == 0), 1 - par)
                    if not route and not early:
                        finish(t - 2, j - 1, par)
                    if not first:
                        h_rest(t - 1)
                    if route:
                        choose(t)
                    if not last:
                        x_rest(t + 1, 1 - par)
                    multiply(t)

            if route:
                dve.wait_ge(s_init, 1)
                dve.tensor_scalar(gate2[:], gate[:], SCALE, None, ALU.mult)
                norm(0, 0, 0)
            x_rest(0, 0)
            for m in range(3):
                for half in range(2):
                    dve.wait_ge(s_whi, 2 * m + half + 1)
                    dve.tensor_tensor(wsp[:, m, 1, halves[half]], raw[:, m % 2, halves[half]],
                                      f32(wsp[:, m, 0, halves[half]]), ALU.subtract).then_inc(s_wlo, 1)
            turns(dve, TT // 2, pair, last=True, first=2)
            if route:
                queue(TT - 1, TT // 2 - 1, 1)
            else:
                finish(TT - 2, TT // 2 - 1, 0)
            h_rest(TT - 1)
            if not route:
                finish(TT - 1, TT // 2 - 1, 1)


def experts(nc, io, dr):
    with ExitStack() as ctx:
        sb = lambda name, shape, dt=F32: ctx.enter_context(nc.sbuf_tensor(name, shape, dt))
        ps = lambda name, shape: ctx.enter_context(nc.psum_tensor(name, shape, F32))
        sem = Semaphores(nc, ctx)
        KF = F // P
        WN = KH * F
        IR, WR, XT = 4, 4, 4
        raw = sb("raw", [P, 2, WN])
        wsp = sb("wsp", [P, WR, 2, WN], F32R)
        ident = sb("ident4", [P, P])
        ids = sb("ids", [P, IR], I32)
        xg = sb("xg", [P, TPE, H])
        xT = sb("xgT", [P, TPE, 2, KH, P], F32R)
        sg = sb("sg4", [P, TPE, F])
        hT = sb("hT4", [P, TPE, 2, KF, P], F32R)
        ob = sb("ob", [P, TPE, H])
        psG = [ps(f"psG4{t}", [P, F]) for t in range(TPE)]
        psU = [ps(f"psU4{t}", [P, F]) for t in range(TPE)]
        psO = [ps(f"psO4{t}", [P, HB]) for t in range(2)]
        psT = [ps(f"psT4{t}", [P, 4, P]) for t in range(2)]

        s_c = sem("p4_constants")
        s_raw = [sem(f"p4_matrix_loaded{i}") for i in range(2)]
        s_ids = [sem(f"p4_ids_loaded{i}") for i in range(IR)]
        s_gat = [sem(f"p4_rows_gathered{i}") for i in range(TPE)]
        s_obst = [sem(f"p4_rows_stored{i}") for i in range(TPE)]
        s_whi = sem("p4_matrix_heads")
        s_wlo = sem("p4_matrix_rests")
        s_tr = sem("p4_transposed")
        s_thi = sem("p4_transposed_heads")
        s_tlo = sem("p4_transposed_rests")
        s_g = sem("p4_gate_product")
        s_u = sem("p4_up_product")
        s_sg = sem("p4_silu")
        s_h = sem("p4_hidden")
        s_d = sem("p4_down_product")
        s_oa = sem("p4_out_first_half")
        s_ob = sem("p4_out_second_half")
        s_carry = sem("p4_pool_carry")
        block = ctx.enter_context(nc.Block())
        f32 = lambda ap: ap.bitcast(F32)

        ROUNDS = [("h", 0, 0), ("x", 0, 0), ("x", 0, 1), ("h", 1, 0), ("x", 1, 0), ("x", 1, 1)]
        NR = len(ROUNDS)
        HEAD = 2 * TPE

        def rounds(e):
            last = isinstance(e, int) and e == NE - 1
            kept = [r for r in ROUNDS if r[0] == "h" or not last]
            return [(kind, t, hb, HEAD + e * NR + n, n % 2) for n, (kind, t, hb) in enumerate(kept)]

        def four(body):
            def turn(j):
                for x in range(XT):
                    body(j * XT + x, j, x)
            return turn

        @block.sync
        def _(sp):
            tab = dr["tab"].rearrange("(s p) o -> s p o", p=P)

            def load_ids(s, r):
                sp.dma_start(ids[:, r:r + 1], tab[s]).then_inc(s_ids[r], 16)

            def load_matrix(e, j, x, m):
                c = (3 * x + m) % 2
                after(sp, s_wlo, 3 * e + m - 1)
                src = (io["w1"], io["w3"], io["w2"])[m][e]
                sp.dma_start(raw[:, c, :].rearrange("p (k f) -> p k f", k=KF if m == 2 else KH),
                             src.rearrange("(k p) f -> p k f", p=P)).then_inc(s_raw[c], 16)

            for r in range(TPE):
                load_ids(r, r)
            load_matrix(0, 0, 0, 0)
            sp.dma_start(ident[:], io["ident"]).then_inc(s_c, 16)
            for r in range(TPE, IR):
                load_ids(r, r)
            load_matrix(0, 0, 0, 1)

            def expert(e, j, x):
                first, last = isinstance(e, int) and e == 0, isinstance(e, int) and e == NE - 1
                load_matrix(e, j, x, 2)
                if not last:
                    nj, nx = (j, x + 1) if x + 1 < XT else (j + 1, 0)
                    load_matrix(e + 1, nj, nx, 0)
                for t in range(TPE):
                    if not first:
                        sp.wait_ge(s_oa, TPE * (e - 1) + t + 1)
                        sp.wait_ge(s_ob, TPE * (e - 1) + t + 1)
                        sp.dma_start(dr["ob"].rearrange("(s p) h -> s p h", p=P)[TPE * (e - 1) + t], ob[:, t, :])\
                            .then_inc(s_obst[t], 16)
                if not (isinstance(e, int) and e + 2 >= NE):
                    for t in range(TPE):
                        sp.wait_ge(s_gat[t], e * 16 + 16)
                        load_ids(TPE * (e + 2) + t, (TPE * x + t) % IR)
                if not last:
                    load_matrix(e + 1, nj, nx, 1)

            turns(sp, NE // XT, four(expert), last=True)
            for t in range(TPE):
                sp.wait_ge(s_oa, TPE * (NE - 1) + t + 1)
                sp.wait_ge(s_ob, TPE * (NE - 1) + t + 1)
                sp.dma_start(dr["ob"].rearrange("(s p) h -> s p h", p=P)[TPE * (NE - 1) + t], ob[:, t, :])\
                    .then_inc(s_obst[t], 16)
            for s in s_obst:
                sp.wait_ge(s, 16 * NE)

        @block.gpsimd
        def _(pool):
            def expert(e, j, x):
                for t in range(TPE):
                    pool.wait_ge(s_ids[(TPE * x + t) % IR], (e // 2) * 16 + 16)
                    if isinstance(e, int) and e < 2:
                        pool.wait_ge(s_tr, 2 * t + 2) if e else None
                    else:
                        pool.wait_ge(s_tr, HEAD + (e - 2) * NR + (3 if t == 0 else 6))
                    pool.sem_inc(s_carry, 1)
                    r = (TPE * x + t) % IR
                    pool.indirect_dma_start(xg[:, t, :], None, dr["xn"],
                                            bass.IndirectOffsetOnAxis(ap=ids[:, r:r + 1], axis=0),
                                            bounds_check=NT - 1, oob_is_err=False).then_inc(s_gat[t], 16)

            turns(pool, NE // XT, four(expert))

        @block.tensor
        def _(pe):
            pe.wait_ge(s_c, 16)

            def transpose_round(kind, t, hb, n, bank, e):
                if kind == "h":
                    pe.wait_ge(s_h, TPE * e + t + 1)
                else:
                    pe.wait_ge(s_gat[t], e * 16 + 16)
                after(pe, s_tlo, n - 1)
                src = sg[:, t, :] if kind == "h" else xg[:, t, hb * HB:(hb + 1) * HB]
                for k in range(4):
                    mm = pe.transpose(psT[bank][:, k, :], src[:, k * P:(k + 1) * P], ident[:])
                mm.then_inc(s_tr, 1)

            def product(dst, lhs, rhs, done):
                for n, (l, r) in enumerate(zip(lhs, rhs)):
                    pe.matmul(dst, l[0], r[0], start=(n == 0), stop=False)
                    pe.matmul(dst, l[0], r[1], start=False, stop=False)
                    mm = pe.matmul(dst, l[1], r[0], start=False, stop=(n == len(lhs) - 1))
                mm.then_inc(done, 1)

            def weights_of(x, m, k, c0):
                slot = (3 * x + m) % WR
                width = H if m == 2 else F
                return [wsp[:, slot, part, k * width + c0:k * width + c0 + HB] for part in range(2)]

            def expert(e, j, x):
                for m, dst, done, read in ((0, psG, s_g, s_sg), (1, psU, s_u, s_h)):
                    pe.wait_ge(s_wlo, 3 * e + m + 1)
                    for t in range(TPE):
                        if m == 0:
                            pe.wait_ge(s_tlo, (HEAD + (e - 1) * NR + (3 if t == 0 else 6)) if not (isinstance(e, int) and e == 0)
                                       else 2 * t + 2)
                        after(pe, read, TPE * (e - 1) + t + 1 if not (isinstance(e, int) and e == 0) else 0)
                        product(dst[t][:], [[xT[:, t, part, k, :] for part in range(2)] for k in range(KH)],
                                [weights_of(x, m, k, 0) for k in range(KH)], done)
                for kind, t, hb, n, bank in rounds(e):
                    transpose_round(kind, t, hb, n, bank, e if kind == "h" else e + 1)
                pe.wait_ge(s_wlo, 3 * e + 3)
                rest = {(kind, t): n for kind, t, hb, n, bank in rounds(e)}
                for t in range(TPE):
                    pe.wait_ge(s_tlo, rest["h", t] + 1)
                    for hb in range(2):
                        after(pe, (s_oa, s_ob)[hb], TPE * e + t)
                        product(psO[hb][:], [[hT[:, t, part, k, :] for part in range(2)] for k in range(KF)],
                                [weights_of(x, 2, k, hb * HB) for k in range(KF)], s_d)

            for n in range(HEAD):
                transpose_round("x", n // 2, n % 2, n, n % 2, 0)
            turns(pe, NE // XT, four(expert), last=True)

        def splits(eng, e, step):
            for kind, t, hb, n, bank in rounds(e):
                dst = hT[:, t, :, :, :] if kind == "h" else xT[:, t, :, 4 * hb:4 * hb + 4, :]
                step(kind, t, n, bank, dst, e)

        @block.scalar
        def _(act):
            def head(kind, t, n, bank, dst, e):
                act.wait_ge(s_tr, n + 1)
                if kind == "h":
                    after(act, s_d, 4 * (e - 1) + 2 * t + 2 if not (isinstance(e, int) and e == 0) else 0)
                elif e is not None:
                    act.wait_ge(s_u, TPE * e + TPE)
                act.activation(dst[:, 0], psT[bank][:], ACT.Copy).then_inc(s_thi, 1)

            def matrix_head(e, j, x, m):
                c, slot = (3 * x + m) % 2, (3 * x + m) % WR
                act.wait_ge(s_raw[c], ((3 * e + m) // 2) * 16 + 16)
                if m == 0:
                    after(act, s_d, 4 * (e - 1) if not (isinstance(e, int) and e < 2) else 0)
                else:
                    after(act, (s_g, s_u)[m - 1], TPE * e)
                act.activation(wsp[:, slot, 0, :], raw[:, c, :], ACT.Copy).then_inc(s_whi, 1)

            def out_half(e, t):
                act.wait_ge(s_d, 4 * e + 2 * t + 1)
                after(act, s_obst[t], e * 16)
                act.activation(ob[:, t, 0:HB], psO[0][:], ACT.Copy).then_inc(s_oa, 1)

            def silu(e, t):
                act.wait_ge(s_g, TPE * e + t + 1)
                if not (isinstance(e, int) and e == 0):
                    act.wait_ge(s_tr, HEAD + (e - 1) * NR + (1 if t == 0 else 4))
                act.activation(sg[:, t, :], psG[t][:], ACT.Silu).then_inc(s_sg, 1)

            def expert(e, j, x):
                last = isinstance(e, int) and e == NE - 1
                nj, nx = (j, x + 1) if x + 1 < XT else (j + 1, 0)
                matrix_head(e, j, x, 2)
                for t in range(TPE):
                    silu(e, t)
                if not last:
                    matrix_head(e + 1, nj, nx, 0)
                splits(act, e, head)
                out_half(e, 0)
                if not last:
                    matrix_head(e + 1, nj, nx, 1)
                out_half(e, 1)

            for n in range(HEAD):
                head("x", n // 2, n, n % 2, xT[:, n // 2, :, 4 * (n % 2):4 * (n % 2) + 4, :], None)
            matrix_head(0, 0, 0, 0)
            matrix_head(0, 0, 0, 1)
            turns(act, NE // XT, four(expert), last=True)

        @block.vector
        def _(dve):
            def rest(kind, t, n, bank, dst, e):
                dve.wait_ge(s_thi, n + 1)
                dve.tensor_tensor(dst[:, 1], psT[bank][:], f32(dst[:, 0]), ALU.subtract).then_inc(s_tlo, 1)

            def matrix_rest(e, j, x, m):
                c, slot = (3 * x + m) % 2, (3 * x + m) % WR
                dve.wait_ge(s_whi, 3 * e + m + 1)
                dve.tensor_tensor(wsp[:, slot, 1, :], raw[:, c, :], f32(wsp[:, slot, 0, :]), ALU.subtract).then_inc(s_wlo, 1)

            def out_half(e, t):
                dve.wait_ge(s_d, 4 * e + 2 * t + 2)
                after(dve, s_obst[t], e * 16)
                dve.tensor_copy(ob[:, t, HB:H], psO[1][:]).then_inc(s_ob, 1)

            def expert(e, j, x):
                last = isinstance(e, int) and e == NE - 1
                nj, nx = (j, x + 1) if x + 1 < XT else (j + 1, 0)
                matrix_rest(e, j, x, 2)
                if not last:
                    matrix_rest(e + 1, nj, nx, 0)
                for t in range(TPE):
                    dve.wait_ge(s_sg, TPE * e + t + 1)
                    dve.wait_ge(s_u, TPE * e + t + 1)
                    dve.tensor_tensor(sg[:, t, :], sg[:, t, :], psU[t][:], ALU.mult).then_inc(s_h, 1)
                splits(dve, e, rest)
                out_half(e, 0)
                if not last:
                    matrix_rest(e + 1, nj, nx, 1)
                out_half(e, 1)

            for n in range(HEAD):
                rest("x", n // 2, n, n % 2, xT[:, n // 2, :, 4 * (n % 2):4 * (n % 2) + 4, :], None)
            matrix_rest(0, 0, 0, 0)
            matrix_rest(0, 0, 0, 1)
            turns(dve, NE // XT, four(expert), last=True)


def program(nc, io, out):
    assert FS == 2 * HB
    dt = lambda name, shape, t=F32: nc.dram_tensor(name, shape, t, kind="Internal").ap()
    dr = {k: dt("scratch_" + k, s) for k, s in dict(
        a=(ET, P, NST + 1), x1=(B, L, H), u=(B * ET, P, L), dl=(B * ET, P, L), du=(B * ET, P, L), sz=(B * ET, P, L),
        bc=(B, NST, 2, L), xn=(NT, H), acc=(TT, P, H), ob=(NE * CAP, H)).items()}
    dr["tab"] = dt("scratch_tab", (NE * CAP, 1), I32)
    mamba_inputs(nc, io, dr)
    selective_scan(nc, io, dr)
    with (nc.sbuf_tensor("slots", [P, TT * TOPK], I32) as slots, nc.sbuf_tensor("weights", [P, TT * TOPK], F32) as weights):
        shared_pass(nc, io, dr, 0, slots, weights)
        experts(nc, io, dr)
        shared_pass(nc, io, dr, 1, slots, weights, out)


def kernel(x, ctx_1024, g_xattn, g_ffn, L0_xattn_in_proj_w, L0_xattn_conv_w, L0_xattn_conv_b, L0_xattn_x_proj_w,
           L0_xattn_dt_proj_w, L0_xattn_dt_proj_b, L0_xattn_A_log, L0_xattn_D, L0_ffn_gate_w, L0_ffn_gate_bias,
           L0_ffn_w1, L0_ffn_w2, L0_ffn_w3, L0_ffn_shared_gate, L0_ffn_shared_up, L0_ffn_shared_down):
    import numpy as np
    import concourse.bacc as bacc
    from concourse.bass_utils import run_bass_kernel_spmd

    per_tile = lambda v: np.ascontiguousarray(np.asarray(v).reshape(-1, P).T)
    t = lambda v: np.ascontiguousarray(np.asarray(v).T)
    arrays = dict(
        x=np.asarray(x), ctxT=np.ascontiguousarray(np.asarray(ctx_1024).transpose(0, 2, 1)),
        w_in=t(L0_xattn_in_proj_w), w_x=t(L0_xattn_x_proj_w), w_dt=t(L0_xattn_dt_proj_w),
        conv_w=np.asarray(L0_xattn_conv_w), conv_b=per_tile(L0_xattn_conv_b), dt_b=per_tile(L0_xattn_dt_proj_b),
        a_log_d=np.concatenate([np.asarray(L0_xattn_A_log), np.asarray(L0_xattn_D)[:, None]], 1), g_x=np.asarray(g_xattn), g_f=np.asarray(g_ffn),
        ident=np.eye(P, dtype=np.float32), tri=np.triu(np.ones((P, P), np.float32), 1),
        iota=np.arange(NE, dtype=np.float32), lower=np.tril(np.ones((NG, NG), np.float32), -1).reshape(-1),
        tok=(np.arange(P)[:, None] + P * np.arange(2)[None, :]).astype(np.int32), gate_w=t(L0_ffn_gate_w),
        gate_b=np.asarray(L0_ffn_gate_bias), w1=np.asarray(L0_ffn_w1), w2=np.asarray(L0_ffn_w2), w3=np.asarray(L0_ffn_w3),
        w_sg=np.asarray(L0_ffn_shared_gate), w_su=np.asarray(L0_ffn_shared_up), w_sd=np.asarray(L0_ffn_shared_down))
    nc = bacc.Bacc("TRN2", target_bir_lowering=False, num_devices=1)
    io = {k: nc.dram_tensor("in_" + k, a.shape, mybir.dt.from_np(a.dtype), kind="ExternalInput").ap()
          for k, a in arrays.items()}
    out = nc.dram_tensor("out", (B, L, H), F32, kind="ExternalOutput").ap()
    program(nc, io, out)
    r = run_bass_kernel_spmd(nc, [{"in_" + k: a for k, a in arrays.items()}], core_ids=[0])
    return r.results[0]["out"]
```
